# Optimizing a Trainium2 kernel written in Bass

```python
import numpy as np
import jax
import jax.numpy as jnp

def _softmax(x, axis=-1):
    return jax.nn.softmax(x, axis=axis)
def _gelu(x):
    return jax.nn.gelu(x, approximate=True)
def _silu(x):
    return jax.nn.silu(x)
def _sigmoid(x):
    return jax.nn.sigmoid(x)
def _layernorm(x, axis=-1, eps=1e-5):
    m = jnp.mean(x, axis=axis, keepdims=True)
    v = jnp.var(x, axis=axis, keepdims=True)
    return (x - m) / jnp.sqrt(v + eps)
def _scatter_add(tgt, idx, src, axis=0):
    return tgt.at[idx].add(src)
def _segment_sum(src, seg, n):
    return jax.ops.segment_sum(src, seg, n)

kernel_name = 'mk_conv_seq_d2_conv_nchw192_9d1003'

def setup_inputs(seed: int = 0):
    np.random.seed(seed)
    _w = jnp.asarray
    def _rec_inputs():
        import jax
        import jax.numpy as jnp
        _gk = jax.random.key(seed)
        x = -0.0004039 + 1 * jax.random.normal(jax.random.fold_in(_gk, 1), (4, 192, 128, 128), jnp.float32)
        return x
    x = _rec_inputs()
    def _L0_conv_setup():
        import jax, jax.numpy as jnp
        import numpy as np
        DIM = 192
        HEADS = 6
        HIDDEN = 384

        def conv2d(x, w, b=None, padding=0, groups=1):
            out = jax.lax.conv_general_dilated(x, w, (1, 1), [(padding, padding), (padding, padding)], feature_group_count=groups, dimension_numbers=('NCHW', 'OIHW', 'NCHW'))
            return out if b is None else out + b[None, :, None, None]

        def layernorm(x, g, b, eps=1e-05):
            m = x.mean(-1, keepdims=True)
            v = x.var(-1, keepdims=True)
            return (x - m) / jnp.sqrt(v + eps) * g + b

        def l2norm(x, eps=1e-12):
            n = jnp.linalg.norm(x, axis=-1, keepdims=True)
            return x / jnp.maximum(n, eps)
        key = jax.random.key(seed)
        ks = jax.random.split(key, 12)
        s = 0.02
        return {'x': jax.random.normal(ks[0], (4, DIM, 128, 128), dtype=jnp.float32), 'g1': jnp.ones((DIM,), jnp.float32), 'b1': jnp.zeros((DIM,), jnp.float32), 'w_qkv': jax.random.normal(ks[1], (3 * DIM, DIM, 1, 1), jnp.float32) * s, 'w_dw': jax.random.normal(ks[2], (3 * DIM, 1, 3, 3), jnp.float32) * s, 'temp': jnp.ones((HEADS, 1, 1), jnp.float32), 'w_head': jax.random.normal(ks[3], (HEADS, HEADS, 3, 3), jnp.float32) * s, 'w_proj': jax.random.normal(ks[4], (DIM, DIM, 1, 1), jnp.float32) * s, 'g2': jnp.ones((DIM,), jnp.float32), 'b2': jnp.zeros((DIM,), jnp.float32), 'w_fc1': jax.random.normal(ks[5], (HIDDEN, DIM), jnp.float32) * s, 'b_fc1': jnp.zeros((HIDDEN,), jnp.float32), 'w_fc2': jax.random.normal(ks[6], (DIM, HIDDEN), jnp.float32) * s, 'b_fc2': jnp.zeros((DIM,), jnp.float32), 'w_sa': jax.random.normal(ks[7], (1, DIM, 3, 3), jnp.float32) * s, 'b_sa': jnp.zeros((1,), jnp.float32)}
    _L0_conv_all = _L0_conv_setup()
    _L0_conv_in = {k: v for k, v in _L0_conv_all.items() if k in ('g1', 'b1', 'w_qkv', 'w_dw', 'temp', 'w_head', 'w_proj', 'g2', 'b2', 'w_fc1', 'b_fc1', 'w_fc2', 'b_fc2', 'w_sa', 'b_sa', )}
    del _L0_conv_all

    def _L1_conv_setup():
        import jax, jax.numpy as jnp
        import numpy as np
        B, C, H, W = (8, 192, 64, 64)
        D_INNER = 192
        N_STATE = 4
        DT_RANK = 12
        K_DIRS = 4

        def _ln_cf(x, w, b, eps=1e-05):
            mu = x.mean(1, keepdims=True)
            var = ((x - mu) ** 2).mean(1, keepdims=True)
            return (x - mu) / jnp.sqrt(var + eps) * w[None, :, None, None] + b[None, :, None, None]

        def _selective_scan(u, dt, A, Bv, Cv):

            def step(h, inp):
                dt_t, u_t, B_t, C_t = inp
                dA = jnp.exp(dt_t[..., None] * A)
                h = dA * h + dt_t[..., None] * B_t[:, :, None, :] * u_t[..., None]
                y = jnp.einsum('bkdn,bkn->bkd', h, C_t)
                return (h, y)
            h0 = jnp.zeros(u.shape[:3] + (A.shape[-1],), u.dtype)
            xs = (jnp.moveaxis(dt, -1, 0), jnp.moveaxis(u, -1, 0), jnp.moveaxis(Bv, -1, 0), jnp.moveaxis(Cv, -1, 0))
            _, ys = jax.lax.scan(step, h0, xs)
            return jnp.moveaxis(ys, 0, -1)
        key = jax.random.key(seed)
        ks = jax.random.split(key, 8)
        s = 0.02
        return {'x': jax.random.normal(ks[0], (B, C, H, W), jnp.float32), 'ln_w': jnp.ones((C,), jnp.float32), 'ln_b': jnp.zeros((C,), jnp.float32), 'in_proj_w': jax.random.normal(ks[1], (2 * D_INNER, C), jnp.float32) * s, 'conv_w': jax.random.normal(ks[2], (D_INNER, 1, 3, 3), jnp.float32) * s, 'conv_b': jnp.zeros((D_INNER,), jnp.float32), 'x_proj_w': jax.random.normal(ks[3], (K_DIRS, DT_RANK + 2 * N_STATE, D_INNER), jnp.float32) * s, 'dt_proj_w': jax.random.normal(ks[4], (K_DIRS, D_INNER, DT_RANK), jnp.float32) * s, 'dt_proj_b': jnp.full((K_DIRS, D_INNER), -4.6, jnp.float32), 'A_log': jnp.log(jnp.broadcast_to(jnp.arange(1, N_STATE + 1, dtype=jnp.float32), (K_DIRS, D_INNER, N_STATE))), 'Ds': jnp.ones((K_DIRS, D_INNER), jnp.float32), 'out_norm_w': jnp.ones((D_INNER,), jnp.float32), 'out_norm_b': jnp.zeros((D_INNER,), jnp.float32), 'out_proj_w': jax.random.normal(ks[5], (C, D_INNER), jnp.float32) * s}
    _L1_conv_all = _L1_conv_setup()
    _L1_conv_in = {k: v for k, v in _L1_conv_all.items() if k in ('ln_w', 'ln_b', 'in_proj_w', 'conv_w', 'conv_b', 'x_proj_w', 'dt_proj_w', 'dt_proj_b', 'A_log', 'Ds', 'out_norm_w', 'out_norm_b', 'out_proj_w', )}
    del _L1_conv_all

    return {
        "x": x,
        "L0_conv_g1": _L0_conv_in["g1"],
        "L0_conv_b1": _L0_conv_in["b1"],
        "L0_conv_w_qkv": _L0_conv_in["w_qkv"],
        "L0_conv_w_dw": _L0_conv_in["w_dw"],
        "L0_conv_temp": _L0_conv_in["temp"],
        "L0_conv_w_head": _L0_conv_in["w_head"],
        "L0_conv_w_proj": _L0_conv_in["w_proj"],
        "L0_conv_g2": _L0_conv_in["g2"],
        "L0_conv_b2": _L0_conv_in["b2"],
        "L0_conv_w_fc1": _L0_conv_in["w_fc1"],
        "L0_conv_b_fc1": _L0_conv_in["b_fc1"],
        "L0_conv_w_fc2": _L0_conv_in["w_fc2"],
        "L0_conv_b_fc2": _L0_conv_in["b_fc2"],
        "L0_conv_w_sa": _L0_conv_in["w_sa"],
        "L0_conv_b_sa": _L0_conv_in["b_sa"],
        "L1_conv_ln_w": _L1_conv_in["ln_w"],
        "L1_conv_ln_b": _L1_conv_in["ln_b"],
        "L1_conv_in_proj_w": _L1_conv_in["in_proj_w"],
        "L1_conv_conv_w": _L1_conv_in["conv_w"],
        "L1_conv_conv_b": _L1_conv_in["conv_b"],
        "L1_conv_x_proj_w": _L1_conv_in["x_proj_w"],
        "L1_conv_dt_proj_w": _L1_conv_in["dt_proj_w"],
        "L1_conv_dt_proj_b": _L1_conv_in["dt_proj_b"],
        "L1_conv_A_log": _L1_conv_in["A_log"],
        "L1_conv_Ds": _L1_conv_in["Ds"],
        "L1_conv_out_norm_w": _L1_conv_in["out_norm_w"],
        "L1_conv_out_norm_b": _L1_conv_in["out_norm_b"],
        "L1_conv_out_proj_w": _L1_conv_in["out_proj_w"],
    }

def reference(x, L0_conv_g1, L0_conv_b1, L0_conv_w_qkv, L0_conv_w_dw, L0_conv_temp, L0_conv_w_head, L0_conv_w_proj, L0_conv_g2, L0_conv_b2, L0_conv_w_fc1, L0_conv_b_fc1, L0_conv_w_fc2, L0_conv_b_fc2, L0_conv_w_sa, L0_conv_b_sa, L1_conv_ln_w, L1_conv_ln_b, L1_conv_in_proj_w, L1_conv_conv_w, L1_conv_conv_b, L1_conv_x_proj_w, L1_conv_dt_proj_w, L1_conv_dt_proj_b, L1_conv_A_log, L1_conv_Ds, L1_conv_out_norm_w, L1_conv_out_norm_b, L1_conv_out_proj_w):
    import jax
    import jax.numpy as jnp
    def _L0_conv_ref(x, g1, b1, w_qkv, w_dw, temp, w_head, w_proj, g2, b2, w_fc1, b_fc1, w_fc2, b_fc2, w_sa, b_sa):
        import jax, jax.numpy as jnp
        import numpy as np
        DIM = 192
        HEADS = 6
        HIDDEN = 384

        def conv2d(x, w, b=None, padding=0, groups=1):
            out = jax.lax.conv_general_dilated(x, w, (1, 1), [(padding, padding), (padding, padding)], feature_group_count=groups, dimension_numbers=('NCHW', 'OIHW', 'NCHW'))
            return out if b is None else out + b[None, :, None, None]

        def layernorm(x, g, b, eps=1e-05):
            m = x.mean(-1, keepdims=True)
            v = x.var(-1, keepdims=True)
            return (x - m) / jnp.sqrt(v + eps) * g + b

        def l2norm(x, eps=1e-12):
            n = jnp.linalg.norm(x, axis=-1, keepdims=True)
            return x / jnp.maximum(n, eps)
        b, c, h, w = x.shape
        hw = h * w
        xf = x.reshape(b, c, hw).transpose(0, 2, 1)
        x1 = layernorm(xf, g1, b1).transpose(0, 2, 1).reshape(b, c, h, w)
        qkv = conv2d(conv2d(x1, w_qkv), w_dw, padding=1, groups=3 * c)
        q, k, v = jnp.split(qkv, 3, axis=1)
        cp = c // HEADS
        q = l2norm(q.reshape(b, HEADS, cp, hw))
        k = l2norm(k.reshape(b, HEADS, cp, hw))
        v = v.reshape(b, HEADS, cp, hw)
        attn = jnp.einsum('bhcn,bhdn->bhcd', q, k) * temp
        attn = conv2d(attn, w_head, padding=1)
        attn = jax.nn.softmax(attn, axis=-1)
        out = jnp.einsum('bhcd,bhdn->bhcn', attn, v).reshape(b, c, h, w)
        out = conv2d(out, w_proj)
        x2 = x1 + out
        x3 = x2.reshape(b, c, hw).transpose(0, 2, 1)
        y = layernorm(x3, g2, b2)
        y = jax.nn.gelu(y @ w_fc1.T + b_fc1, approximate=False)
        y = y @ w_fc2.T + b_fc2
        y = jax.nn.gelu(y, approximate=False)
        y4 = y.reshape(b, h, w, c).transpose(0, 3, 1, 2)
        gate = jax.nn.sigmoid(conv2d(y4, w_sa, b_sa, padding=1))
        y = (y4 * gate).reshape(b, c, hw).transpose(0, 2, 1)
        x4 = x3 + y
        return x4.transpose(0, 2, 1).reshape(b, c, h, w)

    def _L1_conv_ref(x, ln_w, ln_b, in_proj_w, conv_w, conv_b, x_proj_w, dt_proj_w, dt_proj_b, A_log, Ds, out_norm_w, out_norm_b, out_proj_w):
        import jax, jax.numpy as jnp
        import numpy as np
        B, C, H, W = (8, 192, 64, 64)
        D_INNER = 192
        N_STATE = 4
        DT_RANK = 12
        K_DIRS = 4

        def _ln_cf(x, w, b, eps=1e-05):
            mu = x.mean(1, keepdims=True)
            var = ((x - mu) ** 2).mean(1, keepdims=True)
            return (x - mu) / jnp.sqrt(var + eps) * w[None, :, None, None] + b[None, :, None, None]

        def _selective_scan(u, dt, A, Bv, Cv):

            def step(h, inp):
                dt_t, u_t, B_t, C_t = inp
                dA = jnp.exp(dt_t[..., None] * A)
                h = dA * h + dt_t[..., None] * B_t[:, :, None, :] * u_t[..., None]
                y = jnp.einsum('bkdn,bkn->bkd', h, C_t)
                return (h, y)
            h0 = jnp.zeros(u.shape[:3] + (A.shape[-1],), u.dtype)
            xs = (jnp.moveaxis(dt, -1, 0), jnp.moveaxis(u, -1, 0), jnp.moveaxis(Bv, -1, 0), jnp.moveaxis(Cv, -1, 0))
            _, ys = jax.lax.scan(step, h0, xs)
            return jnp.moveaxis(ys, 0, -1)
        R = dt_proj_w.shape[-1]
        N = A_log.shape[-1]
        xn = _ln_cf(x, ln_w, ln_b)
        xz = jnp.einsum('dc,bchw->bdhw', in_proj_w, xn)
        xc, z = jnp.split(xz, 2, axis=1)
        xc = jax.lax.conv_general_dilated(xc, conv_w, (1, 1), 'SAME', feature_group_count=xc.shape[1])
        xc = jax.nn.silu(xc + conv_b[None, :, None, None])
        Bsz, D, Hh, Ww = xc.shape
        L = Hh * Ww
        x_hw = xc.reshape(Bsz, D, L)
        x_wh = xc.transpose(0, 1, 3, 2).reshape(Bsz, D, L)
        xs = jnp.stack([x_hw, x_wh, x_hw[..., ::-1], x_wh[..., ::-1]], axis=1)
        x_dbl = jnp.einsum('kcd,bkdl->bkcl', x_proj_w, xs)
        dts, Bv, Cv = jnp.split(x_dbl, [R, R + N], axis=2)
        dt = jnp.einsum('kdr,bkrl->bkdl', dt_proj_w, dts) + dt_proj_b[None, :, :, None]
        dt = jax.nn.softplus(dt)
        A = -jnp.exp(A_log)
        ys = _selective_scan(xs, dt, A, Bv, Cv) + Ds[None, :, :, None] * xs
        y = ys[:, 0] + ys[:, 2, :, ::-1] + ys[:, 1].reshape(Bsz, D, Ww, Hh).transpose(0, 1, 3, 2).reshape(Bsz, D, L) + ys[:, 3, :, ::-1].reshape(Bsz, D, Ww, Hh).transpose(0, 1, 3, 2).reshape(Bsz, D, L)
        y = y.reshape(Bsz, D, Hh, Ww)
        y = _ln_cf(y, out_norm_w, out_norm_b)
        y = y * jax.nn.silu(z)
        out = jnp.einsum('cd,bdhw->bchw', out_proj_w, y)
        return x + out

    def _gn(v, G=32, eps=1e-5):
        B_, C_, H_, W_ = v.shape
        g = v.reshape(B_, G, C_ // G, H_, W_)
        m = jnp.mean(g, axis=(2, 3, 4), keepdims=True)
        s = jnp.var(g, axis=(2, 3, 4), keepdims=True)
        return ((g - m) / jnp.sqrt(s + eps)).reshape(v.shape)

    def _ln_c(v, eps=1e-6):
        m = jnp.mean(v, axis=1, keepdims=True)
        s = jnp.var(v, axis=1, keepdims=True)
        return (v - m) / jnp.sqrt(s + eps)

    def _ln_t(v, eps=1e-5):
        m = jnp.mean(v, axis=-1, keepdims=True)
        s = jnp.var(v, axis=-1, keepdims=True)
        return (v - m) / jnp.sqrt(s + eps)

    def _to_tokens(v):
        B_, C_, H_, W_ = v.shape
        return v.reshape(B_, C_, H_ * W_).transpose(0, 2, 1)
    def _from_tokens(t, like):
        B_, C_, H_, W_ = like.shape
        return t.transpose(0, 2, 1).reshape(B_, C_, H_, W_)

    x = _L0_conv_ref(x, L0_conv_g1, L0_conv_b1, L0_conv_w_qkv, L0_conv_w_dw, L0_conv_temp, L0_conv_w_head, L0_conv_w_proj, L0_conv_g2, L0_conv_b2, L0_conv_w_fc1, L0_conv_b_fc1, L0_conv_w_fc2, L0_conv_b_fc2, L0_conv_w_sa, L0_conv_b_sa)
    x = _L1_conv_ref(x, L1_conv_ln_w, L1_conv_ln_b, L1_conv_in_proj_w, L1_conv_conv_w, L1_conv_conv_b, L1_conv_x_proj_w, L1_conv_dt_proj_w, L1_conv_dt_proj_b, L1_conv_A_log, L1_conv_Ds, L1_conv_out_norm_w, L1_conv_out_norm_b, L1_conv_out_proj_w)
    return x


_drawn_inputs = setup_inputs


def setup_inputs(seed=0):
    import zlib

    import numpy as np

    out = dict(_drawn_inputs(seed))
    spreads = {'L0_conv_g1': (1.0, 0.2),
     'L0_conv_b1': (0.0, 0.1),
     'L0_conv_temp': (1.0, 0.6),
     'L0_conv_g2': (1.0, 0.6),
     'L0_conv_b2': (0.0, 0.8),
     'L0_conv_b_fc1': (0.0, 0.8),
     'L0_conv_b_fc2': (0.0, 0.341),
     'L1_conv_ln_w': (1.0, 0.6),
     'L1_conv_ln_b': (0.0, 0.8),
     'L1_conv_conv_b': (0.0, 0.1),
     'L1_conv_dt_proj_b': (-4.599999904632568, 0.6),
     'L1_conv_Ds': (1.0, 0.6),
     'L1_conv_out_norm_w': (1.0, 0.6),
     'L1_conv_out_norm_b': (0.0, 0.8)}
    factors = {'L0_conv_w_qkv': 8.0,
     'L0_conv_w_dw': 8.0,
     'L0_conv_w_head': 8.0,
     'L0_conv_w_proj': 8.0,
     'L0_conv_w_fc1': 3.909,
     'L0_conv_w_fc2': 3.548,
     'L0_conv_w_sa': 8.0,
     'L1_conv_conv_w': 8.0,
     'L1_conv_x_proj_w': 64.0,
     'L1_conv_dt_proj_w': 64.0,
     'L1_conv_A_log': 64.0}
    for name, (base, spread) in spreads.items():
        noise = np.random.default_rng([zlib.crc32(name.encode()), seed]).standard_normal(out[name].shape)
        drawn = base * np.exp(spread * noise) if base else spread * noise
        out[name] = jnp.asarray(drawn.astype(out[name].dtype))
    for name, factor in factors.items():
        out[name] = (out[name] * factor).astype(out[name].dtype)
    return out
```

```python
import concourse.bass as bass
from concourse import mybir
from contextlib import ExitStack
import numpy as np

FP32 = mybir.dt.float32
BF16 = mybir.dt.bfloat16
ALU = mybir.AluOpType
ACT = mybir.ActivationFunctionType
AXX = mybir.AxisListType.X

B, C, HH, WW = 4, 192, 128, 128
L = HH * WW
P = 96
ROWS = 4
NPX = ROWS * WW
CHUNKS = HH // ROWS
HEADS, HD = 6, 32
HID = 384
TAPS = [(dy, dx) for dy in range(3) for dx in range(3)]
PLANE = (HH + 2) * (WW + 2)
LN_EPS = 1e-5
DMA = 16


def attention_statistics(nc, d):
    with ExitStack() as ctx:
        def sb(name, shape, dt=FP32):
            return ctx.enter_context(nc.sbuf_tensor("a_" + name, shape, dt))

        def ps(name, shape):
            return ctx.enter_context(nc.psum_tensor("a_" + name, shape, FP32))

        sems = []
        ctx.callback(nc.all_engine_barrier)
        ctx.callback(nc.clear_and_free_semaphores, sems)

        def sem(name):
            sems.append(nc.alloc_semaphore("a_" + name))
            return sems[-1]

        mean_w = sb("mean_w", [P, P])
        ones = sb("ones", [P, P])
        ident = sb("ident", [P, P])
        ln_gb = sb("ln_gb", [P, 2, 2])
        wqkv = sb("wqkv", [P, 2, 3 * C])
        wdw = sb("wdw", [P, 6, 9])
        qdiag = sb("qdiag", [P, 2, 9, P])
        wproj = sb("wproj", [P, 2, C])
        temp = sb("temp", [P, 2])
        head_w = sb("head_w", [P, 2, 9, C])
        head_mask = sb("head_mask", [P, 2, 3, C])
        head_conv = sb("head_conv", [P, 2, 3, C])
        consts = sb("consts", [P, 2])
        x_in = [sb(f"x_in{p}", [P, 2, NPX]) for p in range(2)]
        xc = [sb(f"xc{p}", [P, 2, NPX]) for p in range(2)]
        sq = sb("sq", [P, 2, NPX])
        rstd = sb("rstd", [P, 2, NPX])
        x1 = [sb(f"x1{p}", [P, 2, NPX]) for p in range(2)]
        raw = [sb(f"raw{p}", [P, 6, ROWS + 2, WW + 2]) for p in range(2)]
        zeros = sb("zeros", [P, WW])
        kc = sb("kc", [P, 2, ROWS, WW])
        vc = [sb(f"vc{p}", [P, 2, ROWS, WW]) for p in range(2)]
        qkt = sb("qkt", [128, ROWS, 2, 2, P])
        gs = sb("gs", [P, 2, HD])
        dq = sb("dq", [P, 2, P])
        dk = sb("dk", [P, 2, P])
        nq = sb("nq", [P, 2])
        nk = sb("nk", [P, 2, HD])
        nqs = sb("nqs", [P, 2])
        nks = sb("nks", [P, 2, HD])
        s_pad = sb("s_pad", [P, 2, HD + 2])
        mx = sb("mx", [P, 2])
        ex = sb("ex", [P, 2, HD])
        sm = sb("sm", [P, 2])
        attn_bd = sb("attn_bd", [P, 2, P])
        mt = sb("mt", [P, 2, C])

        stat_ps = ps("stat_ps", [P, NPX])
        kt_ps = ps("kt_ps", [128, 2, 2, P])
        qkv_ps = [ps(f"qkv_ps{p}", [P, NPX]) for p in range(2)]
        qt_ps = [ps(f"qt_ps{p}", [128, 2, 2, P]) for p in range(2)]
        gram_ps = ps("gram_ps", [P, 2, 512])
        nk_ps = stat_ps[:, 0:2 * P].rearrange("p (h d) -> p h d", h=2)
        conv_ps = kt_ps[0:P, 0, 0, 0:2 * HD].rearrange("p (h d) -> p h d", h=2)
        mt_ps = qkv_ps[0][:, 0:2 * C].rearrange("p (h d) -> p h d", h=2)

        w_loaded = sem("w_loaded")
        w_ready = sem("w_ready")
        v_prep = sem("v_prep")
        x_loaded = [sem(f"x_loaded{p}") for p in range(2)]
        x1_stored = [sem(f"x1_stored{p}") for p in range(2)]
        v_stored = [sem(f"v_stored{p}") for p in range(2)]
        mt_stored = sem("mt_stored")
        img_done = sem("img_done")
        mu_ready = sem("mu_ready")
        xc_ready = sem("xc_ready")
        sq_ready = sem("sq_ready")
        var_ready = sem("var_ready")
        ln_done = sem("ln_done")
        r_ready = sem("r_ready")
        xr_done = sem("xr_done")
        x1_ready = sem("x1_ready")
        qkv_ready = sem("qkv_ready")
        qkv_evac = sem("qkv_evac")
        zero_row_ready = sem("zero_row_ready")
        zeros_ready = sem("zeros_ready")
        carried = sem("carried")
        raw_ready = sem("raw_ready")
        conv_seq = sem("conv_seq")
        qt_ready = sem("qt_ready")
        qt_evac = sem("qt_evac")
        kt_ready = sem("kt_ready")
        kt_evac = sem("kt_evac")
        gram_done = sem("gram_done")
        fin_v = sem("fin_v")
        fin_s = sem("fin_s")
        fin_t = sem("fin_t")
        FIN_V, FIN_S, FIN_T = 15, 2, 3

        loads = [(ident, d["ident"][0:P, 0:P]), (ln_gb, d["ln1_gb"]), (wqkv, d["wqkv"]), (wdw, d["wdw"]),
                 (wproj, d["wproj"]), (temp, d["temp"]), (head_w, d["head_w"]), (head_mask, d["head_mask"])]
        xv = d["x"].rearrange("b (h p) n -> b p h n", h=2)
        x1v = d["x1"].rearrange("b (h p) n -> b p h n", h=2)
        vv = d["v"].rearrange("b (h p) n -> b p h n", h=2)

        def image_loop(eng, start, step, end):
            with eng.Fori(0, B) as b:
                start(b)
                step(b, 0, 0, 0, "first")
                step(b, 1, 1, 0, "second")
                with eng.Fori(0, CHUNKS // 2 - 1) as j:
                    step(b, 2 * j + 2, 0, j + 1, "middle")
                    step(b, 2 * j + 3, 1, j + 1, "middle")
                end(b)

        def convolved(b, s):
            return b * (CHUNKS + 1) + s

        block = ctx.enter_context(nc.Block())

        @block.sync
        def _(sp):
            for dst, src in loads:
                sp.dma_start(dst[:], src).then_inc(w_loaded, DMA)

            def load(b, s, p, early):
                if early:
                    sp.wait_ge(img_done, b)
                else:
                    sp.wait_ge(xc_ready, b * CHUNKS + s - 1)
                sp.dma_start(x_in[p][:], xv[b, :, :, bass.ds(s * NPX, NPX)]).then_inc(x_loaded[p], DMA)

            def store_x1(b, s, p):
                sp.wait_ge(x1_ready, b * CHUNKS + s + 1)
                sp.dma_start(x1v[b, :, :, bass.ds(s * NPX, NPX)], x1[p][:]).then_inc(x1_stored[p], DMA)

            def store_v(b, s, p, lo, hi):
                sp.wait_ge(conv_seq, convolved(b, s) * 36 + 36)
                sp.dma_start(vv[b, :, :, bass.ds(s * NPX + (lo - 1) * WW, (hi - lo) * WW)],
                             vc[p][:, :, lo:hi, :].rearrange("p h r w -> p h (r w)")).then_inc(v_stored[p], DMA)

            with sp.Fori(0, B) as b:
                load(b, 0, 0, True)
                load(b, 1, 1, True)
                store_x1(b, 0, 0)
                load(b, 2, 0, False)
                store_x1(b, 1, 1)
                load(b, 3, 1, False)
                store_v(b, 0, 0, 1, ROWS)
                with sp.Fori(0, CHUNKS // 2 - 2) as j:
                    store_x1(b, 2 * j + 2, 0)
                    load(b, 2 * j + 4, 0, False)
                    store_v(b, 2 * j + 1, 1, 0, ROWS)
                    store_x1(b, 2 * j + 3, 1)
                    load(b, 2 * j + 5, 1, False)
                    store_v(b, 2 * j + 2, 0, 0, ROWS)
                store_x1(b, CHUNKS - 2, 0)
                store_v(b, CHUNKS - 3, 1, 0, ROWS)
                store_x1(b, CHUNKS - 1, 1)
                store_v(b, CHUNKS - 2, 0, 0, ROWS)
                store_v(b, CHUNKS - 1, 1, 0, ROWS)
                store_v(b, CHUNKS, 0, 0, 1)
                sp.wait_ge(img_done, b + 1)
                sp.dma_start(d["mt"][b], mt[:]).then_inc(mt_stored, DMA)
            for p in range(2):
                sp.wait_ge(x1_stored[p], DMA * B * CHUNKS // 2)
            sp.wait_ge(v_stored[0], DMA * B * (CHUNKS // 2 + 1))
            sp.wait_ge(v_stored[1], DMA * B * (CHUNKS // 2))
            sp.wait_ge(mt_stored, DMA * B)

        @block.gpsimd
        def _(pool):
            nc.gpsimd.memset(mean_w[:], 1.0 / C)
            nc.gpsimd.memset(ones[:], 1.0)
            nc.gpsimd.memset(consts[:, 0:1], LN_EPS)
            nc.gpsimd.memset(consts[:, 1:2], 0.0)
            nc.gpsimd.memset(s_pad[:], 0.0)
            nc.gpsimd.memset(attn_bd[:], 0.0)
            nc.gpsimd.memset(zeros[:], 0.0).then_inc(zero_row_ready, 1)
            for p in range(2):
                nc.gpsimd.memset(raw[p][:, :, :, 0:1], 0.0)
                last = nc.gpsimd.memset(raw[p][:, :, :, WW + 1:WW + 2], 0.0)
            last.then_inc(w_ready, 1)
            def clear(rows):
                z = zeros[:, None, None, :].to_broadcast(rows.shape)
                nc.gpsimd.tensor_tensor(rows, z, z, ALU.add).then_inc(zeros_ready, 1)

            with pool.Fori(0, B) as b:
                pool.wait_ge(zero_row_ready, 1)
                pool.wait_ge(img_done, b)
                clear(raw[0][:, :, 0:2, 1:WW + 1])
                pool.wait_ge(conv_seq, convolved(b, CHUNKS - 1) * 36)
                pool.wait_ge(qt_ready, convolved(b, CHUNKS - 1) * 2)
                clear(raw[0][:, :, 2:3, 1:WW + 1])

        @block.vector
        def _(dve):
            dve.wait_ge(w_loaded, DMA * len(loads))
            for h in range(2):
                for t in range(9):
                    nc.vector.tensor_scalar(qdiag[:, h, t, :], ident[:], wdw[:, h, t:t + 1], None, ALU.mult)
            for dx in range(3):
                nc.vector.tensor_tensor(head_w[:, :, 3 * dx:3 * dx + 3, :], head_w[:, :, 3 * dx:3 * dx + 3, :],
                                        head_mask[:], ALU.mult).then_inc(v_prep, 1)
            dve.wait_ge(v_prep, 3)
            hw = head_w[:].rearrange("p h (x y) c -> p h x y c", x=3)
            for h in range(2):
                nc.vector.tensor_tensor(head_conv[:, h], hw[:, h, :, 0, :], hw[:, h, :, 1, :], ALU.add).then_inc(v_prep, 1)
            dve.wait_ge(v_prep, 5)
            for h in range(2):
                last = nc.vector.tensor_tensor(head_conv[:, h], head_conv[:, h], hw[:, h, :, 2, :], ALU.add)
            last.then_inc(w_ready, 1)
            dve.wait_ge(w_ready, 2)

            def conv(b, s, p, src, out, op0):
                done = convolved(b, s) * 36 + op0
                for t, (dy, dx) in enumerate(TAPS):
                    for h in range(2):
                        window = raw[p][:, src + h, dy:dy + ROWS, dx:dx + WW]
                        w = wdw[:, src + h, t:t + 1]
                        if t == 0:
                            ins = nc.vector.tensor_scalar(out[:, h], window, w, None, ALU.mult)
                        else:
                            dve.wait_ge(conv_seq, done + 2 * t + h - 1)
                            ins = nc.vector.scalar_tensor_tensor(out[:, h], window, w, out[:, h], ALU.mult, ALU.add)
                        ins.then_inc(conv_seq, 1)

            def conv_k(b, s, p):
                dve.wait_ge(raw_ready, convolved(b, s) + 1)
                dve.wait_ge(kt_ready, convolved(b, s) * 2)
                conv(b, s, p, 2, kc, 0)

            def conv_v(b, s, p, half):
                dve.wait_ge(v_stored[p], (b * (CHUNKS // 2 + 1 - p) + half) * DMA)
                conv(b, s, p, 4, vc[p], 18)

            def start(b):
                pass

            def step(b, s, p, half, kind):
                q = b * CHUNKS + s
                half_before = half - 1 + p
                dve.wait_ge(mu_ready, q + 1)
                if kind != "first":
                    dve.wait_ge(x1_ready, q)
                mu = stat_ps[:].unsqueeze(1).broadcast_to([P, 2, NPX])
                nc.vector.tensor_tensor(xc[p][:], x_in[p][:], mu, ALU.subtract).then_inc(xc_ready, 1)
                if kind != "first":
                    conv_k(b, s - 1, 1 - p)
                dve.wait_ge(r_ready, q + 1)
                dve.wait_ge(xc_ready, q + 1)
                r = rstd[:, 1:2, :].broadcast_to([P, 2, NPX])
                nc.vector.tensor_tensor(xc[p][:], xc[p][:], r, ALU.mult).then_inc(xr_done, 1)
                dve.wait_ge(xr_done, q + 1)
                dve.wait_ge(x1_stored[p], (b * (CHUNKS // 2) + half) * DMA)
                if kind == "middle":
                    dve.wait_ge(qkv_ready, (q - 1) * 6)
                for h in range(2):
                    last = nc.vector.tensor_scalar(x1[p][:, h], xc[p][:, h], ln_gb[:, h, 0:1], ln_gb[:, h, 1:2],
                                                   ALU.mult, ALU.add)
                last.then_inc(x1_ready, 1)
                if kind != "first":
                    conv_v(b, s - 1, 1 - p, half_before)

            def end(b):
                conv_k(b, CHUNKS - 1, 1)
                conv_v(b, CHUNKS - 1, 1, CHUNKS // 2 - 1)
                conv_k(b, CHUNKS, 0)
                conv_v(b, CHUNKS, 0, CHUNKS // 2)
                n = [0]

                def link(ins):
                    n[0] += 1
                    ins.then_inc(fin_v, 1)
                    return n[0]

                def after(k):
                    dve.wait_ge(fin_v, b * FIN_V + k)

                dve.wait_ge(gram_done, convolved(b, CHUNKS + 1))
                eye = ident[:].unsqueeze(1).broadcast_to([P, 2, P])
                nc.vector.tensor_tensor(dk[:], gram_ps[:, :, 2 * P:3 * P], eye, ALU.mult).then_inc(fin_v, 1)
                n[0] = 1
                dq_done = link(nc.vector.tensor_tensor(dq[:], gram_ps[:, :, 0:P], eye, ALU.mult))
                for j in range(3):
                    r = slice(32 * j, 32 * j + 32)
                    last = nc.vector.tensor_copy(gs[r], gram_ps[r, :, P + 32 * j:P + 32 * j + 32])
                gs_done = link(last)
                after(dq_done)
                link(nc.vector.reduce_sum(nq[:], dq[:], axis=AXX))
                dve.wait_ge(fin_t, b * FIN_T + 1)
                for j in range(3):
                    r = slice(32 * j, 32 * j + 32)
                    last = nc.vector.tensor_copy(nk[r], nk_ps[r, :, 32 * j:32 * j + 32])
                link(last)
                dve.wait_ge(fin_s, b * FIN_S + 1)
                k = link(nc.vector.tensor_scalar(nqs[:], nqs[:], 1e-12, None, ALU.max))
                link(nc.vector.tensor_scalar(nks[:], nks[:], 1e-12, None, ALU.max))
                after(k + 1)
                link(nc.vector.reciprocal(nqs[:], nqs[:]))
                k = link(nc.vector.reciprocal(nks[:], nks[:]))
                after(k)
                for h in range(2):
                    last = nc.vector.tensor_scalar(gs[:, h], gs[:, h], nqs[:, h:h + 1], temp[:, h:h + 1],
                                                   ALU.mult, ALU.mult)
                k = link(last)
                after(k)
                k = link(nc.vector.tensor_tensor(s_pad[:, :, 1:HD + 1], gs[:], nks[:], ALU.mult))
                dve.wait_ge(fin_t, b * FIN_T + 2)
                k = link(nc.vector.reduce_max(mx[:], conv_ps, axis=AXX))
                after(k)
                link(nc.vector.tensor_scalar(mx[:], mx[:], -1.0, None, ALU.mult))
                dve.wait_ge(fin_s, b * FIN_S + 2)
                k = link(nc.vector.reciprocal(sm[:], sm[:]))
                after(k)
                for h in range(2):
                    for j in range(3):
                        r = slice(32 * j, 32 * j + 32)
                        last = nc.vector.tensor_scalar(attn_bd[r, h, r], ex[r, h], sm[r, h:h + 1], None, ALU.mult)
                link(last)
                assert n[0] == FIN_V
                dve.wait_ge(fin_t, b * FIN_T + 3)
                dve.wait_ge(mt_stored, b * DMA)
                nc.vector.tensor_copy(mt[:], mt_ps).then_inc(img_done, 1)

            image_loop(dve, start, step, end)

        @block.scalar
        def _(act):
            act.wait_ge(w_ready, 2)

            def carry(b, s, p):
                act.wait_ge(conv_seq, convolved(b, s - 1) * 36)
                act.wait_ge(qt_ready, convolved(b, s - 1) * 2)
                act.wait_ge(raw_ready, convolved(b, s))
                nc.scalar.copy(raw[p][:, :, 0:2, 1:WW + 1], raw[1 - p][:, :, ROWS:ROWS + 2, 1:WW + 1]).then_inc(carried, 1)

            def evac_q(b, s):
                c = convolved(b, s)
                act.wait_ge(gram_done, c)
                for i in range(2):
                    act.wait_ge(qt_ready, c * 2 + i + 1)
                    nc.scalar.copy(qkt[:, 2 * i:2 * i + 2, :, 0, :], qt_ps[i][:]).then_inc(qt_evac, 1)

            def evac_k(b, s, i):
                act.wait_ge(kt_ready, convolved(b, s) * 2 + i + 1)
                nc.scalar.copy(qkt[:, 2 * i:2 * i + 2, :, 1, :], kt_ps[:]).then_inc(kt_evac, 1)

            def evac_qkv(b, s, p, tiles):
                for t in tiles:
                    act.wait_ge(qkv_ready, (b * CHUNKS + s) * 6 + t + 1)
                    nc.scalar.copy(raw[p][:, t, 2:ROWS + 2, 1:WW + 1],
                                   qkv_ps[t % 2][:].rearrange("p (r w) -> p r w", w=WW)).then_inc(qkv_evac, 1)

            def start(b):
                pass

            def step(b, s, p, half, kind):
                q = b * CHUNKS + s
                act.wait_ge(xc_ready, q + 1)
                act.wait_ge(var_ready, q)
                nc.scalar.activation(sq[:], xc[p][:], ACT.Square).then_inc(sq_ready, 1)
                if kind != "first":
                    carry(b, s, p)
                act.wait_ge(var_ready, q + 1)
                act.wait_ge(xr_done, q)
                nc.scalar.activation(rstd[:, 0], stat_ps[:], ACT.Ln, bias=consts[:, 0:1]).then_inc(ln_done, 1)
                act.wait_ge(ln_done, q + 1)
                nc.scalar.activation(rstd[:, 1], rstd[:, 0], ACT.Exp, scale=-0.5, bias=consts[:, 1:2]).then_inc(r_ready, 1)
                if kind == "first":
                    act.wait_ge(zeros_ready, b * 2 + 1)
                else:
                    evac_q(b, s - 1)
                    evac_k(b, s - 1, 0)
                evac_qkv(b, s, p, range(0, 3))
                if kind != "first":
                    evac_k(b, s - 1, 1)
                evac_qkv(b, s, p, range(3, 6))
                act.wait_ge(qkv_evac, q * 6 + 6)
                act.sem_inc(raw_ready, 1)

            def end(b):
                evac_q(b, CHUNKS - 1)
                evac_k(b, CHUNKS - 1, 0)
                evac_k(b, CHUNKS - 1, 1)
                carry(b, CHUNKS, 0)
                act.wait_ge(zeros_ready, b * 2 + 2)
                act.wait_ge(carried, (b + 1) * CHUNKS)
                act.sem_inc(raw_ready, 1)
                evac_q(b, CHUNKS)
                evac_k(b, CHUNKS, 0)
                evac_k(b, CHUNKS, 1)
                nc.scalar.preload_act_table_set("sqrt_and_others")
                act.wait_ge(fin_v, b * FIN_V + 5)
                nc.scalar.activation(nqs[:], nq[:], ACT.Sqrt, bias=consts[:, 1:2])
                nc.scalar.activation(nks[:], nk[:], ACT.Sqrt, bias=consts[:, 1:2]).then_inc(fin_s, 1)
                nc.scalar.preload_act_table_set("natural_log_exp_and_others")
                act.wait_ge(fin_v, b * FIN_V + 13)
                for h in range(2):
                    last = nc.scalar.activation(ex[:, h], conv_ps[:, h], ACT.Exp, bias=mx[:, h:h + 1],
                                                accum_out=sm[:, h:h + 1])
                last.then_inc(fin_s, 1)

            nc.scalar.preload_act_table_set("natural_log_exp_and_others")
            image_loop(act, start, step, end)

        @block.tensor
        def _(pe):
            pe.wait_ge(w_ready, 2)
            pe.wait_ge(w_loaded, DMA * len(loads))

            def q_conv(b, s, p, i):
                c = convolved(b, s)
                pe.wait_ge(qt_evac, c * 2)
                for r in range(2):
                    for h in range(2):
                        for t, (dy, dx) in enumerate(TAPS):
                            last = nc.tensor.matmul(qt_ps[i][:, r, h], raw[p][:, h, 2 * i + r + dy, dx:dx + WW],
                                                    qdiag[:, h, t], start=(t == 0), stop=(t == 8))
                last.then_inc(qt_ready, 1)

            def k_transpose(b, s, i):
                c = convolved(b, s)
                pe.wait_ge(conv_seq, c * 36 + 18)
                pe.wait_ge(kt_evac, c * 2 + i)
                for r in range(2):
                    for h in range(2):
                        last = nc.tensor.transpose(kt_ps[:, r, h], kc[:, h, 2 * i + r], ident[:])
                last.then_inc(kt_ready, 1)

            def gram(b, s, rows, first):
                c = convolved(b, s)
                pe.wait_ge(qt_evac, c * 2 + 2)
                pe.wait_ge(kt_evac, c * 2 + 2)
                for n, r in enumerate(rows):
                    for h in range(2):
                        nc.tensor.matmul(gram_ps[:, h, 0:2 * P], qkt[:, r, h, 0], qkt[:, r, h],
                                         start=first and n == 0, stop=True, skip_group_check=True)
                        last = nc.tensor.matmul(gram_ps[:, h, 2 * P:3 * P], qkt[:, r, h, 1], qkt[:, r, h, 1],
                                                start=False, stop=True, skip_group_check=True)
                last.then_inc(gram_done, 1)

            def qkv(b, s, p, tiles):
                q = b * CHUNKS + s
                pe.wait_ge(x1_ready, q + 1)
                for t in tiles:
                    if t >= 2:
                        pe.wait_ge(qkv_evac, q * 6 + t - 1)
                    for h in range(2):
                        last = nc.tensor.matmul(qkv_ps[t % 2][:], wqkv[:, h, t * P:(t + 1) * P], x1[p][:, h],
                                                start=(h == 0), stop=(h == 1))
                    last.then_inc(qkv_ready, 1)

            def start(b):
                pe.wait_ge(img_done, b)

            def step(b, s, p, half, kind):
                q = b * CHUNKS + s
                conv = kind != "first"
                pe.wait_ge(x_loaded[p], (b * (CHUNKS // 2) + half + 1) * DMA)
                pe.wait_ge(r_ready, q)
                for h in range(2):
                    last = nc.tensor.matmul(stat_ps[:], mean_w[:], x_in[p][:, h], start=(h == 0), stop=(h == 1))
                last.then_inc(mu_ready, 1)
                if conv:
                    pe.wait_ge(raw_ready, convolved(b, s))
                    q_conv(b, s - 1, 1 - p, 0)
                pe.wait_ge(sq_ready, q + 1)
                for h in range(2):
                    last = nc.tensor.matmul(stat_ps[:], mean_w[:], sq[:, h], start=(h == 0), stop=(h == 1))
                last.then_inc(var_ready, 1)
                if conv:
                    q_conv(b, s - 1, 1 - p, 1)
                    k_transpose(b, s - 1, 0)
                    pe.wait_ge(qkv_evac, q * 6)
                qkv(b, s, p, range(0, 3))
                if conv:
                    k_transpose(b, s - 1, 1)
                qkv(b, s, p, range(3, 6))
                if conv:
                    gram(b, s - 1, range(1, ROWS) if kind == "second" else range(ROWS), kind == "second")

            def end(b):
                pe.wait_ge(raw_ready, convolved(b, CHUNKS))
                for s, p, rows in ((CHUNKS - 1, 1, range(ROWS)), (CHUNKS, 0, range(1))):
                    pe.wait_ge(raw_ready, convolved(b, s) + 1)
                    q_conv(b, s, p, 0)
                    q_conv(b, s, p, 1)
                    k_transpose(b, s, 0)
                    k_transpose(b, s, 1)
                    gram(b, s, rows, False)
                pe.wait_ge(fin_v, b * FIN_V + 1)
                for h in range(2):
                    last = nc.tensor.matmul(nk_ps[:, h], ones[:], dk[:, h], start=True, stop=True)
                last.then_inc(fin_t, 1)
                pe.wait_ge(fin_v, b * FIN_V + 11)
                for o in range(2):
                    for n, (h, dx) in enumerate((h, dx) for h in range(2) for dx in range(3)):
                        last = nc.tensor.matmul(conv_ps[:, o], head_conv[:, h, dx, o * P:(o + 1) * P],
                                                s_pad[:, h, dx:dx + HD], start=(n == 0), stop=(n == 5))
                last.then_inc(fin_t, 1)
                pe.wait_ge(fin_v, b * FIN_V + 15)
                for h in range(2):
                    last = nc.tensor.matmul(mt_ps[:, h], attn_bd[:, h], wproj[:, h], start=True, stop=True)
                last.then_inc(fin_t, 1)

            image_loop(pe, start, step, end)


def attention_and_mlp(nc, d):
    with ExitStack() as ctx:
        def sb(name, shape, dt=FP32):
            return ctx.enter_context(nc.sbuf_tensor("b_" + name, shape, dt))

        def ps(name, shape):
            return ctx.enter_context(nc.psum_tensor("b_" + name, shape, FP32))

        sems = []
        ctx.callback(nc.all_engine_barrier)
        ctx.callback(nc.clear_and_free_semaphores, sems)

        def sem(name):
            sems.append(nc.alloc_semaphore("b_" + name))
            return sems[-1]

        mean_w = sb("mean_w", [P, P])
        ln_gb = sb("ln_gb", [P, 2, 2])
        w1 = sb("w1", [P, 2, HID])
        b1 = sb("b1", [128, 3])
        w2 = sb("w2", [128, 3, C])
        b2 = sb("b2", [P, 2])
        wsa = sb("wsa", [P, 2, 9])
        consts = sb("consts", [P, 2])
        zeros = sb("zeros", [9 * PLANE // 1300, 1300])
        mt = sb("mt", [P, 2, C])
        x1 = [sb(f"x1{p}", [P, 2, NPX]) for p in range(2)]
        v = [sb(f"v{p}", [P, 2, NPX]) for p in range(2)]
        x2 = [sb(f"x2{p}", [P, 2, NPX]) for p in range(2)]
        xn = [sb(f"xn{p}", [P, 2, NPX]) for p in range(2)]
        xg = [sb(f"xg{p}", [P, 2, NPX]) for p in range(2)]
        sq = sb("sq", [P, 2, NPX])
        rstd = sb("rstd", [P, 2, NPX])
        hid = sb("hid", [128, 3, NPX])
        y = [sb(f"y{p}", [P, 2, NPX]) for p in range(2)]
        taps = [sb(f"taps{p}", [9, NPX]) for p in range(2)]

        o_ps = ps("o_ps", [P, 2, NPX])
        stat_ps = ps("stat_ps", [P, NPX])
        h_ps = [ps(f"h_ps{p}", [128, NPX]) for p in range(2)]
        y_ps = [ps(f"y_ps{p}", [P, NPX]) for p in range(2)]
        taps_ps = ps("taps_ps", [9, NPX])

        w_loaded = sem("w_loaded")
        w_ready = sem("w_ready")
        border_zero = sem("border_zero")
        mt_loaded = sem("mt_loaded")
        xv_loaded = [sem(f"xv_loaded{p}") for p in range(2)]
        x2_stored = [sem(f"x2_stored{p}") for p in range(2)]
        y_stored = [sem(f"y_stored{p}") for p in range(2)]
        o_ready = sem("o_ready")
        x2_ready = sem("x2_ready")
        mu_ready = sem("mu_ready")
        xc_ready = sem("xc_ready")
        sq_ready = sem("sq_ready")
        var_ready = sem("var_ready")
        ln_done = sem("ln_done")
        r_ready = sem("r_ready")
        xr_done = sem("xr_done")
        xg_ready = sem("xg_ready")
        h_ready = sem("h_ready")
        h_gelu = sem("h_gelu")
        y_ready = sem("y_ready")
        y_gelu = sem("y_gelu")
        taps_ready = sem("taps_ready")
        taps_copied = sem("taps_copied")

        loads = [(ln_gb, d["ln2_gb"]), (w1, d["w1"]), (b1, d["b1"]), (w2, d["w2"]), (b2, d["b2"]), (wsa, d["wsa"])]
        x1v, vv, x2v, yv = (d[k].rearrange("b (h p) n -> b p h n", h=2) for k in ("x1", "v", "x2", "y"))
        planes = d["planes"][:, 0:9 * PLANE].rearrange("b (t r c) -> b t r c", t=9, c=WW + 2)

        def image_loop(eng, start, step, end):
            with eng.Fori(0, B) as b:
                start(b)
                step(b, 0, 0, 0, True)
                step(b, 1, 1, 0, False)
                with eng.Fori(0, CHUNKS // 2 - 1) as j:
                    step(b, 2 * j + 2, 0, j + 1, False)
                    step(b, 2 * j + 3, 1, j + 1, False)
                end(b)

        block = ctx.enter_context(nc.Block())

        @block.sync
        def _(sp):
            for dst, src in loads:
                sp.dma_start(dst[:], src).then_inc(w_loaded, DMA)
            sp.wait_ge(w_ready, 1)
            for b in range(B):
                sp.dma_start(d["planes"][b, 0:9 * PLANE].rearrange("(p n) -> p n", n=1300), zeros[:]).then_inc(border_zero, DMA)
            sp.wait_ge(border_zero, DMA * B)

            def load(b, s, p, half):
                if isinstance(s, int) and s < 2:
                    sp.wait_ge(x2_ready, b * CHUNKS)
                else:
                    sp.wait_ge(x2_ready, b * CHUNKS + s - 1)
                px = bass.ds(s * NPX, NPX)
                sp.dma_start(x1[p][:], x1v[b, :, :, px]).then_inc(xv_loaded[p], DMA)
                sp.dma_start(v[p][:], vv[b, :, :, px]).then_inc(xv_loaded[p], DMA)

            def store_x2(b, s, p):
                sp.wait_ge(x2_ready, b * CHUNKS + s + 1)
                sp.dma_start(x2v[b, :, :, bass.ds(s * NPX, NPX)], x2[p][:]).then_inc(x2_stored[p], DMA)

            def store_y(b, s, p):
                q = b * CHUNKS + s
                sp.wait_ge(y_gelu, (q + 1) * 2)
                sp.dma_start(yv[b, :, :, bass.ds(s * NPX, NPX)], y[p][:]).then_inc(y_stored[p], DMA)
                sp.wait_ge(taps_copied, q + 1)
                sp.dma_start(planes[b, :, bass.ds(s * ROWS + 1, ROWS), 1:WW + 1],
                             taps[p][:].rearrange("t (r w) -> t r w", w=WW)).then_inc(y_stored[p], DMA)

            with sp.Fori(0, B) as b:
                sp.wait_ge(o_ready, b * CHUNKS)
                sp.dma_start(mt[:], d["mt"][b]).then_inc(mt_loaded, DMA)
                load(b, 0, 0, 0)
                load(b, 1, 1, 0)
                store_x2(b, 0, 0)
                load(b, 2, 0, 1)
                store_x2(b, 1, 1)
                load(b, 3, 1, 1)
                store_y(b, 0, 0)
                with sp.Fori(0, CHUNKS // 2 - 2) as j:
                    store_x2(b, 2 * j + 2, 0)
                    load(b, 2 * j + 4, 0, j + 2)
                    store_y(b, 2 * j + 1, 1)
                    store_x2(b, 2 * j + 3, 1)
                    load(b, 2 * j + 5, 1, j + 2)
                    store_y(b, 2 * j + 2, 0)
                store_x2(b, CHUNKS - 2, 0)
                store_y(b, CHUNKS - 3, 1)
                store_x2(b, CHUNKS - 1, 1)
                store_y(b, CHUNKS - 2, 0)
                store_y(b, CHUNKS - 1, 1)
            for p in range(2):
                sp.wait_ge(x2_stored[p], DMA * B * CHUNKS // 2)
                sp.wait_ge(y_stored[p], DMA * B * CHUNKS)

        @block.gpsimd
        def _(pool):
            nc.gpsimd.memset(zeros[:], 0.0)
            nc.gpsimd.memset(mean_w[:], 1.0 / C)
            nc.gpsimd.memset(consts[:, 0:1], LN_EPS)
            nc.gpsimd.memset(consts[:, 1:2], 0.0).then_inc(w_ready, 1)

        @block.vector
        def _(dve):
            dve.wait_ge(w_loaded, DMA * len(loads))

            def copy_taps(b, s, p, half):
                q = b * CHUNKS + s
                dve.wait_ge(taps_ready, q + 1)
                dve.wait_ge(y_stored[p], (b * (CHUNKS // 2) + half) * 2 * DMA)
                nc.vector.tensor_copy(taps[p][:], taps_ps[:]).then_inc(taps_copied, 1)

            def step(b, s, p, half, first):
                q = b * CHUNKS + s
                dve.wait_ge(o_ready, q + 1)
                dve.wait_ge(x2_stored[p], (b * (CHUNKS // 2) + half) * DMA)
                nc.vector.tensor_tensor(x2[p][:], x1[p][:], o_ps[:], ALU.add).then_inc(x2_ready, 1)
                dve.wait_ge(mu_ready, q + 1)
                dve.wait_ge(x2_ready, q + 1)
                dve.wait_ge(xg_ready, q)
                mu = stat_ps[:].unsqueeze(1).broadcast_to([P, 2, NPX])
                nc.vector.tensor_tensor(xn[p][:], x2[p][:], mu, ALU.subtract).then_inc(xc_ready, 1)
                dve.wait_ge(r_ready, q + 1)
                dve.wait_ge(xc_ready, q + 1)
                r = rstd[:, 1:2, :].broadcast_to([P, 2, NPX])
                nc.vector.tensor_tensor(xn[p][:], xn[p][:], r, ALU.mult).then_inc(xr_done, 1)
                dve.wait_ge(xr_done, q + 1)
                for h in range(2):
                    last = nc.vector.tensor_scalar(xg[p][:, h], xn[p][:, h], ln_gb[:, h, 0:1], ln_gb[:, h, 1:2],
                                                   ALU.mult, ALU.add)
                last.then_inc(xg_ready, 1)
                if not first:
                    copy_taps(b, s - 1, 1 - p, half - 1 + p)

            def start(b):
                pass

            def end(b):
                copy_taps(b, CHUNKS - 1, 1, CHUNKS // 2 - 1)

            image_loop(dve, start, step, end)

        @block.scalar
        def _(act):
            act.wait_ge(w_ready, 1)
            act.wait_ge(w_loaded, DMA * len(loads))

            def gelu_h(b, s):
                nc.scalar.preload_act_table_set("gelu_and_others")
                q = b * CHUNKS + s
                act.wait_ge(y_ready, q * 2)
                for t in range(3):
                    act.wait_ge(h_ready, q * 3 + t + 1)
                    nc.scalar.activation(hid[:, t], h_ps[t % 2][:], ACT.Gelu, bias=b1[:, t:t + 1]).then_inc(h_gelu, 1)

            def gelu_y(b, s, p, half):
                q = b * CHUNKS + s
                act.wait_ge(y_stored[p], (b * (CHUNKS // 2) + half) * 2 * DMA)
                for h in range(2):
                    act.wait_ge(y_ready, q * 2 + h + 1)
                    nc.scalar.activation(y[p][:, h], y_ps[h][:], ACT.Gelu, bias=b2[:, h:h + 1]).then_inc(y_gelu, 1)

            def start(b):
                pass

            def step(b, s, p, half, first):
                q = b * CHUNKS + s
                if not first:
                    gelu_h(b, s - 1)
                act.wait_ge(xc_ready, q + 1)
                act.wait_ge(var_ready, q)
                nc.scalar.activation(sq[:], xn[p][:], ACT.Square).then_inc(sq_ready, 1)
                if not first:
                    gelu_y(b, s - 1, 1 - p, half - 1 + p)
                nc.scalar.preload_act_table_set("natural_log_exp_and_others")
                act.wait_ge(var_ready, q + 1)
                act.wait_ge(xr_done, q)
                nc.scalar.activation(rstd[:, 0], stat_ps[:], ACT.Ln, bias=consts[:, 0:1]).then_inc(ln_done, 1)
                act.wait_ge(ln_done, q + 1)
                nc.scalar.activation(rstd[:, 1], rstd[:, 0], ACT.Exp, scale=-0.5, bias=consts[:, 1:2]).then_inc(r_ready, 1)

            def end(b):
                gelu_h(b, CHUNKS - 1)
                gelu_y(b, CHUNKS - 1, 1, CHUNKS // 2 - 1)

            image_loop(act, start, step, end)

        @block.tensor
        def _(pe):
            pe.wait_ge(w_ready, 1)
            pe.wait_ge(w_loaded, DMA * len(loads))

            def fc1(b, s, p, tiles):
                q = b * CHUNKS + s
                pe.wait_ge(xg_ready, q + 1)
                for t in tiles:
                    pe.wait_ge(h_gelu, q * 3 + t - 1 if t >= 2 else q * 3)
                    for h in range(2):
                        last = nc.tensor.matmul(h_ps[t % 2][:], w1[:, h, 128 * t:128 * t + 128], xg[p][:, h],
                                                start=(h == 0), stop=(h == 1))
                    last.then_inc(h_ready, 1)

            def fc2(b, s, h):
                q = b * CHUNKS + s
                pe.wait_ge(h_gelu, q * 3 + 3)
                pe.wait_ge(y_gelu, q * 2)
                for t in range(3):
                    last = nc.tensor.matmul(y_ps[h][:], w2[:, t, P * h:P * h + P], hid[:, t], start=(t == 0), stop=(t == 2))
                last.then_inc(y_ready, 1)

            def gate_taps(b, s, p):
                q = b * CHUNKS + s
                pe.wait_ge(taps_copied, q)
                for h in range(2):
                    pe.wait_ge(y_gelu, q * 2 + h + 1)
                    last = nc.tensor.matmul(taps_ps[:], wsa[:, h], y[p][:, h], start=(h == 0), stop=(h == 1))
                last.then_inc(taps_ready, 1)

            def start(b):
                pe.wait_ge(mt_loaded, (b + 1) * DMA)

            def step(b, s, p, half, first):
                q = b * CHUNKS + s
                pe.wait_ge(xv_loaded[p], (b * (CHUNKS // 2) + half + 1) * 2 * DMA)
                pe.wait_ge(x2_ready, q)
                for o in range(2):
                    for h in range(2):
                        last = nc.tensor.matmul(o_ps[:, o], mt[:, h, P * o:P * o + P], v[p][:, h],
                                                start=(h == 0), stop=(h == 1))
                last.then_inc(o_ready, 1)
                if not first:
                    fc1(b, s - 1, 1 - p, range(0, 2))
                pe.wait_ge(x2_ready, q + 1)
                pe.wait_ge(r_ready, q)
                for h in range(2):
                    last = nc.tensor.matmul(stat_ps[:], mean_w[:], x2[p][:, h], start=(h == 0), stop=(h == 1))
                last.then_inc(mu_ready, 1)
                if not first:
                    fc1(b, s - 1, 1 - p, range(2, 3))
                    fc2(b, s - 1, 0)
                pe.wait_ge(sq_ready, q + 1)
                for h in range(2):
                    last = nc.tensor.matmul(stat_ps[:], mean_w[:], sq[:, h], start=(h == 0), stop=(h == 1))
                last.then_inc(var_ready, 1)
                if not first:
                    fc2(b, s - 1, 1)
                    gate_taps(b, s - 1, 1 - p)

            def end(b):
                fc1(b, CHUNKS - 1, 1, range(3))
                fc2(b, CHUNKS - 1, 0)
                fc2(b, CHUNKS - 1, 1)
                gate_taps(b, CHUNKS - 1, 1)

            image_loop(pe, start, step, end)


DIRS, RANK, STATES = 4, 12, 4
NDT, NBC = DIRS * RANK, DIRS * 2 * STATES


def gate_and_scan_inputs(nc, d):
    with ExitStack() as ctx:
        def sb(name, shape, dt=FP32):
            return ctx.enter_context(nc.sbuf_tensor("c_" + name, shape, dt))

        def ps(name, shape):
            return ctx.enter_context(nc.psum_tensor("c_" + name, shape, FP32))

        sems = []
        ctx.callback(nc.all_engine_barrier)
        ctx.callback(nc.clear_and_free_semaphores, sems)

        def sem(name):
            sems.append(nc.alloc_semaphore("c_" + name))
            return sems[-1]

        mean_w = sb("mean_w", [P, P])
        ones = sb("ones", [9, P])
        ln_gb = sb("ln_gb", [P, 2, 2])
        w_in = sb("w_in", [P, 2, 2 * C])
        cw = sb("cw", [P, 2, 9])
        cb = sb("cb", [P, 2])
        w_x = sb("w_x", [P, 2, NDT + NBC])
        b_sa = sb("b_sa", [P, 1])
        consts = sb("consts", [P, 2])
        x2 = [sb(f"x2{p}", [P, 2, NPX]) for p in range(2)]
        y = [sb(f"y{p}", [P, 2, NPX]) for p in range(2)]
        taps = [sb(f"taps{p}", [9, NPX]) for p in range(2)]
        gate = sb("gate", [P, NPX])
        x4 = [sb(f"x4{p}", [P, 2, NPX]) for p in range(2)]
        xn = [sb(f"xn{p}", [P, 2, NPX]) for p in range(2)]
        xg = sb("xg", [P, 2, NPX])
        sq = sb("sq", [P, 2, NPX])
        rstd = sb("rstd", [P, 2, NPX])
        raw = [sb(f"raw{p}", [P, 2, ROWS + 2, WW + 2]) for p in range(2)]
        zeros = sb("zeros", [P, WW])
        acc = sb("acc", [P, 2, ROWS, WW])
        sz = [sb(f"sz{p}", [P, 2, NPX]) for p in range(2)]
        u = [sb(f"u{p}", [P, 2, ROWS, WW]) for p in range(2)]
        xd = [sb(f"xd{p}", [NDT + NBC, NPX]) for p in range(2)]

        gate_ps = ps("gate_ps", [P, NPX])
        stat_ps = ps("stat_ps", [P, NPX])
        xz_ps = [ps(f"xz_ps{t}", [P, NPX]) for t in range(4)]
        xd_ps = ps("xd_ps", [NDT + NBC, NPX])

        w_loaded = sem("w_loaded")
        w_ready = sem("w_ready")
        in_loaded = [sem(f"in_loaded{p}") for p in range(2)]
        x4_stored = [sem(f"x4_stored{p}") for p in range(2)]
        z_stored = [sem(f"z_stored{p}") for p in range(2)]
        u_stored = [sem(f"u_stored{p}") for p in range(2)]
        gate_sum = sem("gate_sum")
        gate_ready = sem("gate_ready")
        gated = sem("gated")
        x4_ready = sem("x4_ready")
        mu_ready = sem("mu_ready")
        xc_ready = sem("xc_ready")
        sq_ready = sem("sq_ready")
        var_ready = sem("var_ready")
        ln_done = sem("ln_done")
        r_ready = sem("r_ready")
        xr_done = sem("xr_done")
        xg_ready = sem("xg_ready")
        xz_ready = sem("xz_ready")
        x_evac = sem("x_evac")
        z_ready = sem("z_ready")
        zero_row_ready = sem("zero_row_ready")
        zeros_ready = sem("zeros_ready")
        carried = sem("carried")
        raw_ready = sem("raw_ready")
        conv_seq = sem("conv_seq")
        u_ready = sem("u_ready")
        xd_ready = sem("xd_ready")
        xd_evac = sem("xd_evac")
        img_done = sem("img_done")

        IN_DMAS, U_DMAS = 5, 3
        loads = [(ln_gb, d["ln3_gb"]), (w_in, d["w_in"]), (cw, d["cw"]), (cb, d["cb"]), (w_x, d["w_x"]), (b_sa, d["b_sa"])]
        x2v, yv, x4v, zv, uv = (d[k].rearrange("b (h p) n -> b p h n", h=2) for k in ("x2", "y", "x4", "sz", "u"))

        def image_loop(eng, start, step, end):
            with eng.Fori(0, B) as b:
                start(b)
                step(b, 0, 0, 0, True)
                step(b, 1, 1, 0, False)
                with eng.Fori(0, CHUNKS // 2 - 1) as j:
                    step(b, 2 * j + 2, 0, j + 1, False)
                    step(b, 2 * j + 3, 1, j + 1, False)
                end(b)

        def convolved(b, s):
            return b * (CHUNKS + 1) + s

        def convolved_of(b, p, half):
            return b * (CHUNKS // 2 + 1 - p) + half

        block = ctx.enter_context(nc.Block())

        @block.sync
        def _(sp):
            for dst, src in loads:
                sp.dma_start(dst[:], src).then_inc(w_loaded, DMA)

            def load(b, s, p):
                if isinstance(s, int) and s < 2:
                    sp.wait_ge(x4_ready, b * CHUNKS)
                else:
                    sp.wait_ge(x4_ready, b * CHUNKS + s - 1)
                px = bass.ds(s * NPX, NPX)
                sp.dma_start(x2[p][:], x2v[b, :, :, px]).then_inc(in_loaded[p], DMA)
                sp.dma_start(y[p][:], yv[b, :, :, px]).then_inc(in_loaded[p], DMA)
                for dy in range(3):
                    view = d["planes"][b, 3 * dy * PLANE:3 * dy * PLANE + 3 * (PLANE + 1)].rearrange("(t n) -> t n", t=3)
                    rows = view[:, bass.ds((s * ROWS + dy) * (WW + 2), ROWS * (WW + 2))]
                    rows = rows.rearrange("t (r c) -> t r c", c=WW + 2)[:, :, 0:WW]
                    sp.dma_start(taps[p][3 * dy:3 * dy + 3, :].rearrange("t (r w) -> t r w", w=WW),
                                 rows).then_inc(in_loaded[p], DMA)

            def store_x4(b, s, p):
                sp.wait_ge(x4_ready, b * CHUNKS + s + 1)
                sp.dma_start(x4v[b, :, :, bass.ds(s * NPX, NPX)], x4[p][:]).then_inc(x4_stored[p], DMA)

            def store_z(b, s, p):
                sp.wait_ge(z_ready, b * CHUNKS + s + 1)
                sp.dma_start(zv[b, :, :, bass.ds(s * NPX, NPX)], sz[p][:]).then_inc(z_stored[p], DMA)

            def store_u(b, s, p, lo, hi):
                sp.wait_ge(u_ready, convolved(b, s) + 1)
                px = bass.ds(s * NPX + (lo - 1) * WW, (hi - lo) * WW)
                own = slice(lo * WW, hi * WW)
                sp.dma_start(uv[b, :, :, px], u[p][:, :, lo:hi, :].rearrange("p h r w -> p h (r w)")).then_inc(u_stored[p], DMA)
                sp.wait_ge(xd_evac, convolved(b, s) + 1)
                sp.dma_start(d["dts"][:, b, :, px], xd[p][0:NDT, own]).then_inc(u_stored[p], DMA)
                sp.dma_start(d["bc"][:, b, :, px], xd[p][NDT:NDT + NBC, own]).then_inc(u_stored[p], DMA)

            with sp.Fori(0, B) as b:
                load(b, 0, 0)
                load(b, 1, 1)
                store_x4(b, 0, 0)
                load(b, 2, 0)
                store_z(b, 0, 0)
                store_x4(b, 1, 1)
                load(b, 3, 1)
                store_z(b, 1, 1)
                store_u(b, 0, 0, 1, ROWS)
                with sp.Fori(0, CHUNKS // 2 - 2) as j:
                    store_x4(b, 2 * j + 2, 0)
                    load(b, 2 * j + 4, 0)
                    store_z(b, 2 * j + 2, 0)
                    store_u(b, 2 * j + 1, 1, 0, ROWS)
                    store_x4(b, 2 * j + 3, 1)
                    load(b, 2 * j + 5, 1)
                    store_z(b, 2 * j + 3, 1)
                    store_u(b, 2 * j + 2, 0, 0, ROWS)
                store_x4(b, CHUNKS - 2, 0)
                store_z(b, CHUNKS - 2, 0)
                store_u(b, CHUNKS - 3, 1, 0, ROWS)
                store_x4(b, CHUNKS - 1, 1)
                store_z(b, CHUNKS - 1, 1)
                store_u(b, CHUNKS - 2, 0, 0, ROWS)
                store_u(b, CHUNKS - 1, 1, 0, ROWS)
                store_u(b, CHUNKS, 0, 0, 1)
            for p in range(2):
                sp.wait_ge(x4_stored[p], DMA * B * CHUNKS // 2)
                sp.wait_ge(z_stored[p], DMA * B * CHUNKS // 2)
                sp.wait_ge(u_stored[p], DMA * U_DMAS * B * (CHUNKS // 2 + 1 - p))

        @block.gpsimd
        def _(pool):
            nc.gpsimd.memset(mean_w[:], 1.0 / C)
            nc.gpsimd.memset(ones[:], 1.0)
            nc.gpsimd.memset(consts[:, 0:1], LN_EPS)
            nc.gpsimd.memset(consts[:, 1:2], 0.0)
            nc.gpsimd.memset(zeros[:], 0.0).then_inc(zero_row_ready, 1)
            for p in range(2):
                nc.gpsimd.memset(raw[p][:, :, :, 0:1], 0.0)
                last = nc.gpsimd.memset(raw[p][:, :, :, WW + 1:WW + 2], 0.0)
            last.then_inc(w_ready, 1)
            def clear(rows):
                z = zeros[:, None, None, :].to_broadcast(rows.shape)
                nc.gpsimd.tensor_tensor(rows, z, z, ALU.add).then_inc(zeros_ready, 1)

            with pool.Fori(0, B) as b:
                pool.wait_ge(zero_row_ready, 1)
                pool.wait_ge(conv_seq, convolved(b, 0) * 18)
                clear(raw[0][:, :, 0:2, 1:WW + 1])
                pool.wait_ge(conv_seq, convolved(b, CHUNKS - 1) * 18)
                clear(raw[0][:, :, 2:3, 1:WW + 1])

        @block.vector
        def _(dve):
            dve.wait_ge(w_loaded, DMA * len(loads))
            dve.wait_ge(w_ready, 1)

            def conv(b, s, p):
                done = convolved(b, s)
                dve.wait_ge(raw_ready, done + 1)
                dve.wait_ge(u_ready, done)
                for t, (dy, dx) in enumerate(TAPS):
                    for h in range(2):
                        window = raw[p][:, h, dy:dy + ROWS, dx:dx + WW]
                        w = cw[:, h, t:t + 1]
                        if t == 0:
                            ins = nc.vector.tensor_scalar(acc[:, h], window, w, None, ALU.mult)
                        else:
                            dve.wait_ge(conv_seq, done * 18 + 2 * t + h - 1)
                            ins = nc.vector.scalar_tensor_tensor(acc[:, h], window, w, acc[:, h], ALU.mult, ALU.add)
                        ins.then_inc(conv_seq, 1)

            def start(b):
                pass

            def step(b, s, p, half, first):
                q = b * CHUNKS + s
                dve.wait_ge(gate_ready, q + 1)
                dve.wait_ge(in_loaded[p], (b * (CHUNKS // 2) + half + 1) * IN_DMAS * DMA)
                g = gate[:].unsqueeze(1).broadcast_to([P, 2, NPX])
                nc.vector.tensor_tensor(y[p][:], y[p][:], g, ALU.mult).then_inc(gated, 1)
                dve.wait_ge(x4_stored[p], (b * (CHUNKS // 2) + half) * DMA)
                dve.wait_ge(gated, q + 1)
                nc.vector.tensor_tensor(x4[p][:], x2[p][:], y[p][:], ALU.add).then_inc(x4_ready, 1)
                dve.wait_ge(mu_ready, q + 1)
                dve.wait_ge(x4_ready, q + 1)
                dve.wait_ge(xg_ready, q)
                mu = stat_ps[:].unsqueeze(1).broadcast_to([P, 2, NPX])
                nc.vector.tensor_tensor(xn[p][:], x4[p][:], mu, ALU.subtract).then_inc(xc_ready, 1)
                if not first:
                    conv(b, s - 1, 1 - p)
                dve.wait_ge(r_ready, q + 1)
                dve.wait_ge(xc_ready, q + 1)
                r = rstd[:, 1:2, :].broadcast_to([P, 2, NPX])
                nc.vector.tensor_tensor(xn[p][:], xn[p][:], r, ALU.mult).then_inc(xr_done, 1)
                dve.wait_ge(xr_done, q + 1)
                dve.wait_ge(xz_ready, q * 4)
                for h in range(2):
                    last = nc.vector.tensor_scalar(xg[:, h], xn[p][:, h], ln_gb[:, h, 0:1], ln_gb[:, h, 1:2],
                                                   ALU.mult, ALU.add)
                last.then_inc(xg_ready, 1)

            def end(b):
                conv(b, CHUNKS - 1, 1)
                conv(b, CHUNKS, 0)

            image_loop(dve, start, step, end)

        @block.scalar
        def _(act):
            act.wait_ge(w_ready, 1)
            act.wait_ge(w_loaded, DMA * len(loads))

            def carry(b, s, p):
                act.wait_ge(conv_seq, convolved(b, s - 1) * 18)
                act.wait_ge(raw_ready, convolved(b, s))
                nc.scalar.copy(raw[p][:, :, 0:2, 1:WW + 1], raw[1 - p][:, :, ROWS:ROWS + 2, 1:WW + 1]).then_inc(carried, 1)

            def silu_u(b, s, p, half):
                nc.scalar.preload_act_table_set("silu_and_others")
                act.wait_ge(conv_seq, convolved(b, s) * 18 + 18)
                act.wait_ge(u_stored[p], convolved_of(b, p, half) * U_DMAS * DMA)
                for h in range(2):
                    last = nc.scalar.activation(u[p][:, h], acc[:, h], ACT.Silu, bias=cb[:, h:h + 1])
                last.then_inc(u_ready, 1)

            def evac_xd(b, s, p, half):
                act.wait_ge(xd_ready, convolved(b, s) + 1)
                act.wait_ge(u_stored[p], convolved_of(b, p, half) * U_DMAS * DMA)
                nc.scalar.copy(xd[p][:], xd_ps[:]).then_inc(xd_evac, 1)

            def start(b):
                pass

            def step(b, s, p, half, first):
                q = b * CHUNKS + s
                nc.scalar.preload_act_table_set("sigmoid_and_others")
                act.wait_ge(gate_sum, q + 1)
                act.wait_ge(gated, q)
                nc.scalar.activation(gate[:], gate_ps[:], ACT.Sigmoid, bias=b_sa[:]).then_inc(gate_ready, 1)
                act.wait_ge(xc_ready, q + 1)
                act.wait_ge(var_ready, q)
                nc.scalar.activation(sq[:], xn[p][:], ACT.Square).then_inc(sq_ready, 1)
                if not first:
                    carry(b, s, p)
                nc.scalar.preload_act_table_set("natural_log_exp_and_others")
                if first:
                    act.wait_ge(zeros_ready, b * 2 + 1)
                act.wait_ge(var_ready, q + 1)
                act.wait_ge(xr_done, q)
                nc.scalar.activation(rstd[:, 0], stat_ps[:], ACT.Ln, bias=consts[:, 0:1]).then_inc(ln_done, 1)
                act.wait_ge(ln_done, q + 1)
                nc.scalar.activation(rstd[:, 1], rstd[:, 0], ACT.Exp, scale=-0.5, bias=consts[:, 1:2]).then_inc(r_ready, 1)
                if not first:
                    silu_u(b, s - 1, 1 - p, half - 1 + p)
                if first:
                    nc.scalar.preload_act_table_set("silu_and_others")
                act.wait_ge(z_stored[p], (b * (CHUNKS // 2) + half) * DMA)
                for t in range(2):
                    act.wait_ge(xz_ready, q * 4 + t + 1)
                    nc.scalar.copy(raw[p][:, t, 2:ROWS + 2, 1:WW + 1],
                                   xz_ps[t][:].rearrange("p (r w) -> p r w", w=WW)).then_inc(x_evac, 1)
                act.wait_ge(x_evac, q * 2 + 2)
                act.sem_inc(raw_ready, 1)
                for t in range(2):
                    act.wait_ge(xz_ready, q * 4 + t + 3)
                    last = nc.scalar.activation(sz[p][:, t], xz_ps[2 + t][:], ACT.Silu, bias=consts[:, 1:2])
                last.then_inc(z_ready, 1)
                if not first:
                    evac_xd(b, s - 1, 1 - p, half - 1 + p)

            def end(b):
                carry(b, CHUNKS, 0)
                act.wait_ge(zeros_ready, b * 2 + 2)
                act.wait_ge(carried, (b + 1) * CHUNKS)
                act.sem_inc(raw_ready, 1)
                silu_u(b, CHUNKS - 1, 1, CHUNKS // 2 - 1)
                evac_xd(b, CHUNKS - 1, 1, CHUNKS // 2 - 1)
                silu_u(b, CHUNKS, 0, CHUNKS // 2)
                evac_xd(b, CHUNKS, 0, CHUNKS // 2)

            image_loop(act, start, step, end)

        @block.tensor
        def _(pe):
            pe.wait_ge(w_ready, 1)
            pe.wait_ge(w_loaded, DMA * len(loads))

            def x_proj(b, s, p):
                c = convolved(b, s)
                pe.wait_ge(u_ready, c + 1)
                pe.wait_ge(xd_evac, c)
                for h in range(2):
                    last = nc.tensor.matmul(xd_ps[:], w_x[:, h], u[p][:, h].rearrange("p r w -> p (r w)"),
                                            start=(h == 0), stop=(h == 1))
                last.then_inc(xd_ready, 1)

            def start(b):
                pass

            def step(b, s, p, half, first):
                q = b * CHUNKS + s
                pe.wait_ge(in_loaded[p], (b * (CHUNKS // 2) + half + 1) * IN_DMAS * DMA)
                pe.wait_ge(gate_ready, q)
                nc.tensor.matmul(gate_ps[:], ones[:], taps[p][:], start=True, stop=True).then_inc(gate_sum, 1)
                pe.wait_ge(x4_ready, q + 1)
                pe.wait_ge(r_ready, q)
                for h in range(2):
                    last = nc.tensor.matmul(stat_ps[:], mean_w[:], x4[p][:, h], start=(h == 0), stop=(h == 1))
                last.then_inc(mu_ready, 1)
                pe.wait_ge(sq_ready, q + 1)
                for h in range(2):
                    last = nc.tensor.matmul(stat_ps[:], mean_w[:], sq[:, h], start=(h == 0), stop=(h == 1))
                last.then_inc(var_ready, 1)
                if not first:
                    x_proj(b, s - 1, 1 - p)
                pe.wait_ge(xg_ready, q + 1)
                pe.wait_ge(z_ready, q)
                for t in range(4):
                    for h in range(2):
                        last = nc.tensor.matmul(xz_ps[t][:], w_in[:, h, P * t:P * t + P], xg[:, h],
                                                start=(h == 0), stop=(h == 1))
                    last.then_inc(xz_ready, 1)

            def end(b):
                x_proj(b, CHUNKS - 1, 1)
                x_proj(b, CHUNKS, 0)

            image_loop(pe, start, step, end)


SPLIT = 1024
PAIRS = B // 2


def split_and_turn(nc, d):
    with ExitStack() as ctx:
        def sb(name, shape, dt=FP32):
            return ctx.enter_context(nc.sbuf_tensor("t_" + name, shape, dt))

        sems = []
        ctx.callback(nc.all_engine_barrier)
        ctx.callback(nc.clear_and_free_semaphores, sems)

        def sem(name):
            sems.append(nc.alloc_semaphore("t_" + name))
            return sems[-1]

        rows = sb("rows", [128, L])
        dts = sb("dts", [2 * B * RANK, L])
        flat = [sb(f"flat{p}", [128, SPLIT]) for p in range(2)]
        rest = [sb(f"rest{p}", [128, SPLIT]) for p in range(2)]
        parts = [sb(f"parts{p}", [128, 3, SPLIT], BF16) for p in range(2)]
        dtt = [sb(f"dtt{p}", [2 * B * RANK, SPLIT]) for p in range(2)]

        loaded = sem("loaded")
        dt_loaded = sem("dt_loaded")
        by_row = [sem(f"by_row{p}") for p in range(2)]
        by_col = [sem(f"by_col{p}") for p in range(2)]
        high = [sem(f"high{p}") for p in range(2)]
        rested = [sem(f"rested{p}") for p in range(2)]
        middle = [sem(f"middle{p}") for p in range(2)]
        low = [sem(f"low{p}") for p in range(2)]
        turned = [sem(f"turned{p}") for p in range(2)]
        stored = [sem(f"stored{p}") for p in range(2)]
        dt_stored = [sem(f"dt_stored{p}") for p in range(2)]
        STORES = 12
        COLS = SPLIT // HH
        by_order = d["bc"].rearrange("(e g) b r n -> g e (b r) n", g=2)
        dt_order = d["dts"].rearrange("(e g) b r n -> g e (b r) n", g=2)[1]
        turn = lambda x: x.rearrange("p (h w) -> p w h", w=WW)

        block = ctx.enter_context(nc.Block())

        def steps(eng, step):
            with eng.Fori(0, L // SPLIT // 2) as j:
                step(2 * j, 0, j)
                step(2 * j + 1, 1, j)

        @block.sync
        def _(sp):
            for g in range(2):
                for e in range(2):
                    at = 64 * g + 32 * e
                    sp.dma_start(rows[at:at + 32, :], by_order[g, e]).then_inc(loaded, DMA)
            for e in range(2):
                at = B * RANK * e
                sp.dma_start(dts[at:at + B * RANK, :], dt_order[e]).then_inc(dt_loaded, DMA)

            def step(n, p, j):
                px = bass.ds(n * SPLIT, SPLIT)
                sp.wait_ge(low[p], j + 1)
                sp.wait_ge(middle[p], j + 1)
                sp.wait_ge(high[p], j + 1)
                for g in range(2):
                    for e in range(2):
                        at = 64 * g + 32 * e
                        for k in range(3):
                            dst = d["bcs"][2 * e + g].rearrange("q (k r) n -> k q r n", k=3)[k]
                            sp.dma_start(dst[:, :, px], parts[p][at:at + 32, k, :]).then_inc(stored[p], DMA)
                sp.wait_ge(turned[p], j + 1)
                for e in range(2):
                    at = B * RANK * e
                    sp.dma_start(dt_order[e][:, px], dtt[p][at:at + B * RANK, :]).then_inc(dt_stored[p], DMA)

            steps(sp, step)
            for p in range(2):
                sp.wait_ge(stored[p], L // SPLIT // 2 * STORES * DMA)
                sp.wait_ge(dt_stored[p], L // SPLIT // 2 * 2 * DMA)

        @block.gpsimd
        def _(pool):
            pool.wait_ge(dt_loaded, 2 * DMA)

            def step(n, p, j):
                pool.wait_ge(dt_stored[p], j * 2 * DMA)
                out = dtt[p][:].rearrange("p (w h) -> p w h", h=HH)
                nc.gpsimd.tensor_copy(out, turn(dts[:])[:, bass.ds(n * COLS, COLS), :]).then_inc(turned[p], 1)

            steps(pool, step)

        @block.scalar
        def _(act):
            act.wait_ge(loaded, 4 * DMA)

            def step(n, p, j):
                act.wait_ge(rested[p], j)
                nc.scalar.copy(flat[p][0:64, :], rows[0:64, bass.ds(n * SPLIT, SPLIT)]).then_inc(by_row[p], 1)
                act.wait_ge(rested[p], j + 1)
                act.wait_ge(stored[p], j * STORES * DMA)
                nc.scalar.copy(parts[p][:, 1, :], rest[p][:]).then_inc(middle[p], 1)

            steps(act, step)

        @block.vector
        def _(dve):
            dve.wait_ge(loaded, 4 * DMA)

            def step(n, p, j):
                dve.wait_ge(rested[p], j)
                nc.vector.tensor_copy(flat[p][64:128, :].rearrange("p (w h) -> p w h", h=HH),
                                      turn(rows[64:128, :])[:, bass.ds(n * COLS, COLS), :]).then_inc(by_col[p], 1)
                dve.wait_ge(by_row[p], j + 1)
                dve.wait_ge(by_col[p], j + 1)
                dve.wait_ge(stored[p], j * STORES * DMA)
                nc.vector.tensor_copy(parts[p][:, 0, :], flat[p][:]).then_inc(high[p], 1)
                dve.wait_ge(high[p], j + 1)
                dve.wait_ge(low[p], j)
                dve.wait_ge(middle[p], j)
                nc.vector.tensor_tensor(rest[p][:], flat[p][:], parts[p][:, 0, :], ALU.subtract).then_inc(rested[p], 1)
                dve.wait_ge(middle[p], j + 1)
                dve.wait_ge(rested[p], j + 1)
                nc.vector.tensor_tensor(parts[p][:, 2, :], rest[p][:], parts[p][:, 1, :], ALU.subtract).then_inc(low[p], 1)

            steps(dve, step)


UNIT = 512
UNITS = L // UNIT
GROUPS = UNITS // 4
TILES = B * C // 128
ORDER = [(0, False, False), (1, True, False), (3, True, True), (2, False, True)]
EXP_CAP = 2.0 ** 63
LOG_MAX = 88.72283
TINY = 2.0 ** -22
RATE_MAX = 2.0 ** 120
DT_MIN = 2.0 ** -113


def selective_scans(nc, d):
    with ExitStack() as ctx:
        def sb(name, shape, dt=FP32):
            return ctx.enter_context(nc.sbuf_tensor("d_" + name, shape, dt))

        def ps(name, shape):
            return ctx.enter_context(nc.psum_tensor("d_" + name, shape, FP32))

        sems = []
        ctx.callback(nc.all_engine_barrier)
        ctx.callback(nc.clear_and_free_semaphores, sems)

        def sem(name):
            sems.append(nc.alloc_semaphore("d_" + name))
            return sems[-1]

        def two(name):
            return [sem(f"{name}{p}") for p in range(2)]

        u = sb("u", [128, L])
        y = sb("y", [128, L])
        ident = sb("ident", [128, 128])
        sel = sb("sel", [6 * 2 * STATES, 2 * STATES, 128], BF16)
        w_dt = sb("w_dt", [2 * RANK, DIRS, 128])
        dt_bias = sb("dt_bias", [128, DIRS])
        a_log = sb("a_log", [128, DIRS * STATES])
        a = sb("a", [128, DIRS * STATES])
        skip = sb("skip", [128, DIRS])
        skip_sum = sb("skip_sum", [128, 1])
        zero = sb("zero", [128, 2])
        dts = [sb(f"dts{h}", [2 * RANK, 2 * UNIT]) for h in range(2)]
        bcs = [sb(f"bcs{h}", [6 * 2 * STATES, 2 * UNIT], BF16) for h in range(2)]
        ex = [sb(f"ex{p}", [128, UNIT]) for p in range(2)]
        dt = [sb(f"dt{p}", [128, UNIT]) for p in range(2)]
        du = [sb(f"du{p}", [128, UNIT]) for p in range(2)]
        da = [sb(f"da{p}", [128, STATES, UNIT]) for p in range(2)]
        h = [sb(f"h{p}", [128, STATES, UNIT]) for p in range(2)]
        cs = sb("cs", [128, STATES, UNIT])
        hc = sb("hc", [128, STATES, UNIT])
        sel32 = hc[0:6 * 2 * STATES, 0:2].rearrange("p a (b c) -> p (a b) c", c=128)

        raw_ps = ps("raw_ps", [128, UNIT])
        b_ps = [ps(f"b_ps{n}", [128, UNIT]) for n in range(STATES)]
        c_ps = [ps(f"c_ps{p}", [128, UNIT]) for p in range(2)]
        y_ps = ps("y_ps", [128, UNIT])

        const_ready = sem("const_ready")
        ident_loaded = sem("ident_loaded")
        w_loaded = sem("w_loaded")
        u_begun = sem("u_begun")
        u_loaded = sem("u_loaded")
        a_capped = sem("a_capped")
        sel_ready = sem("sel_ready")
        a_exp = sem("a_exp")
        a_ready = sem("a_ready")
        y_stored = sem("y_stored")
        xd_loaded = two("xd_loaded")
        raw_ready = two("raw_ready")
        e_ready = two("e_ready")
        clipped = two("clipped")
        ln_ready = two("ln_ready")
        dt_max = two("dt_max")
        dt_ready = two("dt_ready")
        du_ready = two("du_ready")
        da_ready = two("da_ready")
        b_ready = two("b_ready")
        dbu_ready = two("dbu_ready")
        scanned = two("scanned")
        c_ready = two("c_ready")
        cs_ready = two("cs_ready")
        hc_ready = two("hc_ready")
        y_summed = two("y_summed")
        y_added = two("y_added")

        W_DMAS, HALF, U_CUT = 5, UNITS // 2, L // 4
        uv = d["u"].rearrange("b c n -> (b c) n")
        yv = d["ys"].rearrange("b c n -> (b c) n")

        class Unit:

            def __init__(self, t, o, j, i):
                self.t, self.o, self.j, self.i, self.p = t, o, j, i, i % 2
                self.first = isinstance(j, int) and j == 0 and i == 0
                self.direction, self.columns, self.reverse = ORDER[o]
                self.n = (t * len(ORDER) + o) * HALF + j * 2 + i // 2
                self.k = j * -4 + (UNITS - 1 - i) if self.reverse else j * 4 + i
                self.groups = (t * len(ORDER) + o) * GROUPS + j
                self.very_first = self.first and o == 0

            def loaded(self, x):
                at = (1 - self.p if self.reverse else self.p) * UNIT
                return x[self.i // 2][:, at:at + UNIT]

            def states(self, k):
                return self.n * STATES + k

            def before(self, k):
                if self.very_first:
                    return self.n * STATES
                return self.n * STATES + (k if self.p else k - STATES)

            def where(self, x):
                if self.columns:
                    return x[:].rearrange("p (h w) -> p w h", w=WW)[:, bass.ds(self.k * (UNIT // HH), UNIT // HH), :]
                return x[:, bass.ds(self.k * UNIT, UNIT)]

            def shaped(self, x):
                return x.rearrange("p (w h) -> p w h", h=HH) if self.columns else x

            def run(self, x):
                return x[:, ::-1] if self.reverse else x

        def units(eng, body, start, end):
            with eng.Fori(0, PAIRS) as pair:
                with eng.Fori(0, TILES // PAIRS) as third:
                    t = pair * (TILES // PAIRS) + third
                    start(t, pair, third)
                    last = None
                    for o in range(len(ORDER)):
                        def group(j, before, after):
                            own = [before, *(Unit(t, o, j, i) for i in range(4)), after]
                            for i in range(4):
                                body(*own[i:i + 3])
                            return own[4]

                        group(0, last, Unit(t, o, 1, 0))
                        with eng.Fori(1, GROUPS - 1) as j:
                            group(j, Unit(t, o, j - 1, 3), Unit(t, o, j + 1, 0))
                        last = group(GROUPS - 1, Unit(t, o, GROUPS - 2, 3),
                                     Unit(t, o + 1, 0, 0) if o + 1 < len(ORDER) else None)
                    end(t, last)

        block = ctx.enter_context(nc.Block())

        @block.sync
        def _(sp):
            sp.dma_start(ident[:], d["ident"]).then_inc(ident_loaded, DMA)

            with sp.Fori(0, PAIRS) as pair:
                with sp.Fori(0, TILES // PAIRS) as third:
                    t = pair * (TILES // PAIRS) + third
                    sp.wait_ge(y_added[1], t * len(ORDER) * HALF)
                    sp.wait_ge(y_added[0], t * len(ORDER) * HALF)
                    sp.dma_start(w_dt[:], d["w_dt"][third]).then_inc(w_loaded, DMA)
                    sp.dma_start(dt_bias[:], d["dt_bias"][third]).then_inc(w_loaded, DMA)
                    sp.dma_start(a_log[:], d["a_log"][third]).then_inc(w_loaded, DMA)
                    sp.dma_start(skip[:], d["skip"][third]).then_inc(w_loaded, DMA)
                    sp.dma_start(sel32, d["sel"][third]).then_inc(w_loaded, DMA)
                    sp.dma_start(u[:, 0:U_CUT], uv[bass.ds(t * 128, 128), 0:U_CUT]).then_inc(u_begun, DMA)

                    def store(x):
                        px = bass.ds(x.k * UNIT, UNIT)
                        sp.wait_ge(y_added[x.p], x.n + 1)
                        sp.dma_start(yv[bass.ds(t * 128, 128), px], y[:, px]).then_inc(y_stored, DMA)

                    def load(o, j, half):
                        x = Unit(t, o, j, 2 * half + 1)
                        k = x.k if x.reverse else j * 4 + 2 * half
                        px = bass.ds(k * UNIT, 2 * UNIT)
                        if not (o == 0 and isinstance(j, int) and j == 0):
                            sp.wait_ge(c_ready[1], x.states(0) - STATES)
                        src = d["dts"][x.direction, bass.ds(pair * 2, 2), :, px]
                        sp.dma_start(dts[half][:], src.rearrange("i r n -> (i r) n")).then_inc(xd_loaded[half], DMA)
                        sp.dma_start(bcs[half][:], d["bcs"][x.direction, pair, :, px]).then_inc(xd_loaded[half], DMA)

                    for o in range(len(ORDER)):
                        stores = o == len(ORDER) - 1
                        for half in range(2):
                            load(o, 0, half)
                        if o == 0:
                            for at in range(U_CUT, L, U_CUT):
                                sp.dma_start(u[:, at:at + U_CUT],
                                             uv[bass.ds(t * 128, 128), at:at + U_CUT]).then_inc(u_loaded, DMA)
                        with sp.Fori(1, GROUPS) as j:
                            for half in range(2):
                                load(o, j, half)
                                if stores:
                                    store(Unit(t, o, j - 1, 2 * half))
                                    store(Unit(t, o, j - 1, 2 * half + 1))
                        if stores:
                            for i in range(4):
                                store(Unit(t, o, GROUPS - 1, i))
            sp.wait_ge(y_stored, TILES * UNITS * DMA)

        @block.gpsimd
        def _(pool):
            nc.gpsimd.memset(zero[:, 0:1], 0.0)
            nc.gpsimd.memset(zero[:, 1:2], 1.0).then_inc(const_ready, 1)

            def start(t, pair, third):
                pool.wait_ge(u_begun, (t + 1) * DMA)
                times_u(Unit(t, 0, 0, 0))

            def times_u(x):
                pool.wait_ge(dt_ready[x.p], x.n + 1)
                pool.wait_ge(dbu_ready[x.p], x.states(0))
                nc.gpsimd.tensor_tensor(x.shaped(du[x.p][:]), x.shaped(dt[x.p][:]), x.where(u),
                                        ALU.mult).then_inc(du_ready[x.p], 1)

            def times_c(x, n):
                pool.wait_ge(scanned[x.p], x.states(n + 1))
                pool.wait_ge(cs_ready[x.p], x.states(n + 1))
                pool.wait_ge(y_summed[1 - x.p], x.before(n + 1))
                nc.gpsimd.tensor_tensor(hc[:, n], h[x.p][:, n], cs[:, n], ALU.mult).then_inc(hc_ready[x.p], 1)

            def body(before, x, after):
                times_c(x, 0)
                times_c(x, 1)
                if x.o == 0 and x.i == 3 and isinstance(x.j, int) and x.j == 0:
                    pool.wait_ge(u_loaded, (x.t + 1) * 3 * DMA)
                if after:
                    times_u(after)
                times_c(x, 2)
                times_c(x, 3)

            units(pool, body, start, lambda t, last: None)

        @block.vector
        def _(dve):
            dve.wait_ge(const_ready, 1)

            def clip(x):
                dve.wait_ge(e_ready[x.p], x.n + 1)
                nc.vector.tensor_scalar(ex[x.p][:], ex[x.p][:], EXP_CAP, DT_MIN, ALU.min, ALU.max).then_inc(clipped[x.p], 1)

            def softplus(x):
                dve.wait_ge(ln_ready[x.p], x.n + 1)
                o = x.direction
                nc.vector.scalar_tensor_tensor(dt[x.p][:], raw_ps[:], dt_bias[:, o:o + 1], dt[x.p][:],
                                               ALU.add, ALU.max).then_inc(dt_max[x.p], 1)

            def softplus_tiny(x):
                dve.wait_ge(dt_max[x.p], x.n + 1)
                nc.vector.scalar_tensor_tensor(dt[x.p][:], dt[x.p][:], TINY, ex[x.p][:],
                                               ALU.max, ALU.min).then_inc(dt_ready[x.p], 1)

            def times_b(x, n):
                dve.wait_ge(b_ready[x.p], x.states(n + 1))
                dve.wait_ge(du_ready[x.p], x.n + 1)
                nc.vector.tensor_tensor(b_ps[n][:], b_ps[n][:], du[x.p][:], ALU.mult).then_inc(dbu_ready[x.p], 1)

            def scan(x, n):
                dve.wait_ge(dbu_ready[x.p], x.states(n + 1))
                dve.wait_ge(da_ready[x.p], x.states(n + 1))
                dve.wait_ge(hc_ready[x.p], x.states(0))
                initial = 0.0
                if not x.first:
                    dve.wait_ge(scanned[1 - x.p], x.before(n + 1))
                    end = 0 if x.reverse else UNIT - 1
                    initial = h[1 - x.p][:, n, end:end + 1]
                nc.vector.tensor_tensor_scan(x.run(h[x.p][:, n]), x.run(da[x.p][:, n]), x.run(b_ps[n][:]), initial,
                                             ALU.mult, ALU.add).then_inc(scanned[x.p], 1)

            def add_y(x):
                dve.wait_ge(y_summed[x.p], x.states(STATES))
                at, new = x.where(y), x.shaped(y_ps[:])
                if x.first and x.o:
                    dve.wait_ge(y_added[1], x.n)
                    dve.wait_ge(y_added[0], x.n)
                if x.o == 0:
                    ins = nc.vector.scalar_tensor_tensor(at, x.where(u), skip_sum[:], new, ALU.mult, ALU.add)
                else:
                    ins = nc.vector.tensor_tensor(at, at, new, ALU.add)
                ins.then_inc(y_added[x.p], 1)

            def start(t, pair, third):
                dve.wait_ge(w_loaded, (t + 1) * W_DMAS * DMA)
                dve.wait_ge(u_begun, (t + 1) * DMA)
                dve.wait_ge(y_stored, t * UNITS * DMA)
                nc.vector.tensor_scalar(a_log[:], a_log[:], LOG_MAX, None, ALU.min).then_inc(a_capped, 1)
                nc.vector.tensor_copy(sel[:], sel32).then_inc(sel_ready, 1)
                nc.vector.reduce_sum(skip_sum[:], skip[:], axis=AXX)
                dve.wait_ge(a_exp, t + 1)
                nc.vector.tensor_scalar(a[:], a[:], RATE_MAX, -1.0, ALU.min, ALU.mult).then_inc(a_ready, 1)
                dve.wait_ge(a_ready, t + 1)
                x = Unit(t, 0, 0, 0)
                clip(x)
                softplus(x)
                softplus_tiny(x)

            def body(before, x, after):
                if x.o == 0 and x.i == 3 and isinstance(x.j, int) and x.j == 0:
                    dve.wait_ge(u_loaded, (x.t + 1) * 3 * DMA)
                times_b(x, 0)
                times_b(x, 1)
                scan(x, 0)
                if after:
                    clip(after)
                scan(x, 1)
                times_b(x, 2)
                times_b(x, 3)
                if after:
                    softplus(after)
                if before:
                    add_y(before)
                if after:
                    softplus_tiny(after)
                scan(x, 2)
                scan(x, 3)

            units(dve, body, start, lambda t, last: add_y(last))

        @block.scalar
        def _(act):
            act.wait_ge(const_ready, 1)
            nc.scalar.preload_act_table_set("natural_log_exp_and_others")

            def e_of(x):
                act.wait_ge(raw_ready[x.p], x.n + 1)
                act.wait_ge(dt_ready[x.p], x.n)
                o = x.direction
                nc.scalar.activation(ex[x.p][:], raw_ps[:], ACT.Exp, bias=dt_bias[:, o:o + 1]).then_inc(e_ready[x.p], 1)

            def ln_of(x):
                act.wait_ge(clipped[x.p], x.n + 1)
                act.wait_ge(du_ready[x.p], x.n)
                act.wait_ge(da_ready[x.p], x.states(0))
                nc.scalar.activation(dt[x.p][:], ex[x.p][:], ACT.Ln, bias=zero[:, 1:2]).then_inc(ln_ready[x.p], 1)

            def decay(x, n):
                act.wait_ge(dt_ready[x.p], x.n + 1)
                act.wait_ge(scanned[x.p], x.states(0))
                o = x.direction * STATES + n
                nc.scalar.activation(da[x.p][:, n], dt[x.p][:], ACT.Exp, scale=a[:, o:o + 1],
                                     bias=zero[:, 0:1]).then_inc(da_ready[x.p], 1)

            def copy_c(x, n):
                act.wait_ge(c_ready[x.p], x.states(n + 1))
                act.wait_ge(hc_ready[1 - x.p], x.before(n + 1))
                nc.scalar.copy(cs[:, n], c_ps[n % 2][:]).then_inc(cs_ready[x.p], 1)

            def start(t, pair, third):
                act.wait_ge(w_loaded, (t + 1) * W_DMAS * DMA)
                act.wait_ge(a_capped, t + 1)
                nc.scalar.activation(a[:], a_log[:], ACT.Exp, bias=zero[:, 0:1]).then_inc(a_exp, 1)
                act.wait_ge(a_ready, t + 1)
                x = Unit(t, 0, 0, 0)
                e_of(x)
                ln_of(x)

            def body(before, x, after):
                decay(x, 0)
                decay(x, 1)
                if after:
                    e_of(after)
                copy_c(x, 0)
                if after:
                    ln_of(after)
                copy_c(x, 1)
                decay(x, 2)
                decay(x, 3)
                copy_c(x, 2)
                copy_c(x, 3)

            units(act, body, start, lambda t, last: None)

        @block.tensor
        def _(pe):
            pe.wait_ge(ident_loaded, DMA)

            def raw_dt(x):
                pe.wait_ge(xd_loaded[x.i // 2], (x.groups + 1) * 2 * DMA)
                pe.wait_ge(dt_max[1 - x.p], x.n if x.p == 0 else x.n + 1)
                nc.tensor.matmul(raw_ps[:], w_dt[:, x.direction], x.loaded(dts), start=True,
                                 stop=True).then_inc(raw_ready[x.p], 1)

            def spread_b(x, n):
                pe.wait_ge(scanned[1 - x.p], x.before(n + 1))
                nc.tensor.matmul(b_ps[n][:], sel[:, n], x.loaded(bcs), start=True, stop=True).then_inc(b_ready[x.p], 1)

            def spread_c(x, n):
                if n < 2:
                    pe.wait_ge(cs_ready[1 - x.p], x.before(n + 3))
                else:
                    pe.wait_ge(cs_ready[x.p], x.states(n - 1))
                nc.tensor.matmul(c_ps[n % 2][:], sel[:, STATES + n], x.loaded(bcs), start=True,
                                 stop=True).then_inc(c_ready[x.p], 1)

            def sum_y(x, n):
                if n == 0:
                    pe.wait_ge(y_added[1 - x.p], x.n if x.p == 0 else x.n + 1)
                pe.wait_ge(hc_ready[x.p], x.states(n + 1))
                nc.tensor.matmul(y_ps[:], ident[:], hc[:, n], start=(n == 0),
                                 stop=(n == STATES - 1)).then_inc(y_summed[x.p], 1)

            def start(t, pair, third):
                pe.wait_ge(w_loaded, (t + 1) * W_DMAS * DMA)
                pe.wait_ge(sel_ready, t + 1)
                x = Unit(t, 0, 0, 0)
                raw_dt(x)
                spread_b(x, 0)
                spread_b(x, 1)

            def body(before, x, after):
                if after:
                    raw_dt(after)
                spread_b(x, 2)
                spread_b(x, 3)
                spread_c(x, 0)
                spread_c(x, 1)
                if before:
                    sum_y(before, 2)
                    sum_y(before, 3)
                spread_c(x, 2)
                spread_c(x, 3)
                if after:
                    spread_b(after, 0)
                    spread_b(after, 1)
                sum_y(x, 0)
                sum_y(x, 1)

            def end(t, last):
                sum_y(last, 2)
                sum_y(last, 3)

            units(pe, body, start, end)


def output_projection(nc, d):
    with ExitStack() as ctx:
        def sb(name, shape, dt=FP32):
            return ctx.enter_context(nc.sbuf_tensor("e_" + name, shape, dt))

        def ps(name, shape):
            return ctx.enter_context(nc.psum_tensor("e_" + name, shape, FP32))

        sems = []
        ctx.callback(nc.all_engine_barrier)
        ctx.callback(nc.clear_and_free_semaphores, sems)

        def sem(name):
            sems.append(nc.alloc_semaphore("e_" + name))
            return sems[-1]

        mean_w = sb("mean_w", [P, P])
        ln_gb = sb("ln_gb", [P, 2, 2])
        w_out = sb("w_out", [P, 2, C])
        consts = sb("consts", [P, 2])
        y = [sb(f"y{p}", [P, 2, NPX]) for p in range(2)]
        sz = [sb(f"sz{p}", [P, 2, NPX]) for p in range(2)]
        x4 = [sb(f"x4{p}", [P, 2, NPX]) for p in range(2)]
        yn = [sb(f"yn{p}", [P, 2, NPX]) for p in range(2)]
        yz = [sb(f"yz{p}", [P, 2, NPX]) for p in range(2)]
        out = [sb(f"out{p}", [P, 2, NPX]) for p in range(2)]
        sq = sb("sq", [P, 2, NPX])
        rstd = sb("rstd", [P, 2, NPX])
        stat_ps = [ps(f"stat_ps{i}", [P, NPX]) for i in range(2)]
        o_ps = [ps(f"o_ps{p}", [P, 2, NPX]) for p in range(2)]

        w_loaded = sem("w_loaded")
        w_ready = sem("w_ready")
        y_loaded = [sem(f"y_loaded{p}") for p in range(2)]
        zx_loaded = [sem(f"zx_loaded{p}") for p in range(2)]
        stored = [sem(f"stored{p}") for p in range(2)]
        mu_ready = sem("mu_ready")
        yc_ready = sem("yc_ready")
        sq_ready = sem("sq_ready")
        var_ready = sem("var_ready")
        ln_done = sem("ln_done")
        r_ready = sem("r_ready")
        yr_done = sem("yr_done")
        yg_done = sem("yg_done")
        yz_ready = sem("yz_ready")
        o_ready = sem("o_ready")
        out_ready = sem("out_ready")

        HALF = B * CHUNKS // 2
        loads = [(ln_gb, d["ln4_gb"]), (w_out, d["w_out"])]
        yv, zv, x4v, ov = (d[k].rearrange("b (h p) n -> b p h n", h=2) for k in ("ys", "sz", "x4", "out"))

        block = ctx.enter_context(nc.Block())

        def chunk_loop(eng, step, end):
            step(0, 0, 0, True)
            step(1, 1, 0, False)
            with eng.Fori(1, HALF) as j:
                step(2 * j, 0, j, False)
                step(2 * j + 1, 1, j, False)
            end()

        @block.sync
        def _(sp):
            for dst, src in loads:
                sp.dma_start(dst[:], src).then_inc(w_loaded, DMA)

            def load(b, s, p):
                px = bass.ds(s * NPX, NPX)
                sp.dma_start(y[p][:], yv[b, :, :, px]).then_inc(y_loaded[p], DMA)
                sp.dma_start(sz[p][:], zv[b, :, :, px]).then_inc(zx_loaded[p], DMA)
                sp.dma_start(x4[p][:], x4v[b, :, :, px]).then_inc(zx_loaded[p], DMA)

            def store(b, s, p):
                sp.wait_ge(out_ready, b * CHUNKS + s + 1)
                sp.dma_start(ov[b, :, :, bass.ds(s * NPX, NPX)], out[p][:]).then_inc(stored[p], DMA)

            def image(b):
                with sp.Fori(0, CHUNKS // 2 - 1) as j:
                    for p in range(2):
                        store(b, 2 * j + p, p)
                        load(b, 2 * j + 2 + p, p)

            for p in range(2):
                load(0, p, p)
            with sp.Fori(0, B - 1) as b:
                image(b)
                for p in range(2):
                    store(b, CHUNKS - 2 + p, p)
                    load(b + 1, p, p)
            image(B - 1)
            for p in range(2):
                store(B - 1, CHUNKS - 2 + p, p)
            for p in range(2):
                sp.wait_ge(stored[p], HALF * DMA)

        @block.gpsimd
        def _(pool):
            nc.gpsimd.memset(mean_w[:], 1.0 / C)
            nc.gpsimd.memset(consts[:, 0:1], LN_EPS)
            nc.gpsimd.memset(consts[:, 1:2], 0.0).then_inc(w_ready, 1)

        @block.vector
        def _(dve):
            dve.wait_ge(w_loaded, DMA * len(loads))

            def add_x4(q, p, half):
                dve.wait_ge(o_ready, q + 1)
                dve.wait_ge(stored[p], half * DMA)
                nc.vector.tensor_tensor(out[p][:], x4[p][:], o_ps[p][:], ALU.add).then_inc(out_ready, 1)

            def step(q, p, half, first):
                dve.wait_ge(mu_ready, q + 1)
                mu = stat_ps[0][:].unsqueeze(1).broadcast_to([P, 2, NPX])
                nc.vector.tensor_tensor(yn[p][:], y[p][:], mu, ALU.subtract).then_inc(yc_ready, 1)
                if not first:
                    add_x4(q - 1, 1 - p, half - 1 + p)
                dve.wait_ge(r_ready, q + 1)
                dve.wait_ge(yc_ready, q + 1)
                r = rstd[:, 1:2, :].broadcast_to([P, 2, NPX])
                nc.vector.tensor_tensor(yn[p][:], yn[p][:], r, ALU.mult).then_inc(yr_done, 1)
                dve.wait_ge(yr_done, q + 1)
                for h in range(2):
                    last = nc.vector.tensor_scalar(yn[p][:, h], yn[p][:, h], ln_gb[:, h, 0:1], ln_gb[:, h, 1:2],
                                                   ALU.mult, ALU.add)
                last.then_inc(yg_done, 1)
                dve.wait_ge(zx_loaded[p], (half + 1) * 2 * DMA)
                dve.wait_ge(yg_done, q + 1)
                nc.vector.tensor_tensor(yz[p][:], yn[p][:], sz[p][:], ALU.mult).then_inc(yz_ready, 1)

            chunk_loop(dve, step, lambda: add_x4(2 * HALF - 1, 1, HALF - 1))

        @block.scalar
        def _(act):
            act.wait_ge(w_ready, 1)
            nc.scalar.preload_act_table_set("natural_log_exp_and_others")

            def step(q, p, half, first):
                act.wait_ge(yc_ready, q + 1)
                act.wait_ge(var_ready, q)
                nc.scalar.activation(sq[:], yn[p][:], ACT.Square).then_inc(sq_ready, 1)
                act.wait_ge(var_ready, q + 1)
                act.wait_ge(yr_done, q)
                nc.scalar.activation(rstd[:, 0], stat_ps[1][:], ACT.Ln, bias=consts[:, 0:1]).then_inc(ln_done, 1)
                act.wait_ge(ln_done, q + 1)
                nc.scalar.activation(rstd[:, 1], rstd[:, 0], ACT.Exp, scale=-0.5, bias=consts[:, 1:2]).then_inc(r_ready, 1)

            chunk_loop(act, step, lambda: None)

        @block.tensor
        def _(pe):
            pe.wait_ge(w_ready, 1)
            pe.wait_ge(w_loaded, DMA * len(loads))

            def project(q, p, o, half):
                pe.wait_ge(yz_ready, q + 1)
                if o == 0:
                    pe.wait_ge(stored[p], half * DMA)
                for h in range(2):
                    last = nc.tensor.matmul(o_ps[p][:, o], w_out[:, h, P * o:P * o + P], yz[p][:, h],
                                            start=(h == 0), stop=(h == 1))
                if o == 1:
                    last.then_inc(o_ready, 1)

            def step(q, p, half, first):
                pe.wait_ge(y_loaded[p], (half + 1) * DMA)
                pe.wait_ge(yc_ready, q)
                for h in range(2):
                    last = nc.tensor.matmul(stat_ps[0][:], mean_w[:], y[p][:, h], start=(h == 0), stop=(h == 1))
                last.then_inc(mu_ready, 1)
                if not first:
                    project(q - 1, 1 - p, 0, half - 1 + p)
                pe.wait_ge(sq_ready, q + 1)
                pe.wait_ge(r_ready, q)
                for h in range(2):
                    last = nc.tensor.matmul(stat_ps[1][:], mean_w[:], sq[:, h], start=(h == 0), stop=(h == 1))
                last.then_inc(var_ready, 1)
                if not first:
                    project(q - 1, 1 - p, 1, half - 1 + p)

            def end():
                project(2 * HALF - 1, 1, 0, HALF - 1)
                project(2 * HALF - 1, 1, 1, HALF - 1)

            chunk_loop(pe, step, end)


def layout(inputs):
    a = {k: np.asarray(v) for k, v in inputs.items()}
    C, P = 192, 96
    def halves(m):
        return np.ascontiguousarray(m.reshape(2, P, *m.shape[1:]).swapaxes(0, 1))
    out = {}
    out["x"] = a["x"].reshape(4, C, -1)
    out["ident"] = np.eye(128, dtype=np.float32)
    out["ln1_gb"] = halves(np.stack([a["L0_conv_g1"], a["L0_conv_b1"]], -1))
    out["wqkv"] = halves(a["L0_conv_w_qkv"].reshape(576, C).T)
    out["wdw"] = np.ascontiguousarray(a["L0_conv_w_dw"].reshape(6, P, 9).swapaxes(0, 1))
    out["wproj"] = halves(a["L0_conv_w_proj"].reshape(C, C).T)
    out["temp"] = np.ascontiguousarray(np.repeat(a["L0_conv_temp"].reshape(2, 3), 32, 1).T)
    wh = a["L0_conv_w_head"].transpose(1, 3, 2, 0)
    wh = np.repeat(np.repeat(wh, 32, 0), 32, 3)
    out["head_w"] = halves(wh.reshape(C, 9, C))
    c = np.arange(C) % 32
    out["head_mask"] = halves(np.stack([(c[:, None] - c[None, :] + 1 == dy) for dy in range(3)], 1).astype(np.float32))
    out["ln2_gb"] = halves(np.stack([a["L0_conv_g2"], a["L0_conv_b2"]], -1))
    out["w1"] = halves(a["L0_conv_w_fc1"].T)
    out["b1"] = np.ascontiguousarray(a["L0_conv_b_fc1"].reshape(3, 128).T)
    out["w2"] = np.ascontiguousarray(a["L0_conv_w_fc2"].T.reshape(3, 128, C).swapaxes(0, 1))
    out["b2"] = np.ascontiguousarray(a["L0_conv_b_fc2"].reshape(2, P).T)
    out["wsa"] = halves(a["L0_conv_w_sa"].reshape(C, 9))
    out["ln3_gb"] = halves(np.stack([a["L1_conv_ln_w"], a["L1_conv_ln_b"]], -1))
    out["w_in"] = halves(a["L1_conv_in_proj_w"].T)
    out["cw"] = np.ascontiguousarray(a["L1_conv_conv_w"].reshape(2, P, 9).swapaxes(0, 1))
    out["cb"] = np.ascontiguousarray(a["L1_conv_conv_b"].reshape(2, P).T)
    out["b_sa"] = np.repeat(a["L0_conv_b_sa"].reshape(1, 1), P, 0)
    xp = a["L1_conv_x_proj_w"]
    xp = np.concatenate([xp[:, :12].reshape(48, C), xp[:, 12:].reshape(32, C)], 0)
    out["w_x"] = halves(xp.T)
    row = np.arange(384).reshape(3, 128)
    img, ch = row // C, row % C
    w_dt = a["L1_conv_dt_proj_w"][:, ch, :]
    two = np.zeros((3, 2, 12, 4, 128), np.float32)
    for t in range(3):
        for i in range(2):
            two[t, i][:, :, img[t] == i] = w_dt[:, t][:, img[t] == i].transpose(2, 0, 1)
    out["w_dt"] = two.reshape(3, 24, 4, 128)
    out["dt_bias"] = np.ascontiguousarray(a["L1_conv_dt_proj_b"][:, ch].transpose(1, 2, 0))
    out["a_log"] = np.ascontiguousarray(a["L1_conv_A_log"][:, ch].transpose(1, 2, 0, 3).reshape(3, 128, 16))
    out["skip"] = np.ascontiguousarray(a["L1_conv_Ds"][:, ch].transpose(1, 2, 0))
    sel = np.zeros((3, 3, 2, 8, 8, 128), np.float32)
    for t in range(3):
        for i in range(2):
            for r in range(8):
                sel[t, :, i, r, r, img[t] == i] = 1
    out["sel"] = sel.reshape(3, 48, 8, 128)
    out["ln4_gb"] = halves(np.stack([a["L1_conv_out_norm_w"], a["L1_conv_out_norm_b"]], -1))
    out["w_out"] = halves(a["L1_conv_out_proj_w"].T)
    return out


def build(nc, arrays):
    d = {}
    for name, array in arrays.items():
        d[name] = nc.dram_tensor("in_" + name, array.shape, mybir.dt.from_np(array.dtype), kind="ExternalInput").ap()
    image = [B, C, L]
    for name, shape, dt in (("x1", image, FP32), ("v", image, FP32), ("mt", [B, P, 2, C], FP32), ("x2", image, FP32),
                            ("y", image, FP32), ("planes", [B, 9 * PLANE + 3], FP32), ("x4", image, FP32),
                            ("sz", image, FP32), ("u", image, FP32), ("dts", [DIRS, B, RANK, L], FP32),
                            ("bc", [DIRS, B, 2 * STATES, L], FP32),
                            ("bcs", [DIRS, PAIRS, 6 * 2 * STATES, L], BF16), ("ys", image, FP32)):
        d[name] = nc.dram_tensor(name, shape, dt, kind="Internal").ap()
    d["out"] = nc.dram_tensor("out", image, FP32, kind="ExternalOutput").ap()
    attention_statistics(nc, d)
    attention_and_mlp(nc, d)
    gate_and_scan_inputs(nc, d)
    split_and_turn(nc, d)
    selective_scans(nc, d)
    output_projection(nc, d)


def kernel(**inputs):
    import concourse.bacc as bacc
    from concourse.bass_utils import run_bass_kernel_spmd

    arrays = layout(inputs)
    nc = bacc.Bacc("TRN2", target_bir_lowering=False, num_devices=1)
    build(nc, arrays)
    r = run_bass_kernel_spmd(nc, [{"in_" + k: v for k, v in arrays.items()}], core_ids=[0])
    return r.results[0]["out"].reshape(B, C, HH, WW)
```

```python
import concourse.bass as bass
from concourse import mybir
from contextlib import ExitStack
import numpy as np

FP32 = mybir.dt.float32
BF16 = mybir.dt.bfloat16
ALU = mybir.AluOpType
ACT = mybir.ActivationFunctionType
AXX = mybir.AxisListType.X

B, C, HH, WW = 4, 192, 128, 128
L = HH * WW
P = 96
ROWS = 4
NPX = ROWS * WW
CHUNKS = HH // ROWS
HEADS, HD = 6, 32
HID = 384
TAPS = [(dy, dx) for dy in range(3) for dx in range(3)]
PLANE = (HH + 2) * (WW + 2)
LN_EPS = 1e-5
DMA = 16


class Chunk:

    def __init__(self, b, j, i):
        self.b, self.j, self.i, self.p = b, j, i, i % 2
        self.s = 2 * j + i
        self.half = j + i // 2
        self.q = b * CHUNKS + self.s
        self.pairs = b * (CHUNKS // 2) + self.half
        self.c = b * (CHUNKS + 1) + self.s
        self.c_pairs = b * (CHUNKS // 2 + 1 - self.p) + self.half
        known = isinstance(j, int)
        self.is_first = known and self.s == 0
        self.is_real = not known or 0 <= self.s < CHUNKS
        self.is_last = known and self.s == CHUNKS
        self.is_convolved = self.is_real or self.is_last

    def back(self, k):
        return Chunk(self.b, self.j, self.i - k)


def image_loop(eng, step, more=0, start=None, end=None):
    with eng.Fori(0, B) as b:
        if start:
            start(b)
        for i in range(4):
            step(Chunk(b, 0, i))
        with eng.Fori(2, CHUNKS // 2) as j:
            step(Chunk(b, j, 0))
            step(Chunk(b, j, 1))
        for i in range(CHUNKS, CHUNKS + more):
            step(Chunk(b, 0, i))
        if end:
            end(b)


def attention_statistics(nc, d):
    with ExitStack() as ctx:
        def sb(name, shape, dt=FP32):
            return ctx.enter_context(nc.sbuf_tensor("a_" + name, shape, dt))

        def ps(name, shape):
            return ctx.enter_context(nc.psum_tensor("a_" + name, shape, FP32))

        sems = []
        ctx.callback(nc.all_engine_barrier)
        ctx.callback(nc.clear_and_free_semaphores, sems)

        def sem(name):
            sems.append(nc.alloc_semaphore("a_" + name))
            return sems[-1]

        PRODS = 6
        mean_w = sb("mean_w", [P, P])
        ones = sb("ones", [P, P])
        ident = sb("ident", [P, P])
        ln_gb = sb("ln_gb", [P, 2, 2])
        wqkv = sb("wqkv", [P, 2, 3 * C])
        wdw = sb("wdw", [P, 6, 9])
        qdiag = sb("qdiag", [P, 9, P])
        wproj = sb("wproj", [P, 2, C])
        temp = sb("temp", [P, 2])
        head_w = sb("head_w", [P, 2, 9, C])
        head_mask = sb("head_mask", [P, 2, 3, C])
        head_conv = sb("head_conv", [P, 2, 3, C])
        consts = sb("consts", [P, 2])
        x_sum = sb("x_sum", [P, NPX])
        sq_sum = sb("sq_sum", [P, NPX])
        x_in = [sb(f"x_in{p}", [P, 2, NPX]) for p in range(2)]
        xc = [sb(f"xc{p}", [P, 2, NPX]) for p in range(2)]
        sq = sb("sq", [P, 2, NPX])
        rstd = sb("rstd", [P, 2, NPX])
        x1 = [sb(f"x1{p}", [P, 2, NPX]) for p in range(2)]
        raw = [sb(f"raw{p}", [P, 6, ROWS + 2, WW + 2]) for p in range(2)]
        zeros = sb("zeros", [P, WW])
        prod = [sb(f"prod{i}", [P, ROWS, WW]) for i in range(PRODS)]
        qc = sb("qc", [P, ROWS, WW])
        kc = sb("kc", [P, 2, ROWS, WW])
        vc = [sb(f"vc{p}", [P, 2, ROWS, WW]) for p in range(2)]
        qkt = sb("qkt", [128, ROWS, 2, 2, P])
        gs = sb("gs", [P, 2, HD])
        dq = sb("dq", [P, 2, P])
        dk = sb("dk", [P, 2, P])
        nq = sb("nq", [P, 2])
        nk = sb("nk", [P, 2, HD])
        nqs = sb("nqs", [P, 2])
        nks = sb("nks", [P, 2, HD])
        s_pad = sb("s_pad", [P, 2, HD + 2])
        mx = sb("mx", [P, 2])
        ex = sb("ex", [P, 2, HD])
        sm = sb("sm", [P, 2])
        attn_bd = sb("attn_bd", [P, 2, P])
        mt = sb("mt", [P, 2, C])

        stat_ps = ps("stat_ps", [P, NPX])
        kt_ps = ps("kt_ps", [128, 2, 2, P])
        qkv_ps = [ps(f"qkv_ps{p}", [P, NPX]) for p in range(2)]
        qt_ps = [ps(f"qt_ps{p}", [128, 2, 2, P]) for p in range(2)]
        gram_ps = ps("gram_ps", [P, 2, 512])
        nk_ps = stat_ps[:, 0:2 * P].rearrange("p (h d) -> p h d", h=2)
        conv_ps = kt_ps[0:P, 0, 0, 0:2 * HD].rearrange("p (h d) -> p h d", h=2)
        mt_ps = qkv_ps[0][:, 0:2 * C].rearrange("p (h d) -> p h d", h=2)

        w_loaded = sem("w_loaded")
        w_ready = sem("w_ready")
        v_prep = sem("v_prep")
        x_loaded = [sem(f"x_loaded{p}") for p in range(2)]
        x1_stored = [sem(f"x1_stored{p}") for p in range(2)]
        v_stored = [sem(f"v_stored{p}") for p in range(2)]
        mt_stored = sem("mt_stored")
        img_done = sem("img_done")
        x_summed = sem("x_summed")
        sq_summed = sem("sq_summed")
        mu_ready = sem("mu_ready")
        xc_ready = sem("xc_ready")
        sq_ready = sem("sq_ready")
        var_ready = sem("var_ready")
        ln_done = sem("ln_done")
        r_ready = sem("r_ready")
        xr_done = sem("xr_done")
        x1_ready = sem("x1_ready")
        qkv_ready = sem("qkv_ready")
        qkv_evac = sem("qkv_evac")
        zero_row_ready = sem("zero_row_ready")
        zeros_ready = sem("zeros_ready")
        carried = sem("carried")
        raw_ready = sem("raw_ready")
        conv_seq = sem("conv_seq")
        prod_ready = sem("prod_ready")
        add_seq = sem("add_seq")
        qt_ready = sem("qt_ready")
        qt_evac = sem("qt_evac")
        kt_ready = sem("kt_ready")
        kt_evac = sem("kt_evac")
        gram_done = sem("gram_done")
        fin_v = sem("fin_v")
        fin_s = sem("fin_s")
        fin_t = sem("fin_t")
        FIN_V, FIN_S, FIN_T = 15, 2, 3
        VTAPS, PTAPS, PSUMS = 27, 18, 16

        loads = [(ident, d["ident"][0:P, 0:P]), (ln_gb, d["ln1_gb"]), (wqkv, d["wqkv"]), (wdw, d["wdw"]),
                 (wproj, d["wproj"]), (temp, d["temp"]), (head_w, d["head_w"]), (head_mask, d["head_mask"])]
        xv = d["x"].rearrange("b (h p) n -> b p h n", h=2)
        x1v = d["x1"].rearrange("b (h p) n -> b p h n", h=2)
        vv = d["v"].rearrange("b (h p) n -> b p h n", h=2)

        LATE = 4

        block = ctx.enter_context(nc.Block())

        @block.sync
        def _(sp):
            for dst, src in loads:
                sp.dma_start(dst[:], src).then_inc(w_loaded, DMA)

            def load(k, waits=True):
                if waits:
                    sp.wait_ge(xc_ready, k.q - 1)
                sp.dma_start(x_in[k.p][:], xv[k.b, :, :, bass.ds(k.s * NPX, NPX)]).then_inc(x_loaded[k.p], DMA)

            def store_x1(k):
                sp.wait_ge(x1_ready, k.q + 1)
                sp.dma_start(x1v[k.b, :, :, bass.ds(k.s * NPX, NPX)], x1[k.p][:]).then_inc(x1_stored[k.p], DMA)

            def store_v(k):
                lo, hi = 1 if k.is_first else 0, 1 if k.is_last else ROWS
                px = bass.ds(k.s * NPX + (lo - 1) * WW, (hi - lo) * WW)
                for h in range(2):
                    if h == 0:
                        sp.wait_ge(conv_seq, k.c * VTAPS + VTAPS)
                    else:
                        sp.wait_ge(add_seq, k.c * PSUMS + PSUMS)
                    sp.dma_start(vv[k.b, :, h, px],
                                 vc[k.p][:, h, lo:hi, :].rearrange("p r w -> p (r w)")).then_inc(v_stored[k.p], DMA)

            def step(k, following):
                if k.back(1).is_first:
                    store_x1(k.back(1))
                if following:
                    load(following)
                if k.back(4).is_convolved:
                    store_v(k.back(4))
                if k.back(1).is_real and not k.back(1).is_first:
                    store_x1(k.back(1))

            def image(b, more):
                for i in range(6):
                    step(Chunk(b, 0, i), Chunk(b, 0, i + 1) if i else None)
                with sp.Fori(3, CHUNKS // 2 - 1) as j:
                    step(Chunk(b, j, 0), Chunk(b, j, 1))
                    step(Chunk(b, j, 1), Chunk(b, j, 2))
                step(Chunk(b, 0, CHUNKS - 2), Chunk(b, 0, CHUNKS - 1))
                for i in range(2):
                    step(Chunk(b, 0, CHUNKS - 1 + i), Chunk(b + 1, 0, i) if more else None)
                for i in range(1, LATE + 1):
                    step(Chunk(b, 0, CHUNKS + i), None)
                sp.wait_ge(img_done, b + 1)
                sp.dma_start(d["mt"][b], mt[:]).then_inc(mt_stored, DMA)

            for i in range(2):
                load(Chunk(0, 0, i), waits=False)
            with sp.Fori(0, B - 1) as b:
                image(b, True)
            image(B - 1, False)
            for p in range(2):
                sp.wait_ge(x1_stored[p], DMA * B * CHUNKS // 2)
            sp.wait_ge(v_stored[0], 2 * DMA * B * (CHUNKS // 2 + 1))
            sp.wait_ge(v_stored[1], 2 * DMA * B * (CHUNKS // 2))
            sp.wait_ge(mt_stored, DMA * B)

        @block.gpsimd
        def _(pool):
            nc.gpsimd.memset(mean_w[:], 1.0 / C)
            nc.gpsimd.memset(ones[:], 1.0)
            nc.gpsimd.memset(consts[:, 0:1], LN_EPS)
            nc.gpsimd.memset(consts[:, 1:2], 0.0)
            nc.gpsimd.memset(s_pad[:], 0.0)
            nc.gpsimd.memset(attn_bd[:], 0.0)
            nc.gpsimd.memset(zeros[:], 0.0).then_inc(zero_row_ready, 1)
            for p in range(2):
                nc.gpsimd.memset(raw[p][:, :, :, 0:1], 0.0)
                last = nc.gpsimd.memset(raw[p][:, :, :, WW + 1:WW + 2], 0.0)
            last.then_inc(w_ready, 1)

            def clear(rows):
                z = zeros[:, None, None, :].to_broadcast(rows.shape)
                nc.gpsimd.tensor_tensor(rows, z, z, ALU.add).then_inc(zeros_ready, 1)

            def sum_x(k):
                pool.wait_ge(x_loaded[k.p], (k.pairs + 1) * DMA)
                pool.wait_ge(mu_ready, k.q)
                nc.gpsimd.tensor_tensor(x_sum[:], x_in[k.p][:, 0], x_in[k.p][:, 1], ALU.add).then_inc(x_summed, 1)

            def sum_squares(k):
                pool.wait_ge(sq_ready, k.q + 1)
                pool.wait_ge(var_ready, k.q)
                nc.gpsimd.tensor_tensor(sq_sum[:], sq[:, 0], sq[:, 1], ALU.add).then_inc(sq_summed, 1)

            def start(b):
                pool.wait_ge(zero_row_ready, 1)
                pool.wait_ge(img_done, b)
                clear(raw[0][:, :, 0:2, 1:WW + 1])

            def add(k, half, t):
                out = vc[k.p][:, 1] if half else qc[:]
                n = half * 9 + t
                if t == 1:
                    pool.wait_ge(prod_ready, k.c * PTAPS + n + 1)
                    if half:
                        pool.wait_ge(v_stored[k.p], k.c_pairs * 2 * DMA)
                    else:
                        pool.wait_ge(qt_ready, k.c * 2)
                    first = prod[(n - 1) % PRODS][:]
                else:
                    pool.wait_ge(prod_ready, k.c * PTAPS + n + 1)
                    pool.wait_ge(add_seq, k.c * PSUMS + half * 8 + t - 1)
                    first = out
                nc.gpsimd.tensor_tensor(out, first, prod[n % PRODS][:], ALU.add).then_inc(add_seq, 1)

            def step(k):
                if isinstance(k.j, int) and k.s == CHUNKS + 2:
                    pool.wait_ge(conv_seq, k.back(3).c * VTAPS)
                    pool.wait_ge(prod_ready, k.back(3).c * PTAPS)
                    pool.wait_ge(qt_ready, k.back(3).c * 2)
                    clear(raw[0][:, :, 2:3, 1:WW + 1])
                if k.is_real:
                    sum_x(k)
                if k.back(3).is_convolved:
                    add(k.back(3), 0, 1)
                if k.back(1).is_real:
                    sum_squares(k.back(1))
                if k.back(3).is_convolved:
                    for t in range(2, 9):
                        add(k.back(3), 0, t)
                    for t in range(1, 9):
                        add(k.back(3), 1, t)

            image_loop(pool, step, LATE, start)

        @block.vector
        def _(dve):
            dve.wait_ge(w_loaded, DMA * len(loads))
            for t in range(9):
                nc.vector.tensor_scalar(qdiag[:, t, :], ident[:], wdw[:, 0, t:t + 1], None, ALU.mult)
            for dx in range(3):
                nc.vector.tensor_tensor(head_w[:, :, 3 * dx:3 * dx + 3, :], head_w[:, :, 3 * dx:3 * dx + 3, :],
                                        head_mask[:], ALU.mult).then_inc(v_prep, 1)
            dve.wait_ge(v_prep, 3)
            hw = head_w[:].rearrange("p h (x y) c -> p h x y c", x=3)
            for h in range(2):
                nc.vector.tensor_tensor(head_conv[:, h], hw[:, h, :, 0, :], hw[:, h, :, 1, :], ALU.add).then_inc(v_prep, 1)
            dve.wait_ge(v_prep, 5)
            for h in range(2):
                last = nc.vector.tensor_tensor(head_conv[:, h], head_conv[:, h], hw[:, h, :, 2, :], ALU.add)
            last.then_inc(w_ready, 1)
            dve.wait_ge(w_ready, 2)

            def conv(k, tiles, op0):
                done = k.c * VTAPS + op0
                for t, (dy, dx) in enumerate(TAPS):
                    for h, (src, out) in enumerate(tiles):
                        window = raw[k.p][:, src, dy:dy + ROWS, dx:dx + WW]
                        w = wdw[:, src, t:t + 1]
                        if t == 0:
                            ins = nc.vector.tensor_scalar(out, window, w, None, ALU.mult)
                        else:
                            dve.wait_ge(conv_seq, done + len(tiles) * (t - 1) + h + 1)
                            ins = nc.vector.scalar_tensor_tensor(out, window, w, out, ALU.mult, ALU.add)
                        ins.then_inc(conv_seq, 1)

            def conv_k(k):
                dve.wait_ge(raw_ready, k.c + 1)
                dve.wait_ge(kt_ready, k.c * 2)
                conv(k, [(2, kc[:, 0]), (3, kc[:, 1])], 0)

            def conv_v(k):
                dve.wait_ge(v_stored[k.p], k.c_pairs * 2 * DMA)
                conv(k, [(4, vc[k.p][:, 0])], 18)

            def center(k):
                dve.wait_ge(mu_ready, k.q + 1)
                dve.wait_ge(x1_ready, k.q)
                mu = stat_ps[:].unsqueeze(1).broadcast_to([P, 2, NPX])
                nc.vector.tensor_tensor(xc[k.p][:], x_in[k.p][:], mu, ALU.subtract).then_inc(xc_ready, 1)

            def normalize(k):
                dve.wait_ge(r_ready, k.q + 1)
                dve.wait_ge(xc_ready, k.q + 1)
                r = rstd[:, 1:2, :].broadcast_to([P, 2, NPX])
                nc.vector.tensor_tensor(xc[k.p][:], xc[k.p][:], r, ALU.mult).then_inc(xr_done, 1)
                dve.wait_ge(xr_done, k.q + 1)
                dve.wait_ge(x1_stored[k.p], k.pairs * DMA)
                if not k.is_first:
                    dve.wait_ge(qkv_ready, k.q * 6 - 6)
                for h in range(2):
                    last = nc.vector.tensor_scalar(x1[k.p][:, h], xc[k.p][:, h], ln_gb[:, h, 0:1], ln_gb[:, h, 1:2],
                                                   ALU.mult, ALU.add)
                last.then_inc(x1_ready, 1)

            def step(k):
                now, older = k.back(1), k.back(3)
                if now.is_real:
                    center(now)
                if older.is_convolved:
                    conv_k(older)
                if now.is_real:
                    normalize(now)
                if older.is_convolved:
                    conv_v(older)

            def end(b):
                n = [0]

                def link(ins):
                    n[0] += 1
                    ins.then_inc(fin_v, 1)
                    return n[0]

                def after(k):
                    dve.wait_ge(fin_v, b * FIN_V + k)

                dve.wait_ge(gram_done, (b + 1) * (CHUNKS + 1))
                eye = ident[:].unsqueeze(1).broadcast_to([P, 2, P])
                nc.vector.tensor_tensor(dk[:], gram_ps[:, :, 2 * P:3 * P], eye, ALU.mult).then_inc(fin_v, 1)
                n[0] = 1
                dq_done = link(nc.vector.tensor_tensor(dq[:], gram_ps[:, :, 0:P], eye, ALU.mult))
                for j in range(3):
                    r = slice(32 * j, 32 * j + 32)
                    last = nc.vector.tensor_copy(gs[r], gram_ps[r, :, P + 32 * j:P + 32 * j + 32])
                gs_done = link(last)
                after(dq_done)
                link(nc.vector.reduce_sum(nq[:], dq[:], axis=AXX))
                dve.wait_ge(fin_t, b * FIN_T + 1)
                for j in range(3):
                    r = slice(32 * j, 32 * j + 32)
                    last = nc.vector.tensor_copy(nk[r], nk_ps[r, :, 32 * j:32 * j + 32])
                link(last)
                dve.wait_ge(fin_s, b * FIN_S + 1)
                k = link(nc.vector.tensor_scalar(nqs[:], nqs[:], 1e-12, None, ALU.max))
                link(nc.vector.tensor_scalar(nks[:], nks[:], 1e-12, None, ALU.max))
                after(k + 1)
                link(nc.vector.reciprocal(nqs[:], nqs[:]))
                k = link(nc.vector.reciprocal(nks[:], nks[:]))
                after(k)
                for h in range(2):
                    last = nc.vector.tensor_scalar(gs[:, h], gs[:, h], nqs[:, h:h + 1], temp[:, h:h + 1],
                                                   ALU.mult, ALU.mult)
                k = link(last)
                after(k)
                k = link(nc.vector.tensor_tensor(s_pad[:, :, 1:HD + 1], gs[:], nks[:], ALU.mult))
                dve.wait_ge(fin_t, b * FIN_T + 2)
                k = link(nc.vector.reduce_max(mx[:], conv_ps, axis=AXX))
                after(k)
                link(nc.vector.tensor_scalar(mx[:], mx[:], -1.0, None, ALU.mult))
                dve.wait_ge(fin_s, b * FIN_S + 2)
                k = link(nc.vector.reciprocal(sm[:], sm[:]))
                after(k)
                for h in range(2):
                    for j in range(3):
                        r = slice(32 * j, 32 * j + 32)
                        last = nc.vector.tensor_scalar(attn_bd[r, h, r], ex[r, h], sm[r, h:h + 1], None, ALU.mult)
                link(last)
                assert n[0] == FIN_V
                dve.wait_ge(fin_t, b * FIN_T + 3)
                dve.wait_ge(mt_stored, b * DMA)
                nc.vector.tensor_copy(mt[:], mt_ps).then_inc(img_done, 1)

            image_loop(dve, step, LATE, end=end)

        @block.scalar
        def _(act):
            act.wait_ge(w_ready, 2)

            def square(k):
                act.wait_ge(xc_ready, k.q + 1)
                act.wait_ge(sq_summed, k.q)
                nc.scalar.activation(sq[:], xc[k.p][:], ACT.Square).then_inc(sq_ready, 1)

            def deviation(k):
                act.wait_ge(var_ready, k.q + 1)
                act.wait_ge(xr_done, k.q)
                nc.scalar.activation(rstd[:, 0], stat_ps[:], ACT.Ln, bias=consts[:, 0:1]).then_inc(ln_done, 1)
                act.wait_ge(ln_done, k.q + 1)
                nc.scalar.activation(rstd[:, 1], rstd[:, 0], ACT.Exp, scale=-0.5, bias=consts[:, 1:2]).then_inc(r_ready, 1)

            def rows_above(k):
                if k.is_first:
                    act.wait_ge(zeros_ready, k.b * 2 + 1)
                    return
                act.wait_ge(conv_seq, k.back(1).c * VTAPS)
                act.wait_ge(qt_ready, k.back(1).c * 2)
                act.wait_ge(prod_ready, k.back(1).c * PTAPS)
                act.wait_ge(raw_ready, k.c)
                nc.scalar.copy(raw[k.p][:, :, 0:2, 1:WW + 1],
                               raw[1 - k.p][:, :, ROWS:ROWS + 2, 1:WW + 1]).then_inc(carried, 1)
                if k.is_last:
                    act.wait_ge(zeros_ready, k.b * 2 + 2)
                    act.wait_ge(carried, (k.b + 1) * CHUNKS)
                    act.sem_inc(raw_ready, 1)

            def take_qkv(k, tiles):
                for t in tiles:
                    act.wait_ge(qkv_ready, k.q * 6 + t + 1)
                    nc.scalar.copy(raw[k.p][:, t, 2:ROWS + 2, 1:WW + 1],
                                   qkv_ps[t % 2][:].rearrange("p (r w) -> p r w", w=WW)).then_inc(qkv_evac, 1)
                    if t == 5:
                        act.wait_ge(qkv_evac, k.q * 6 + 6)
                        act.sem_inc(raw_ready, 1)

            def take_q(k, i):
                act.wait_ge(gram_done, k.c)
                act.wait_ge(qt_ready, k.c * 2 + i + 1)
                nc.scalar.copy(qkt[:, 2 * i:2 * i + 2, :, 0, :], qt_ps[i][:]).then_inc(qt_evac, 1)

            def take_k(k, i):
                act.wait_ge(kt_ready, k.c * 2 + i + 1)
                nc.scalar.copy(qkt[:, 2 * i:2 * i + 2, :, 1, :], kt_ps[:]).then_inc(kt_evac, 1)

            def product(k, n):
                src, t = 1 if n < 9 else 5, n % 9
                if n == 0:
                    act.wait_ge(raw_ready, k.c + 1)
                added = lambda m: m // 9 * 8 + max(m % 9, 1)
                if n >= PRODS:
                    act.wait_ge(add_seq, k.c * PSUMS + added(n - PRODS))
                elif k.is_first:
                    act.wait_ge(add_seq, k.c * PSUMS)
                else:
                    act.wait_ge(add_seq, k.c * PSUMS - PSUMS + added(n + 18 - PRODS))
                dy, dx = TAPS[t]
                nc.scalar.activation(prod[n % PRODS][:], raw[k.p][:, src, dy:dy + ROWS, dx:dx + WW], ACT.Identity,
                                     scale=wdw[:, src, t:t + 1], bias=consts[:, 1:2]).then_inc(prod_ready, 1)

            def step(k):
                older = k.back(3)

                def products(lo, hi):
                    for n in range(lo, hi):
                        if older.is_convolved:
                            product(older, n)

                def take(tiles):
                    if k.back(2).is_real:
                        take_qkv(k.back(2), tiles)

                products(0, 1)
                if k.back(1).is_real:
                    square(k.back(1))
                products(1, 2)
                if k.back(2).is_convolved:
                    rows_above(k.back(2))
                take([0])
                products(2, 4)
                take([1])
                products(4, 5)
                take([2])
                products(5, 6)
                if k.back(1).is_real:
                    deviation(k.back(1))
                take([3])
                products(6, 8)
                take([4])
                products(8, 9)
                take([5])
                products(9, 12)
                if older.is_convolved:
                    take_q(older, 0)
                    take_k(older, 0)
                products(12, 15)
                if older.is_convolved:
                    take_q(older, 1)
                    take_k(older, 1)
                products(15, 18)

            def end(b):
                nc.scalar.preload_act_table_set("sqrt_and_others")
                act.wait_ge(fin_v, b * FIN_V + 5)
                nc.scalar.activation(nqs[:], nq[:], ACT.Sqrt, bias=consts[:, 1:2])
                nc.scalar.activation(nks[:], nk[:], ACT.Sqrt, bias=consts[:, 1:2]).then_inc(fin_s, 1)
                nc.scalar.preload_act_table_set("natural_log_exp_and_others")
                act.wait_ge(fin_v, b * FIN_V + 13)
                for h in range(2):
                    last = nc.scalar.activation(ex[:, h], conv_ps[:, h], ACT.Exp, bias=mx[:, h:h + 1],
                                                accum_out=sm[:, h:h + 1])
                last.then_inc(fin_s, 1)

            nc.scalar.preload_act_table_set("natural_log_exp_and_others")
            image_loop(act, step, LATE, end=end)

        @block.tensor
        def _(pe):
            pe.wait_ge(w_ready, 2)
            pe.wait_ge(w_loaded, DMA * len(loads))

            def q_conv(k, i):
                pe.wait_ge(raw_ready, k.c + 1)
                pe.wait_ge(qt_evac, k.c * 2)
                for r in range(2):
                    for t, (dy, dx) in enumerate(TAPS):
                        nc.tensor.matmul(qt_ps[i][:, r, 0], raw[k.p][:, 0, 2 * i + r + dy, dx:dx + WW],
                                         qdiag[:, t], start=(t == 0), stop=(t == 8))
                pe.wait_ge(add_seq, k.c * PSUMS + 8)
                for r in range(2):
                    last = nc.tensor.transpose(qt_ps[i][:, r, 1], qc[:, 2 * i + r], ident[:])
                last.then_inc(qt_ready, 1)

            def k_transpose(k, i):
                pe.wait_ge(conv_seq, k.c * VTAPS + 18)
                pe.wait_ge(kt_evac, k.c * 2 + i)
                for r in range(2):
                    for h in range(2):
                        last = nc.tensor.transpose(kt_ps[:, r, h], kc[:, h, 2 * i + r], ident[:])
                last.then_inc(kt_ready, 1)

            def gram(k):
                pe.wait_ge(qt_evac, k.c * 2 + 2)
                pe.wait_ge(kt_evac, k.c * 2 + 2)
                rows = range(1 if k.is_first else 0, 1 if k.is_last else ROWS)
                for n, r in enumerate(rows):
                    for h in range(2):
                        nc.tensor.matmul(gram_ps[:, h, 0:2 * P], qkt[:, r, h, 0], qkt[:, r, h],
                                         start=k.is_first and n == 0, stop=True, skip_group_check=True)
                        last = nc.tensor.matmul(gram_ps[:, h, 2 * P:3 * P], qkt[:, r, h, 1], qkt[:, r, h, 1],
                                                start=False, stop=True, skip_group_check=True)
                last.then_inc(gram_done, 1)

            def qkv(k, tiles):
                pe.wait_ge(x1_ready, k.q + 1)
                for t in tiles:
                    pe.wait_ge(qkv_evac, k.q * 6 + t - 1 if t >= 2 else k.q * 6)
                    for h in range(2):
                        last = nc.tensor.matmul(qkv_ps[t % 2][:], wqkv[:, h, t * P:(t + 1) * P], x1[k.p][:, h],
                                                start=(h == 0), stop=(h == 1))
                    last.then_inc(qkv_ready, 1)

            def mean(k):
                pe.wait_ge(x_summed, k.q + 1)
                pe.wait_ge(r_ready, k.q)
                nc.tensor.matmul(stat_ps[:], mean_w[:], x_sum[:], start=True, stop=True).then_inc(mu_ready, 1)

            def variance(k):
                pe.wait_ge(sq_summed, k.q + 1)
                nc.tensor.matmul(stat_ps[:], mean_w[:], sq_sum[:], start=True, stop=True).then_inc(var_ready, 1)

            def start(b):
                pe.wait_ge(img_done, b)

            def step(k):
                if k.back(2).is_real:
                    qkv(k.back(2), range(0, 3))
                if k.back(1).is_real:
                    variance(k.back(1))
                if k.back(2).is_real:
                    qkv(k.back(2), range(3, 6))
                if k.back(3).is_convolved:
                    for i in range(2):
                        q_conv(k.back(3), i)
                        k_transpose(k.back(3), i)
                if k.is_real:
                    mean(k)
                if k.back(3).is_convolved:
                    gram(k.back(3))

            def end(b):
                pe.wait_ge(fin_v, b * FIN_V + 1)
                for h in range(2):
                    last = nc.tensor.matmul(nk_ps[:, h], ones[:], dk[:, h], start=True, stop=True)
                last.then_inc(fin_t, 1)
                pe.wait_ge(fin_v, b * FIN_V + 11)
                for o in range(2):
                    for n, (h, dx) in enumerate((h, dx) for h in range(2) for dx in range(3)):
                        last = nc.tensor.matmul(conv_ps[:, o], head_conv[:, h, dx, o * P:(o + 1) * P],
                                                s_pad[:, h, dx:dx + HD], start=(n == 0), stop=(n == 5))
                last.then_inc(fin_t, 1)
                pe.wait_ge(fin_v, b * FIN_V + 15)
                for h in range(2):
                    last = nc.tensor.matmul(mt_ps[:, h], attn_bd[:, h], wproj[:, h], start=True, stop=True)
                last.then_inc(fin_t, 1)

            image_loop(pe, step, LATE, start, end)


def attention_and_mlp(nc, d):
    with ExitStack() as ctx:
        def sb(name, shape, dt=FP32):
            return ctx.enter_context(nc.sbuf_tensor("b_" + name, shape, dt))

        def ps(name, shape):
            return ctx.enter_context(nc.psum_tensor("b_" + name, shape, FP32))

        sems = []
        ctx.callback(nc.all_engine_barrier)
        ctx.callback(nc.clear_and_free_semaphores, sems)

        def sem(name):
            sems.append(nc.alloc_semaphore("b_" + name))
            return sems[-1]

        mean_w = sb("mean_w", [P, P])
        ln_gb = sb("ln_gb", [P, 2, 2])
        w1 = sb("w1", [P, 2, HID])
        b1 = sb("b1", [128, 3])
        w2 = sb("w2", [128, 3, C])
        b2 = sb("b2", [P, 2])
        wsa = sb("wsa", [P, 2, 9])
        consts = sb("consts", [P, 2])
        zeros = sb("zeros", [9 * PLANE // 1300, 1300])
        mt = sb("mt", [P, 2, C])
        x1 = [sb(f"x1{p}", [P, 2, NPX]) for p in range(2)]
        v = [sb(f"v{p}", [P, 2, NPX]) for p in range(2)]
        x2 = [sb(f"x2{p}", [P, 2, NPX]) for p in range(2)]
        xn = [sb(f"xn{p}", [P, 2, NPX]) for p in range(2)]
        xg = [sb(f"xg{p}", [P, 2, NPX]) for p in range(2)]
        sq = sb("sq", [P, 2, NPX])
        rstd = sb("rstd", [P, 2, NPX])
        hid = sb("hid", [128, 3, NPX])
        y = [sb(f"y{p}", [P, 2, NPX]) for p in range(2)]
        taps = [sb(f"taps{p}", [9, NPX]) for p in range(2)]

        o_ps = ps("o_ps", [P, 2, NPX])
        stat_ps = ps("stat_ps", [P, NPX])
        h_ps = [ps(f"h_ps{p}", [128, NPX]) for p in range(2)]
        y_ps = [ps(f"y_ps{p}", [P, NPX]) for p in range(2)]
        taps_ps = ps("taps_ps", [9, NPX])

        w_loaded = sem("w_loaded")
        w_ready = sem("w_ready")
        border_zero = sem("border_zero")
        mt_loaded = sem("mt_loaded")
        xv_loaded = [sem(f"xv_loaded{p}") for p in range(2)]
        x2_stored = [sem(f"x2_stored{p}") for p in range(2)]
        y_stored = [sem(f"y_stored{p}") for p in range(2)]
        o_ready = sem("o_ready")
        x2_ready = sem("x2_ready")
        mu_ready = sem("mu_ready")
        xc_ready = sem("xc_ready")
        sq_ready = sem("sq_ready")
        var_ready = sem("var_ready")
        ln_done = sem("ln_done")
        r_ready = sem("r_ready")
        xr_done = sem("xr_done")
        xg_ready = sem("xg_ready")
        h_ready = sem("h_ready")
        h_gelu = sem("h_gelu")
        y_ready = sem("y_ready")
        y_gelu = sem("y_gelu")
        taps_ready = sem("taps_ready")
        taps_copied = sem("taps_copied")

        loads = [(ln_gb, d["ln2_gb"]), (w1, d["w1"]), (b1, d["b1"]), (w2, d["w2"]), (b2, d["b2"]), (wsa, d["wsa"])]
        x1v, vv, x2v, yv = (d[k].rearrange("b (h p) n -> b p h n", h=2) for k in ("x1", "v", "x2", "y"))
        planes = d["planes"][:, 0:9 * PLANE].rearrange("b (t r c) -> b t r c", t=9, c=WW + 2)

        def image_loop(eng, start, step, end):
            with eng.Fori(0, B) as b:
                start(b)
                step(b, 0, 0, 0, True)
                step(b, 1, 1, 0, False)
                with eng.Fori(0, CHUNKS // 2 - 1) as j:
                    step(b, 2 * j + 2, 0, j + 1, False)
                    step(b, 2 * j + 3, 1, j + 1, False)
                end(b)

        block = ctx.enter_context(nc.Block())

        @block.sync
        def _(sp):
            for dst, src in loads:
                sp.dma_start(dst[:], src).then_inc(w_loaded, DMA)
            sp.wait_ge(w_ready, 1)
            for b in range(B):
                sp.dma_start(d["planes"][b, 0:9 * PLANE].rearrange("(p n) -> p n", n=1300), zeros[:]).then_inc(border_zero, DMA)
            sp.wait_ge(border_zero, DMA * B)

            def load(b, s, p, half):
                if isinstance(s, int) and s < 2:
                    sp.wait_ge(x2_ready, b * CHUNKS)
                else:
                    sp.wait_ge(x2_ready, b * CHUNKS + s - 1)
                px = bass.ds(s * NPX, NPX)
                sp.dma_start(x1[p][:], x1v[b, :, :, px]).then_inc(xv_loaded[p], DMA)
                sp.dma_start(v[p][:], vv[b, :, :, px]).then_inc(xv_loaded[p], DMA)

            def store_x2(b, s, p):
                sp.wait_ge(x2_ready, b * CHUNKS + s + 1)
                sp.dma_start(x2v[b, :, :, bass.ds(s * NPX, NPX)], x2[p][:]).then_inc(x2_stored[p], DMA)

            def store_y(b, s, p):
                q = b * CHUNKS + s
                sp.wait_ge(y_gelu, (q + 1) * 2)
                sp.dma_start(yv[b, :, :, bass.ds(s * NPX, NPX)], y[p][:]).then_inc(y_stored[p], DMA)
                sp.wait_ge(taps_copied, q + 1)
                sp.dma_start(planes[b, :, bass.ds(s * ROWS + 1, ROWS), 1:WW + 1],
                             taps[p][:].rearrange("t (r w) -> t r w", w=WW)).then_inc(y_stored[p], DMA)

            with sp.Fori(0, B) as b:
                sp.wait_ge(o_ready, b * CHUNKS)
                sp.dma_start(mt[:], d["mt"][b]).then_inc(mt_loaded, DMA)
                load(b, 0, 0, 0)
                load(b, 1, 1, 0)
                store_x2(b, 0, 0)
                load(b, 2, 0, 1)
                store_x2(b, 1, 1)
                load(b, 3, 1, 1)
                store_y(b, 0, 0)
                with sp.Fori(0, CHUNKS // 2 - 2) as j:
                    store_x2(b, 2 * j + 2, 0)
                    load(b, 2 * j + 4, 0, j + 2)
                    store_y(b, 2 * j + 1, 1)
                    store_x2(b, 2 * j + 3, 1)
                    load(b, 2 * j + 5, 1, j + 2)
                    store_y(b, 2 * j + 2, 0)
                store_x2(b, CHUNKS - 2, 0)
                store_y(b, CHUNKS - 3, 1)
                store_x2(b, CHUNKS - 1, 1)
                store_y(b, CHUNKS - 2, 0)
                store_y(b, CHUNKS - 1, 1)
            for p in range(2):
                sp.wait_ge(x2_stored[p], DMA * B * CHUNKS // 2)
                sp.wait_ge(y_stored[p], DMA * B * CHUNKS)

        @block.gpsimd
        def _(pool):
            nc.gpsimd.memset(zeros[:], 0.0)
            nc.gpsimd.memset(mean_w[:], 1.0 / C)
            nc.gpsimd.memset(consts[:, 0:1], LN_EPS)
            nc.gpsimd.memset(consts[:, 1:2], 0.0).then_inc(w_ready, 1)

        @block.vector
        def _(dve):
            dve.wait_ge(w_loaded, DMA * len(loads))

            def copy_taps(b, s, p, half):
                q = b * CHUNKS + s
                dve.wait_ge(taps_ready, q + 1)
                dve.wait_ge(y_stored[p], (b * (CHUNKS // 2) + half) * 2 * DMA)
                nc.vector.tensor_copy(taps[p][:], taps_ps[:]).then_inc(taps_copied, 1)

            def step(b, s, p, half, first):
                q = b * CHUNKS + s
                dve.wait_ge(o_ready, q + 1)
                dve.wait_ge(x2_stored[p], (b * (CHUNKS // 2) + half) * DMA)
                nc.vector.tensor_tensor(x2[p][:], x1[p][:], o_ps[:], ALU.add).then_inc(x2_ready, 1)
                dve.wait_ge(mu_ready, q + 1)
                dve.wait_ge(x2_ready, q + 1)
                dve.wait_ge(xg_ready, q)
                mu = stat_ps[:].unsqueeze(1).broadcast_to([P, 2, NPX])
                nc.vector.tensor_tensor(xn[p][:], x2[p][:], mu, ALU.subtract).then_inc(xc_ready, 1)
                dve.wait_ge(r_ready, q + 1)
                dve.wait_ge(xc_ready, q + 1)
                r = rstd[:, 1:2, :].broadcast_to([P, 2, NPX])
                nc.vector.tensor_tensor(xn[p][:], xn[p][:], r, ALU.mult).then_inc(xr_done, 1)
                dve.wait_ge(xr_done, q + 1)
                for h in range(2):
                    last = nc.vector.tensor_scalar(xg[p][:, h], xn[p][:, h], ln_gb[:, h, 0:1], ln_gb[:, h, 1:2],
                                                   ALU.mult, ALU.add)
                last.then_inc(xg_ready, 1)
                if not first:
                    copy_taps(b, s - 1, 1 - p, half - 1 + p)

            def start(b):
                pass

            def end(b):
                copy_taps(b, CHUNKS - 1, 1, CHUNKS // 2 - 1)

            image_loop(dve, start, step, end)

        @block.scalar
        def _(act):
            act.wait_ge(w_ready, 1)
            act.wait_ge(w_loaded, DMA * len(loads))

            def gelu_h(b, s):
                nc.scalar.preload_act_table_set("gelu_and_others")
                q = b * CHUNKS + s
                act.wait_ge(y_ready, q * 2)
                for t in range(3):
                    act.wait_ge(h_ready, q * 3 + t + 1)
                    nc.scalar.activation(hid[:, t], h_ps[t % 2][:], ACT.Gelu, bias=b1[:, t:t + 1]).then_inc(h_gelu, 1)

            def gelu_y(b, s, p, half):
                q = b * CHUNKS + s
                act.wait_ge(y_stored[p], (b * (CHUNKS // 2) + half) * 2 * DMA)
                for h in range(2):
                    act.wait_ge(y_ready, q * 2 + h + 1)
                    nc.scalar.activation(y[p][:, h], y_ps[h][:], ACT.Gelu, bias=b2[:, h:h + 1]).then_inc(y_gelu, 1)

            def start(b):
                pass

            def step(b, s, p, half, first):
                q = b * CHUNKS + s
                if not first:
                    gelu_h(b, s - 1)
                act.wait_ge(xc_ready, q + 1)
                act.wait_ge(var_ready, q)
                nc.scalar.activation(sq[:], xn[p][:], ACT.Square).then_inc(sq_ready, 1)
                if not first:
                    gelu_y(b, s - 1, 1 - p, half - 1 + p)
                nc.scalar.preload_act_table_set("natural_log_exp_and_others")
                act.wait_ge(var_ready, q + 1)
                act.wait_ge(xr_done, q)
                nc.scalar.activation(rstd[:, 0], stat_ps[:], ACT.Ln, bias=consts[:, 0:1]).then_inc(ln_done, 1)
                act.wait_ge(ln_done, q + 1)
                nc.scalar.activation(rstd[:, 1], rstd[:, 0], ACT.Exp, scale=-0.5, bias=consts[:, 1:2]).then_inc(r_ready, 1)

            def end(b):
                gelu_h(b, CHUNKS - 1)
                gelu_y(b, CHUNKS - 1, 1, CHUNKS // 2 - 1)

            image_loop(act, start, step, end)

        @block.tensor
        def _(pe):
            pe.wait_ge(w_ready, 1)
            pe.wait_ge(w_loaded, DMA * len(loads))

            def fc1(b, s, p, tiles):
                q = b * CHUNKS + s
                pe.wait_ge(xg_ready, q + 1)
                for t in tiles:
                    pe.wait_ge(h_gelu, q * 3 + t - 1 if t >= 2 else q * 3)
                    for h in range(2):
                        last = nc.tensor.matmul(h_ps[t % 2][:], w1[:, h, 128 * t:128 * t + 128], xg[p][:, h],
                                                start=(h == 0), stop=(h == 1))
                    last.then_inc(h_ready, 1)

            def fc2(b, s, h):
                q = b * CHUNKS + s
                pe.wait_ge(h_gelu, q * 3 + 3)
                pe.wait_ge(y_gelu, q * 2)
                for t in range(3):
                    last = nc.tensor.matmul(y_ps[h][:], w2[:, t, P * h:P * h + P], hid[:, t], start=(t == 0), stop=(t == 2))
                last.then_inc(y_ready, 1)

            def gate_taps(b, s, p):
                q = b * CHUNKS + s
                pe.wait_ge(taps_copied, q)
                for h in range(2):
                    pe.wait_ge(y_gelu, q * 2 + h + 1)
                    last = nc.tensor.matmul(taps_ps[:], wsa[:, h], y[p][:, h], start=(h == 0), stop=(h == 1))
                last.then_inc(taps_ready, 1)

            def start(b):
                pe.wait_ge(mt_loaded, (b + 1) * DMA)

            def step(b, s, p, half, first):
                q = b * CHUNKS + s
                pe.wait_ge(xv_loaded[p], (b * (CHUNKS // 2) + half + 1) * 2 * DMA)
                pe.wait_ge(x2_ready, q)
                for o in range(2):
                    for h in range(2):
                        last = nc.tensor.matmul(o_ps[:, o], mt[:, h, P * o:P * o + P], v[p][:, h],
                                                start=(h == 0), stop=(h == 1))
                last.then_inc(o_ready, 1)
                if not first:
                    fc1(b, s - 1, 1 - p, range(0, 2))
                pe.wait_ge(x2_ready, q + 1)
                pe.wait_ge(r_ready, q)
                for h in range(2):
                    last = nc.tensor.matmul(stat_ps[:], mean_w[:], x2[p][:, h], start=(h == 0), stop=(h == 1))
                last.then_inc(mu_ready, 1)
                if not first:
                    fc1(b, s - 1, 1 - p, range(2, 3))
                    fc2(b, s - 1, 0)
                pe.wait_ge(sq_ready, q + 1)
                for h in range(2):
                    last = nc.tensor.matmul(stat_ps[:], mean_w[:], sq[:, h], start=(h == 0), stop=(h == 1))
                last.then_inc(var_ready, 1)
                if not first:
                    fc2(b, s - 1, 1)
                    gate_taps(b, s - 1, 1 - p)

            def end(b):
                fc1(b, CHUNKS - 1, 1, range(3))
                fc2(b, CHUNKS - 1, 0)
                fc2(b, CHUNKS - 1, 1)
                gate_taps(b, CHUNKS - 1, 1)

            image_loop(pe, start, step, end)


DIRS, RANK, STATES = 4, 12, 4
NDT, NBC = DIRS * RANK, DIRS * 2 * STATES


def gate_and_scan_inputs(nc, d):
    with ExitStack() as ctx:
        def sb(name, shape, dt=FP32):
            return ctx.enter_context(nc.sbuf_tensor("c_" + name, shape, dt))

        def ps(name, shape):
            return ctx.enter_context(nc.psum_tensor("c_" + name, shape, FP32))

        sems = []
        ctx.callback(nc.all_engine_barrier)
        ctx.callback(nc.clear_and_free_semaphores, sems)

        def sem(name):
            sems.append(nc.alloc_semaphore("c_" + name))
            return sems[-1]

        mean_w = sb("mean_w", [P, P])
        ones = sb("ones", [9, P])
        ln_gb = sb("ln_gb", [P, 2, 2])
        w_in = sb("w_in", [P, 2, 2 * C])
        cw = sb("cw", [P, 2, 9])
        cb = sb("cb", [P, 2])
        w_x = sb("w_x", [P, 2, NDT + NBC])
        b_sa = sb("b_sa", [P, 1])
        consts = sb("consts", [P, 2])
        x2 = [sb(f"x2{p}", [P, 2, NPX]) for p in range(2)]
        y = [sb(f"y{p}", [P, 2, NPX]) for p in range(2)]
        taps = [sb(f"taps{p}", [9, NPX]) for p in range(2)]
        gate = sb("gate", [P, NPX])
        x4 = [sb(f"x4{p}", [P, 2, NPX]) for p in range(2)]
        xn = [sb(f"xn{p}", [P, 2, NPX]) for p in range(2)]
        xg = [sb(f"xg{p}", [P, 2, NPX]) for p in range(2)]
        sq = sb("sq", [P, 2, NPX])
        rstd = sb("rstd", [P, 2, NPX])
        raw = [sb(f"raw{p}", [P, 2, ROWS + 2, WW + 2]) for p in range(2)]
        zeros = sb("zeros", [P, WW])
        acc = [sb(f"acc{p}", [P, 2, ROWS, WW]) for p in range(2)]
        sz = [sb(f"sz{p}", [P, 2, NPX]) for p in range(2)]
        u = [sb(f"u{p}", [P, 2, ROWS, WW]) for p in range(2)]
        xd = [sb(f"xd{p}", [NDT + NBC, NPX]) for p in range(2)]

        gate_ps = ps("gate_ps", [P, NPX])
        mean_ps = ps("mean_ps", [P, NPX])
        var_ps = ps("var_ps", [P, NPX])
        xz_ps = [ps(f"xz_ps{t}", [P, NPX]) for t in range(4)]
        xd_ps = ps("xd_ps", [NDT + NBC, NPX])

        w_loaded = sem("w_loaded")
        w_ready = sem("w_ready")
        in_loaded = [sem(f"in_loaded{p}") for p in range(2)]
        x4_stored = [sem(f"x4_stored{p}") for p in range(2)]
        z_stored = [sem(f"z_stored{p}") for p in range(2)]
        u_stored = [sem(f"u_stored{p}") for p in range(2)]
        gate_sum = sem("gate_sum")
        gate_ready = sem("gate_ready")
        gated = sem("gated")
        x4_ready = sem("x4_ready")
        mu_ready = sem("mu_ready")
        xc_ready = sem("xc_ready")
        sq_ready = sem("sq_ready")
        var_ready = sem("var_ready")
        ln_done = sem("ln_done")
        r_ready = sem("r_ready")
        xr_done = sem("xr_done")
        xg_ready = sem("xg_ready")
        xz_ready = sem("xz_ready")
        x_evac = sem("x_evac")
        z_ready = sem("z_ready")
        zero_row_ready = sem("zero_row_ready")
        zeros_ready = sem("zeros_ready")
        carried = sem("carried")
        raw_ready = sem("raw_ready")
        conv_seq = sem("conv_seq")
        u_ready = sem("u_ready")
        xd_ready = sem("xd_ready")
        xd_evac = sem("xd_evac")

        IN_DMAS, U_DMAS = 5, 3
        loads = [(ln_gb, d["ln3_gb"]), (w_in, d["w_in"]), (cw, d["cw"]), (cb, d["cb"]), (w_x, d["w_x"]), (b_sa, d["b_sa"])]
        x2v, yv, x4v, zv, uv = (d[k].rearrange("b (h p) n -> b p h n", h=2) for k in ("x2", "y", "x4", "sz", "u"))

        LATE = 5

        block = ctx.enter_context(nc.Block())

        @block.sync
        def _(sp):
            for dst, src in loads:
                sp.dma_start(dst[:], src).then_inc(w_loaded, DMA)

            def load(k, waits=True):
                b, s, p = k.b, k.s, k.p
                if waits:
                    sp.wait_ge(x4_ready, k.q - 1)
                px = bass.ds(s * NPX, NPX)
                for dy in range(3):
                    view = d["planes"][b, 3 * dy * PLANE:3 * dy * PLANE + 3 * (PLANE + 1)].rearrange("(t n) -> t n", t=3)
                    rows = view[:, bass.ds((s * ROWS + dy) * (WW + 2), ROWS * (WW + 2))]
                    rows = rows.rearrange("t (r c) -> t r c", c=WW + 2)[:, :, 0:WW]
                    sp.dma_start(taps[p][3 * dy:3 * dy + 3, :].rearrange("t (r w) -> t r w", w=WW),
                                 rows).then_inc(in_loaded[p], DMA)
                sp.dma_start(y[p][:], yv[b, :, :, px]).then_inc(in_loaded[p], DMA)
                sp.dma_start(x2[p][:], x2v[b, :, :, px]).then_inc(in_loaded[p], DMA)

            def store_x4(k):
                sp.wait_ge(x4_ready, k.q + 1)
                sp.dma_start(x4v[k.b, :, :, bass.ds(k.s * NPX, NPX)], x4[k.p][:]).then_inc(x4_stored[k.p], DMA)

            def store_z(k):
                sp.wait_ge(z_ready, k.q + 1)
                sp.dma_start(zv[k.b, :, :, bass.ds(k.s * NPX, NPX)], sz[k.p][:]).then_inc(z_stored[k.p], DMA)

            def store_u(k):
                lo, hi = 1 if k.is_first else 0, 1 if k.is_last else ROWS
                b, p = k.b, k.p
                sp.wait_ge(u_ready, k.c + 1)
                px = bass.ds(k.s * NPX + (lo - 1) * WW, (hi - lo) * WW)
                own = slice(lo * WW, hi * WW)
                sp.dma_start(uv[b, :, :, px], u[p][:, :, lo:hi, :].rearrange("p h r w -> p h (r w)")).then_inc(u_stored[p], DMA)
                sp.wait_ge(xd_evac, k.c + 1)
                sp.dma_start(d["dts"][:, b, :, px], xd[p][0:NDT, own]).then_inc(u_stored[p], DMA)
                sp.dma_start(d["bc"][:, b, :, px], xd[p][NDT:NDT + NBC, own]).then_inc(u_stored[p], DMA)

            def step(k, following=None):
                if k.is_real:
                    store_x4(k)
                    if following:
                        load(following)
                if k.back(2).is_real:
                    store_z(k.back(2))
                if k.back(4).is_convolved:
                    store_u(k.back(4))

            def image(b, more):
                for i in range(6):
                    step(Chunk(b, 0, i), Chunk(b, 0, i + 2))
                with sp.Fori(3, CHUNKS // 2 - 1) as j:
                    step(Chunk(b, j, 0), Chunk(b, j, 2))
                    step(Chunk(b, j, 1), Chunk(b, j, 3))
                for i in range(2):
                    step(Chunk(b, 0, CHUNKS - 2 + i), Chunk(b + 1, 0, i) if more else None)
                for i in range(LATE):
                    step(Chunk(b, 0, CHUNKS + i))

            for i in range(2):
                load(Chunk(0, 0, i), waits=False)
            with sp.Fori(0, B - 1) as b:
                image(b, True)
            image(B - 1, False)
            for p in range(2):
                sp.wait_ge(x4_stored[p], DMA * B * CHUNKS // 2)
                sp.wait_ge(z_stored[p], DMA * B * CHUNKS // 2)
                sp.wait_ge(u_stored[p], DMA * U_DMAS * B * (CHUNKS // 2 + 1 - p))

        @block.gpsimd
        def _(pool):
            nc.gpsimd.memset(mean_w[:], 1.0 / C)
            nc.gpsimd.memset(ones[:], 1.0)
            nc.gpsimd.memset(consts[:, 0:1], LN_EPS)
            nc.gpsimd.memset(consts[:, 1:2], 0.0)
            nc.gpsimd.memset(zeros[:], 0.0).then_inc(zero_row_ready, 1)
            for p in range(2):
                nc.gpsimd.memset(raw[p][:, :, :, 0:1], 0.0)
                last = nc.gpsimd.memset(raw[p][:, :, :, WW + 1:WW + 2], 0.0)
            last.then_inc(w_ready, 1)

            def clear(rows):
                z = zeros[:, None, None, :].to_broadcast(rows.shape)
                nc.gpsimd.tensor_tensor(rows, z, z, ALU.add).then_inc(zeros_ready, 1)

            def step(k):
                if k.is_convolved and k.is_last:
                    pool.wait_ge(conv_seq, k.back(1).c * 18)
                    clear(raw[0][:, :, 2:3, 1:WW + 1])
                    return
                if k.is_first:
                    pool.wait_ge(zero_row_ready, 1)
                    pool.wait_ge(conv_seq, k.c * 18)
                    clear(raw[0][:, :, 0:2, 1:WW + 1])
                pool.wait_ge(gate_ready, k.q + 1)
                pool.wait_ge(in_loaded[k.p], (k.pairs + 1) * IN_DMAS * DMA)
                g = gate[:].unsqueeze(1).broadcast_to([P, 2, NPX])
                nc.gpsimd.tensor_tensor(y[k.p][:], y[k.p][:], g, ALU.mult).then_inc(gated, 1)
                pool.wait_ge(x4_stored[k.p], k.pairs * DMA)
                pool.wait_ge(gated, k.q + 1)
                nc.gpsimd.tensor_tensor(x4[k.p][:], x2[k.p][:], y[k.p][:], ALU.add).then_inc(x4_ready, 1)

            image_loop(pool, step, 1)

        @block.vector
        def _(dve):
            dve.wait_ge(w_loaded, DMA * len(loads))
            dve.wait_ge(w_ready, 1)

            def conv(k, lo, hi):
                if lo == 0:
                    dve.wait_ge(raw_ready, k.c + 1)
                    dve.wait_ge(u_ready, k.c - 1) if not k.is_first else dve.wait_ge(u_ready, k.c)
                for i in range(lo, hi):
                    (dy, dx), h, t = TAPS[i // 2], i % 2, i // 2
                    window = raw[k.p][:, h, dy:dy + ROWS, dx:dx + WW]
                    w = cw[:, h, t:t + 1]
                    if t == 0:
                        ins = nc.vector.tensor_scalar(acc[k.p][:, h], window, w, None, ALU.mult)
                    else:
                        dve.wait_ge(conv_seq, k.c * 18 + i - 1)
                        ins = nc.vector.scalar_tensor_tensor(acc[k.p][:, h], window, w, acc[k.p][:, h], ALU.mult, ALU.add)
                    ins.then_inc(conv_seq, 1)

            def center(k):
                dve.wait_ge(mu_ready, k.q + 1)
                dve.wait_ge(x4_ready, k.q + 1)
                dve.wait_ge(xg_ready, k.q)
                mu = mean_ps[:].unsqueeze(1).broadcast_to([P, 2, NPX])
                nc.vector.tensor_tensor(xn[k.p][:], x4[k.p][:], mu, ALU.subtract).then_inc(xc_ready, 1)

            def normalize(k):
                dve.wait_ge(r_ready, k.q + 1)
                dve.wait_ge(xc_ready, k.q + 1)
                r = rstd[:, 1:2, :].broadcast_to([P, 2, NPX])
                nc.vector.tensor_tensor(xn[k.p][:], xn[k.p][:], r, ALU.mult).then_inc(xr_done, 1)
                dve.wait_ge(xr_done, k.q + 1)
                if k.is_first:
                    dve.wait_ge(xz_ready, k.q * 4)
                else:
                    dve.wait_ge(xz_ready, k.q * 4 - 4)
                for h in range(2):
                    last = nc.vector.tensor_scalar(xg[k.p][:, h], xn[k.p][:, h], ln_gb[:, h, 0:1], ln_gb[:, h, 1:2],
                                                   ALU.mult, ALU.add)
                last.then_inc(xg_ready, 1)

            def step(k):
                now, older = k.back(1), k.back(3)
                if now.is_real:
                    center(now)
                if older.is_convolved:
                    conv(older, 0, 16)
                if now.is_real:
                    normalize(now)
                if older.is_convolved:
                    conv(older, 16, 18)

            image_loop(dve, step, LATE - 1)

        @block.scalar
        def _(act):
            act.wait_ge(w_ready, 1)
            act.wait_ge(w_loaded, DMA * len(loads))

            def square(k):
                act.wait_ge(xc_ready, k.q + 1)
                act.wait_ge(var_ready, k.q)
                nc.scalar.activation(sq[:], xn[k.p][:], ACT.Square).then_inc(sq_ready, 1)

            def gate_of(k):
                nc.scalar.preload_act_table_set("sigmoid_and_others")
                act.wait_ge(gate_sum, k.q + 1)
                act.wait_ge(gated, k.q)
                nc.scalar.activation(gate[:], gate_ps[:], ACT.Sigmoid, bias=b_sa[:]).then_inc(gate_ready, 1)

            def deviation(k):
                nc.scalar.preload_act_table_set("natural_log_exp_and_others")
                act.wait_ge(var_ready, k.q + 1)
                act.wait_ge(xr_done, k.q)
                nc.scalar.activation(rstd[:, 0], var_ps[:], ACT.Ln, bias=consts[:, 0:1]).then_inc(ln_done, 1)
                act.wait_ge(ln_done, k.q + 1)
                nc.scalar.activation(rstd[:, 1], rstd[:, 0], ACT.Exp, scale=-0.5, bias=consts[:, 1:2]).then_inc(r_ready, 1)

            def rows_above(k):
                if k.is_first:
                    act.wait_ge(zeros_ready, k.b * 2 + 1)
                    return
                act.wait_ge(conv_seq, k.back(1).c * 18)
                act.wait_ge(raw_ready, k.c)
                nc.scalar.copy(raw[k.p][:, :, 0:2, 1:WW + 1],
                               raw[1 - k.p][:, :, ROWS:ROWS + 2, 1:WW + 1]).then_inc(carried, 1)
                if k.is_last:
                    act.wait_ge(zeros_ready, k.b * 2 + 2)
                    act.wait_ge(carried, (k.b + 1) * CHUNKS)
                    act.sem_inc(raw_ready, 1)

            def take_x(k):
                for t in range(2):
                    act.wait_ge(xz_ready, k.q * 4 + t + 1)
                    nc.scalar.copy(raw[k.p][:, t, 2:ROWS + 2, 1:WW + 1],
                                   xz_ps[t][:].rearrange("p (r w) -> p r w", w=WW)).then_inc(x_evac, 1)
                act.wait_ge(x_evac, k.q * 2 + 2)
                act.sem_inc(raw_ready, 1)

            def silu_u(k):
                act.wait_ge(conv_seq, k.c * 18 + 18)
                act.wait_ge(u_stored[k.p], k.c_pairs * U_DMAS * DMA)
                for h in range(2):
                    last = nc.scalar.activation(u[k.p][:, h], acc[k.p][:, h], ACT.Silu, bias=cb[:, h:h + 1])
                last.then_inc(u_ready, 1)

            def silu_z(k):
                act.wait_ge(z_stored[k.p], k.pairs * DMA)
                for t in range(2):
                    act.wait_ge(xz_ready, k.q * 4 + t + 3)
                    last = nc.scalar.activation(sz[k.p][:, t], xz_ps[2 + t][:], ACT.Silu, bias=consts[:, 1:2])
                last.then_inc(z_ready, 1)

            def take_xd(k):
                act.wait_ge(xd_ready, k.c + 1)
                act.wait_ge(u_stored[k.p], k.c_pairs * U_DMAS * DMA)
                nc.scalar.copy(xd[k.p][:], xd_ps[:]).then_inc(xd_evac, 1)

            def step(k):
                if k.back(1).is_real:
                    square(k.back(1))
                if k.back(2).is_convolved:
                    rows_above(k.back(2))
                if k.back(2).is_real:
                    take_x(k.back(2))
                if k.is_real:
                    gate_of(k)
                if k.back(1).is_real:
                    deviation(k.back(1))
                if k.back(4).is_convolved or k.back(2).is_real:
                    nc.scalar.preload_act_table_set("silu_and_others")
                if k.back(4).is_convolved:
                    silu_u(k.back(4))
                if k.back(2).is_real:
                    silu_z(k.back(2))
                if k.back(4).is_convolved:
                    take_xd(k.back(4))

            image_loop(act, step, LATE)

        @block.tensor
        def _(pe):
            pe.wait_ge(w_ready, 1)
            pe.wait_ge(w_loaded, DMA * len(loads))

            def project(k, outs):
                pe.wait_ge(xg_ready, k.q + 1)
                for t in outs:
                    if t == 0:
                        pe.wait_ge(x_evac, k.q * 2)
                    if t == 2:
                        pe.wait_ge(z_ready, k.q)
                    for h in range(2):
                        last = nc.tensor.matmul(xz_ps[t][:], w_in[:, h, P * t:P * t + P], xg[k.p][:, h],
                                                start=(h == 0), stop=(h == 1))
                    last.then_inc(xz_ready, 1)

            def sum_taps(k):
                pe.wait_ge(in_loaded[k.p], (k.pairs + 1) * IN_DMAS * DMA)
                pe.wait_ge(gate_ready, k.q)
                nc.tensor.matmul(gate_ps[:], ones[:], taps[k.p][:], start=True, stop=True).then_inc(gate_sum, 1)

            def mean(k):
                pe.wait_ge(x4_ready, k.q + 1)
                pe.wait_ge(xc_ready, k.q)
                for h in range(2):
                    last = nc.tensor.matmul(mean_ps[:], mean_w[:], x4[k.p][:, h], start=(h == 0), stop=(h == 1))
                last.then_inc(mu_ready, 1)

            def variance(k):
                pe.wait_ge(sq_ready, k.q + 1)
                pe.wait_ge(r_ready, k.q)
                for h in range(2):
                    last = nc.tensor.matmul(var_ps[:], mean_w[:], sq[:, h], start=(h == 0), stop=(h == 1))
                last.then_inc(var_ready, 1)

            def x_proj(k):
                pe.wait_ge(u_ready, k.c + 1)
                pe.wait_ge(xd_evac, k.c)
                for h in range(2):
                    last = nc.tensor.matmul(xd_ps[:], w_x[:, h], u[k.p][:, h].rearrange("p r w -> p (r w)"),
                                            start=(h == 0), stop=(h == 1))
                last.then_inc(xd_ready, 1)

            def step(k):
                if k.back(2).is_real:
                    project(k.back(2), (0, 1))
                if k.is_real:
                    sum_taps(k)
                if k.back(1).is_real:
                    variance(k.back(1))
                if k.back(2).is_real:
                    project(k.back(2), (2, 3))
                if k.is_real:
                    mean(k)
                if k.back(4).is_convolved:
                    x_proj(k.back(4))

            image_loop(pe, step, LATE)


SPLIT = 1024
PAIRS = B // 2


def split_and_turn(nc, d):
    with ExitStack() as ctx:
        def sb(name, shape, dt=FP32):
            return ctx.enter_context(nc.sbuf_tensor("t_" + name, shape, dt))

        sems = []
        ctx.callback(nc.all_engine_barrier)
        ctx.callback(nc.clear_and_free_semaphores, sems)

        def sem(name):
            sems.append(nc.alloc_semaphore("t_" + name))
            return sems[-1]

        rows = sb("rows", [128, L])
        dts = sb("dts", [2 * B * RANK, L])
        flat = [sb(f"flat{p}", [128, SPLIT]) for p in range(2)]
        rest = [sb(f"rest{p}", [128, SPLIT]) for p in range(2)]
        parts = [sb(f"parts{p}", [128, 3, SPLIT], BF16) for p in range(2)]
        dtt = [sb(f"dtt{p}", [2 * B * RANK, SPLIT]) for p in range(2)]

        loaded = sem("loaded")
        dt_loaded = sem("dt_loaded")
        by_row = [sem(f"by_row{p}") for p in range(2)]
        by_col = [sem(f"by_col{p}") for p in range(2)]
        high = [sem(f"high{p}") for p in range(2)]
        rested = [sem(f"rested{p}") for p in range(2)]
        middle = [sem(f"middle{p}") for p in range(2)]
        low = [sem(f"low{p}") for p in range(2)]
        turned = [sem(f"turned{p}") for p in range(2)]
        stored = [sem(f"stored{p}") for p in range(2)]
        dt_stored = [sem(f"dt_stored{p}") for p in range(2)]
        STORES = 12
        COLS = SPLIT // HH
        by_order = d["bc"].rearrange("(e g) b r n -> g e (b r) n", g=2)
        dt_order = d["dts"].rearrange("(e g) b r n -> g e (b r) n", g=2)[1]
        turn = lambda x: x.rearrange("p (h w) -> p w h", w=WW)

        block = ctx.enter_context(nc.Block())

        def steps(eng, step):
            with eng.Fori(0, L // SPLIT // 2) as j:
                step(2 * j, 0, j)
                step(2 * j + 1, 1, j)

        @block.sync
        def _(sp):
            for g in range(2):
                for e in range(2):
                    at = 64 * g + 32 * e
                    sp.dma_start(rows[at:at + 32, :], by_order[g, e]).then_inc(loaded, DMA)
            for e in range(2):
                at = B * RANK * e
                sp.dma_start(dts[at:at + B * RANK, :], dt_order[e]).then_inc(dt_loaded, DMA)

            def step(n, p, j):
                px = bass.ds(n * SPLIT, SPLIT)
                sp.wait_ge(low[p], j + 1)
                sp.wait_ge(middle[p], j + 1)
                sp.wait_ge(high[p], j + 1)
                for g in range(2):
                    for e in range(2):
                        at = 64 * g + 32 * e
                        for k in range(3):
                            dst = d["bcs"][2 * e + g].rearrange("q (k r) n -> k q r n", k=3)[k]
                            sp.dma_start(dst[:, :, px], parts[p][at:at + 32, k, :]).then_inc(stored[p], DMA)
                sp.wait_ge(turned[p], j + 1)
                for e in range(2):
                    at = B * RANK * e
                    sp.dma_start(dt_order[e][:, px], dtt[p][at:at + B * RANK, :]).then_inc(dt_stored[p], DMA)

            steps(sp, step)
            for p in range(2):
                sp.wait_ge(stored[p], L // SPLIT // 2 * STORES * DMA)
                sp.wait_ge(dt_stored[p], L // SPLIT // 2 * 2 * DMA)

        @block.gpsimd
        def _(pool):
            pool.wait_ge(dt_loaded, 2 * DMA)

            def step(n, p, j):
                pool.wait_ge(dt_stored[p], j * 2 * DMA)
                out = dtt[p][:].rearrange("p (w h) -> p w h", h=HH)
                nc.gpsimd.tensor_copy(out, turn(dts[:])[:, bass.ds(n * COLS, COLS), :]).then_inc(turned[p], 1)

            steps(pool, step)

        @block.scalar
        def _(act):
            act.wait_ge(loaded, 4 * DMA)

            def step(n, p, j):
                act.wait_ge(rested[p], j)
                nc.scalar.copy(flat[p][0:64, :], rows[0:64, bass.ds(n * SPLIT, SPLIT)]).then_inc(by_row[p], 1)
                act.wait_ge(rested[p], j + 1)
                act.wait_ge(stored[p], j * STORES * DMA)
                nc.scalar.copy(parts[p][:, 1, :], rest[p][:]).then_inc(middle[p], 1)

            steps(act, step)

        @block.vector
        def _(dve):
            dve.wait_ge(loaded, 4 * DMA)

            def step(n, p, j):
                dve.wait_ge(rested[p], j)
                nc.vector.tensor_copy(flat[p][64:128, :].rearrange("p (w h) -> p w h", h=HH),
                                      turn(rows[64:128, :])[:, bass.ds(n * COLS, COLS), :]).then_inc(by_col[p], 1)
                dve.wait_ge(by_row[p], j + 1)
                dve.wait_ge(by_col[p], j + 1)
                dve.wait_ge(stored[p], j * STORES * DMA)
                nc.vector.tensor_copy(parts[p][:, 0, :], flat[p][:]).then_inc(high[p], 1)
                dve.wait_ge(high[p], j + 1)
                dve.wait_ge(low[p], j)
                dve.wait_ge(middle[p], j)
                nc.vector.tensor_tensor(rest[p][:], flat[p][:], parts[p][:, 0, :], ALU.subtract).then_inc(rested[p], 1)
                dve.wait_ge(middle[p], j + 1)
                dve.wait_ge(rested[p], j + 1)
                nc.vector.tensor_tensor(parts[p][:, 2, :], rest[p][:], parts[p][:, 1, :], ALU.subtract).then_inc(low[p], 1)

            steps(dve, step)


UNIT = 512
UNITS = L // UNIT
GROUPS = UNITS // 4
TILES = B * C // 128
ORDER = [(0, False, False), (1, True, False), (3, True, True), (2, False, True)]
EXP_CAP = 2.0 ** 63
LOG_MAX = 88.72283
TINY = 2.0 ** -22
RATE_MAX = 2.0 ** 120
DT_MIN = 2.0 ** -113


def selective_scans(nc, d):
    with ExitStack() as ctx:
        def sb(name, shape, dt=FP32):
            return ctx.enter_context(nc.sbuf_tensor("d_" + name, shape, dt))

        def ps(name, shape):
            return ctx.enter_context(nc.psum_tensor("d_" + name, shape, FP32))

        sems = []
        ctx.callback(nc.all_engine_barrier)
        ctx.callback(nc.clear_and_free_semaphores, sems)

        def sem(name):
            sems.append(nc.alloc_semaphore("d_" + name))
            return sems[-1]

        def two(name):
            return [sem(f"{name}{p}") for p in range(2)]

        u = sb("u", [128, L])
        y = sb("y", [128, L])
        ident = sb("ident", [128, 128])
        sel = sb("sel", [6 * 2 * STATES, 2 * STATES, 128], BF16)
        w_dt = sb("w_dt", [2 * RANK, DIRS, 128])
        dt_bias = sb("dt_bias", [128, DIRS])
        a_log = sb("a_log", [128, DIRS * STATES])
        a = sb("a", [128, DIRS * STATES])
        skip = sb("skip", [128, DIRS])
        skip_sum = sb("skip_sum", [128, 1])
        zero = sb("zero", [128, 2])
        dts = [sb(f"dts{h}", [2 * RANK, 2 * UNIT]) for h in range(2)]
        bcs = [sb(f"bcs{h}", [6 * 2 * STATES, 2 * UNIT], BF16) for h in range(2)]
        ex = [sb(f"ex{p}", [128, UNIT]) for p in range(2)]
        dt = [sb(f"dt{p}", [128, UNIT]) for p in range(2)]
        du = [sb(f"du{p}", [128, UNIT]) for p in range(2)]
        da = [sb(f"da{p}", [128, STATES, UNIT]) for p in range(2)]
        h = [sb(f"h{p}", [128, STATES, UNIT]) for p in range(2)]
        cs = sb("cs", [128, STATES, UNIT])
        hc = sb("hc", [128, STATES, UNIT])
        sel32 = hc[0:6 * 2 * STATES, 0:2].rearrange("p a (b c) -> p (a b) c", c=128)

        raw_ps = ps("raw_ps", [128, UNIT])
        b_ps = [ps(f"b_ps{n}", [128, UNIT]) for n in range(STATES)]
        c_ps = [ps(f"c_ps{p}", [128, UNIT]) for p in range(2)]
        y_ps = ps("y_ps", [128, UNIT])

        const_ready = sem("const_ready")
        ident_loaded = sem("ident_loaded")
        w_loaded = sem("w_loaded")
        u_begun = sem("u_begun")
        u_loaded = sem("u_loaded")
        a_capped = sem("a_capped")
        sel_ready = sem("sel_ready")
        a_exp = sem("a_exp")
        a_ready = sem("a_ready")
        y_stored = sem("y_stored")
        xd_loaded = two("xd_loaded")
        raw_ready = two("raw_ready")
        e_ready = two("e_ready")
        clipped = two("clipped")
        ln_ready = two("ln_ready")
        dt_max = two("dt_max")
        dt_ready = two("dt_ready")
        du_ready = two("du_ready")
        da_ready = two("da_ready")
        b_ready = two("b_ready")
        dbu_ready = two("dbu_ready")
        scanned = two("scanned")
        c_ready = two("c_ready")
        cs_ready = two("cs_ready")
        hc_ready = two("hc_ready")
        y_summed = two("y_summed")
        y_added = two("y_added")

        W_DMAS, HALF, U_CUT = 5, UNITS // 2, L // 4
        uv = d["u"].rearrange("b c n -> (b c) n")
        yv = d["ys"].rearrange("b c n -> (b c) n")

        class Unit:

            def __init__(self, t, o, j, i):
                self.t, self.o, self.j, self.i, self.p = t, o, j, i, i % 2
                self.first = isinstance(j, int) and j == 0 and i == 0
                self.direction, self.columns, self.reverse = ORDER[o]
                self.n = (t * len(ORDER) + o) * HALF + j * 2 + i // 2
                self.k = j * -4 + (UNITS - 1 - i) if self.reverse else j * 4 + i
                self.groups = (t * len(ORDER) + o) * GROUPS + j
                self.very_first = self.first and o == 0

            def loaded(self, x):
                at = (1 - self.p if self.reverse else self.p) * UNIT
                return x[self.i // 2][:, at:at + UNIT]

            def states(self, k):
                return self.n * STATES + k

            def before(self, k):
                if self.very_first:
                    return self.n * STATES
                return self.n * STATES + (k if self.p else k - STATES)

            def where(self, x):
                if self.columns:
                    return x[:].rearrange("p (h w) -> p w h", w=WW)[:, bass.ds(self.k * (UNIT // HH), UNIT // HH), :]
                return x[:, bass.ds(self.k * UNIT, UNIT)]

            def shaped(self, x):
                return x.rearrange("p (w h) -> p w h", h=HH) if self.columns else x

            def run(self, x):
                return x[:, ::-1] if self.reverse else x

        def units(eng, body, start, end):
            with eng.Fori(0, PAIRS) as pair:
                with eng.Fori(0, TILES // PAIRS) as third:
                    t = pair * (TILES // PAIRS) + third
                    start(t, pair, third)
                    last = None
                    for o in range(len(ORDER)):
                        def group(j, before, after):
                            own = [before, *(Unit(t, o, j, i) for i in range(4)), after]
                            for i in range(4):
                                body(*own[i:i + 3])
                            return own[4]

                        group(0, last, Unit(t, o, 1, 0))
                        with eng.Fori(1, GROUPS - 1) as j:
                            group(j, Unit(t, o, j - 1, 3), Unit(t, o, j + 1, 0))
                        last = group(GROUPS - 1, Unit(t, o, GROUPS - 2, 3),
                                     Unit(t, o + 1, 0, 0) if o + 1 < len(ORDER) else None)
                    end(t, last)

        block = ctx.enter_context(nc.Block())

        @block.sync
        def _(sp):
            sp.dma_start(ident[:], d["ident"]).then_inc(ident_loaded, DMA)

            with sp.Fori(0, PAIRS) as pair:
                with sp.Fori(0, TILES // PAIRS) as third:
                    t = pair * (TILES // PAIRS) + third
                    sp.wait_ge(y_added[1], t * len(ORDER) * HALF)
                    sp.wait_ge(y_added[0], t * len(ORDER) * HALF)
                    sp.dma_start(w_dt[:], d["w_dt"][third]).then_inc(w_loaded, DMA)
                    sp.dma_start(dt_bias[:], d["dt_bias"][third]).then_inc(w_loaded, DMA)
                    sp.dma_start(a_log[:], d["a_log"][third]).then_inc(w_loaded, DMA)
                    sp.dma_start(skip[:], d["skip"][third]).then_inc(w_loaded, DMA)
                    sp.dma_start(sel32, d["sel"][third]).then_inc(w_loaded, DMA)
                    sp.dma_start(u[:, 0:U_CUT], uv[bass.ds(t * 128, 128), 0:U_CUT]).then_inc(u_begun, DMA)

                    def store(x):
                        px = bass.ds(x.k * UNIT, UNIT)
                        sp.wait_ge(y_added[x.p], x.n + 1)
                        sp.dma_start(yv[bass.ds(t * 128, 128), px], y[:, px]).then_inc(y_stored, DMA)

                    def load(o, j, half):
                        x = Unit(t, o, j, 2 * half + 1)
                        k = x.k if x.reverse else j * 4 + 2 * half
                        px = bass.ds(k * UNIT, 2 * UNIT)
                        if not (o == 0 and isinstance(j, int) and j == 0):
                            sp.wait_ge(c_ready[1], x.states(0) - STATES)
                        src = d["dts"][x.direction, bass.ds(pair * 2, 2), :, px]
                        sp.dma_start(dts[half][:], src.rearrange("i r n -> (i r) n")).then_inc(xd_loaded[half], DMA)
                        sp.dma_start(bcs[half][:], d["bcs"][x.direction, pair, :, px]).then_inc(xd_loaded[half], DMA)

                    for o in range(len(ORDER)):
                        stores = o == len(ORDER) - 1
                        for half in range(2):
                            load(o, 0, half)
                        if o == 0:
                            for at in range(U_CUT, L, U_CUT):
                                sp.dma_start(u[:, at:at + U_CUT],
                                             uv[bass.ds(t * 128, 128), at:at + U_CUT]).then_inc(u_loaded, DMA)
                        with sp.Fori(1, GROUPS) as j:
                            for half in range(2):
                                load(o, j, half)
                                if stores:
                                    store(Unit(t, o, j - 1, 2 * half))
                                    store(Unit(t, o, j - 1, 2 * half + 1))
                        if stores:
                            for i in range(4):
                                store(Unit(t, o, GROUPS - 1, i))
            sp.wait_ge(y_stored, TILES * UNITS * DMA)

        @block.gpsimd
        def _(pool):
            nc.gpsimd.memset(zero[:, 0:1], 0.0)
            nc.gpsimd.memset(zero[:, 1:2], 1.0).then_inc(const_ready, 1)

            def start(t, pair, third):
                pool.wait_ge(u_begun, (t + 1) * DMA)
                times_u(Unit(t, 0, 0, 0))

            def times_u(x):
                pool.wait_ge(dt_ready[x.p], x.n + 1)
                pool.wait_ge(dbu_ready[x.p], x.states(0))
                nc.gpsimd.tensor_tensor(x.shaped(du[x.p][:]), x.shaped(dt[x.p][:]), x.where(u),
                                        ALU.mult).then_inc(du_ready[x.p], 1)

            def times_c(x, n):
                pool.wait_ge(scanned[x.p], x.states(n + 1))
                pool.wait_ge(cs_ready[x.p], x.states(n + 1))
                pool.wait_ge(y_summed[1 - x.p], x.before(n + 1))
                nc.gpsimd.tensor_tensor(hc[:, n], h[x.p][:, n], cs[:, n], ALU.mult).then_inc(hc_ready[x.p], 1)

            def body(before, x, after):
                times_c(x, 0)
                times_c(x, 1)
                if x.o == 0 and x.i == 3 and isinstance(x.j, int) and x.j == 0:
                    pool.wait_ge(u_loaded, (x.t + 1) * 3 * DMA)
                if after:
                    times_u(after)
                times_c(x, 2)
                times_c(x, 3)

            units(pool, body, start, lambda t, last: None)

        @block.vector
        def _(dve):
            dve.wait_ge(const_ready, 1)

            def clip(x):
                dve.wait_ge(e_ready[x.p], x.n + 1)
                nc.vector.tensor_scalar(ex[x.p][:], ex[x.p][:], EXP_CAP, DT_MIN, ALU.min, ALU.max).then_inc(clipped[x.p], 1)

            def softplus(x):
                dve.wait_ge(ln_ready[x.p], x.n + 1)
                o = x.direction
                nc.vector.scalar_tensor_tensor(dt[x.p][:], raw_ps[:], dt_bias[:, o:o + 1], dt[x.p][:],
                                               ALU.add, ALU.max).then_inc(dt_max[x.p], 1)

            def softplus_tiny(x):
                dve.wait_ge(dt_max[x.p], x.n + 1)
                nc.vector.scalar_tensor_tensor(dt[x.p][:], dt[x.p][:], TINY, ex[x.p][:],
                                               ALU.max, ALU.min).then_inc(dt_ready[x.p], 1)

            def times_b(x, n):
                dve.wait_ge(b_ready[x.p], x.states(n + 1))
                dve.wait_ge(du_ready[x.p], x.n + 1)
                nc.vector.tensor_tensor(b_ps[n][:], b_ps[n][:], du[x.p][:], ALU.mult).then_inc(dbu_ready[x.p], 1)

            def scan(x, n):
                dve.wait_ge(dbu_ready[x.p], x.states(n + 1))
                dve.wait_ge(da_ready[x.p], x.states(n + 1))
                dve.wait_ge(hc_ready[x.p], x.states(0))
                initial = 0.0
                if not x.first:
                    dve.wait_ge(scanned[1 - x.p], x.before(n + 1))
                    end = 0 if x.reverse else UNIT - 1
                    initial = h[1 - x.p][:, n, end:end + 1]
                nc.vector.tensor_tensor_scan(x.run(h[x.p][:, n]), x.run(da[x.p][:, n]), x.run(b_ps[n][:]), initial,
                                             ALU.mult, ALU.add).then_inc(scanned[x.p], 1)

            def add_y(x):
                dve.wait_ge(y_summed[x.p], x.states(STATES))
                at, new = x.where(y), x.shaped(y_ps[:])
                if x.first and x.o:
                    dve.wait_ge(y_added[1], x.n)
                    dve.wait_ge(y_added[0], x.n)
                if x.o == 0:
                    ins = nc.vector.scalar_tensor_tensor(at, x.where(u), skip_sum[:], new, ALU.mult, ALU.add)
                else:
                    ins = nc.vector.tensor_tensor(at, at, new, ALU.add)
                ins.then_inc(y_added[x.p], 1)

            def start(t, pair, third):
                dve.wait_ge(w_loaded, (t + 1) * W_DMAS * DMA)
                dve.wait_ge(u_begun, (t + 1) * DMA)
                dve.wait_ge(y_stored, t * UNITS * DMA)
                nc.vector.tensor_scalar(a_log[:], a_log[:], LOG_MAX, None, ALU.min).then_inc(a_capped, 1)
                nc.vector.tensor_copy(sel[:], sel32).then_inc(sel_ready, 1)
                nc.vector.reduce_sum(skip_sum[:], skip[:], axis=AXX)
                dve.wait_ge(a_exp, t + 1)
                nc.vector.tensor_scalar(a[:], a[:], RATE_MAX, -1.0, ALU.min, ALU.mult).then_inc(a_ready, 1)
                dve.wait_ge(a_ready, t + 1)
                x = Unit(t, 0, 0, 0)
                clip(x)
                softplus(x)
                softplus_tiny(x)

            def body(before, x, after):
                if x.o == 0 and x.i == 3 and isinstance(x.j, int) and x.j == 0:
                    dve.wait_ge(u_loaded, (x.t + 1) * 3 * DMA)
                times_b(x, 0)
                times_b(x, 1)
                scan(x, 0)
                if after:
                    clip(after)
                scan(x, 1)
                times_b(x, 2)
                times_b(x, 3)
                if after:
                    softplus(after)
                if before:
                    add_y(before)
                if after:
                    softplus_tiny(after)
                scan(x, 2)
                scan(x, 3)

            units(dve, body, start, lambda t, last: add_y(last))

        @block.scalar
        def _(act):
            act.wait_ge(const_ready, 1)
            nc.scalar.preload_act_table_set("natural_log_exp_and_others")

            def e_of(x):
                act.wait_ge(raw_ready[x.p], x.n + 1)
                act.wait_ge(dt_ready[x.p], x.n)
                o = x.direction
                nc.scalar.activation(ex[x.p][:], raw_ps[:], ACT.Exp, bias=dt_bias[:, o:o + 1]).then_inc(e_ready[x.p], 1)

            def ln_of(x):
                act.wait_ge(clipped[x.p], x.n + 1)
                act.wait_ge(du_ready[x.p], x.n)
                act.wait_ge(da_ready[x.p], x.states(0))
                nc.scalar.activation(dt[x.p][:], ex[x.p][:], ACT.Ln, bias=zero[:, 1:2]).then_inc(ln_ready[x.p], 1)

            def decay(x, n):
                act.wait_ge(dt_ready[x.p], x.n + 1)
                act.wait_ge(scanned[x.p], x.states(0))
                o = x.direction * STATES + n
                nc.scalar.activation(da[x.p][:, n], dt[x.p][:], ACT.Exp, scale=a[:, o:o + 1],
                                     bias=zero[:, 0:1]).then_inc(da_ready[x.p], 1)

            def copy_c(x, n):
                act.wait_ge(c_ready[x.p], x.states(n + 1))
                act.wait_ge(hc_ready[1 - x.p], x.before(n + 1))
                nc.scalar.copy(cs[:, n], c_ps[n % 2][:]).then_inc(cs_ready[x.p], 1)

            def start(t, pair, third):
                act.wait_ge(w_loaded, (t + 1) * W_DMAS * DMA)
                act.wait_ge(a_capped, t + 1)
                nc.scalar.activation(a[:], a_log[:], ACT.Exp, bias=zero[:, 0:1]).then_inc(a_exp, 1)
                act.wait_ge(a_ready, t + 1)
                x = Unit(t, 0, 0, 0)
                e_of(x)
                ln_of(x)

            def body(before, x, after):
                decay(x, 0)
                decay(x, 1)
                if after:
                    e_of(after)
                copy_c(x, 0)
                if after:
                    ln_of(after)
                copy_c(x, 1)
                decay(x, 2)
                decay(x, 3)
                copy_c(x, 2)
                copy_c(x, 3)

            units(act, body, start, lambda t, last: None)

        @block.tensor
        def _(pe):
            pe.wait_ge(ident_loaded, DMA)

            def raw_dt(x):
                pe.wait_ge(xd_loaded[x.i // 2], (x.groups + 1) * 2 * DMA)
                pe.wait_ge(dt_max[1 - x.p], x.n if x.p == 0 else x.n + 1)
                nc.tensor.matmul(raw_ps[:], w_dt[:, x.direction], x.loaded(dts), start=True,
                                 stop=True).then_inc(raw_ready[x.p], 1)

            def spread_b(x, n):
                pe.wait_ge(scanned[1 - x.p], x.before(n + 1))
                nc.tensor.matmul(b_ps[n][:], sel[:, n], x.loaded(bcs), start=True, stop=True).then_inc(b_ready[x.p], 1)

            def spread_c(x, n):
                if n < 2:
                    pe.wait_ge(cs_ready[1 - x.p], x.before(n + 3))
                else:
                    pe.wait_ge(cs_ready[x.p], x.states(n - 1))
                nc.tensor.matmul(c_ps[n % 2][:], sel[:, STATES + n], x.loaded(bcs), start=True,
                                 stop=True).then_inc(c_ready[x.p], 1)

            def sum_y(x, n):
                if n == 0:
                    pe.wait_ge(y_added[1 - x.p], x.n if x.p == 0 else x.n + 1)
                pe.wait_ge(hc_ready[x.p], x.states(n + 1))
                nc.tensor.matmul(y_ps[:], ident[:], hc[:, n], start=(n == 0),
                                 stop=(n == STATES - 1)).then_inc(y_summed[x.p], 1)

            def start(t, pair, third):
                pe.wait_ge(w_loaded, (t + 1) * W_DMAS * DMA)
                pe.wait_ge(sel_ready, t + 1)
                x = Unit(t, 0, 0, 0)
                raw_dt(x)
                spread_b(x, 0)
                spread_b(x, 1)

            def body(before, x, after):
                if after:
                    raw_dt(after)
                spread_b(x, 2)
                spread_b(x, 3)
                spread_c(x, 0)
                spread_c(x, 1)
                if before:
                    sum_y(before, 2)
                    sum_y(before, 3)
                spread_c(x, 2)
                spread_c(x, 3)
                if after:
                    spread_b(after, 0)
                    spread_b(after, 1)
                sum_y(x, 0)
                sum_y(x, 1)

            def end(t, last):
                sum_y(last, 2)
                sum_y(last, 3)

            units(pe, body, start, end)


def output_projection(nc, d):
    with ExitStack() as ctx:
        def sb(name, shape, dt=FP32):
            return ctx.enter_context(nc.sbuf_tensor("e_" + name, shape, dt))

        def ps(name, shape):
            return ctx.enter_context(nc.psum_tensor("e_" + name, shape, FP32))

        sems = []
        ctx.callback(nc.all_engine_barrier)
        ctx.callback(nc.clear_and_free_semaphores, sems)

        def sem(name):
            sems.append(nc.alloc_semaphore("e_" + name))
            return sems[-1]

        mean_w = sb("mean_w", [P, P])
        ln_gb = sb("ln_gb", [P, 2, 2])
        w_out = sb("w_out", [P, 2, C])
        consts = sb("consts", [P, 2])
        DEEP = 4
        y = [sb(f"y{p}", [P, 2, NPX]) for p in range(DEEP)]
        sz = [sb(f"sz{p}", [P, 2, NPX]) for p in range(DEEP)]
        x4 = [sb(f"x4{p}", [P, 2, NPX]) for p in range(DEEP)]
        yn = [sb(f"yn{p}", [P, 2, NPX]) for p in range(DEEP)]
        yz = [sb(f"yz{p}", [P, 2, NPX]) for p in range(DEEP)]
        out = [sb(f"out{p}", [P, 2, NPX]) for p in range(DEEP)]
        y_sum = sb("y_sum", [P, NPX])
        sq = sb("sq", [P, 2, NPX])
        sq_sum = sb("sq_sum", [P, NPX])
        rstd = sb("rstd", [P, 2, NPX])
        stat_ps = [ps(f"stat_ps{i}", [P, NPX]) for i in range(2)]
        o_ps = [ps(f"o_ps{p}", [P, 2, NPX]) for p in range(2)]

        w_loaded = sem("w_loaded")
        w_ready = sem("w_ready")
        y_loaded = [sem(f"y_loaded{p}") for p in range(DEEP)]
        zx_loaded = [sem(f"zx_loaded{p}") for p in range(DEEP)]
        stored = [sem(f"stored{p}") for p in range(DEEP)]
        y_summed = sem("y_summed")
        sq_summed = sem("sq_summed")
        mu_ready = sem("mu_ready")
        yc_ready = sem("yc_ready")
        sq_ready = sem("sq_ready")
        var_ready = sem("var_ready")
        ln_done = sem("ln_done")
        r_ready = sem("r_ready")
        yr_done = sem("yr_done")
        yz_ready = sem("yz_ready")
        o_ready = sem("o_ready")
        out_ready = sem("out_ready")

        TOTAL = B * CHUNKS
        loads = [(ln_gb, d["ln4_gb"]), (w_out, d["w_out"])]
        yv, zv, x4v, ov = (d[k].rearrange("b (h p) n -> b p h n", h=2) for k in ("ys", "sz", "x4", "out"))

        class Chunk:

            def __init__(self, j, i):
                self.j, self.i, self.p = j, i, i % DEEP
                self.q = DEEP * j + i
                self.turn = j + i // DEEP
                self.is_real = not isinstance(j, int) or 0 <= self.q < TOTAL
                self.is_first = isinstance(j, int) and self.q == 0

            def back(self, k):
                return Chunk(self.j, self.i - k)

        def chunk_loop(eng, step):
            for i in range(DEEP):
                step(Chunk(0, i))
            with eng.Fori(1, TOTAL // DEEP) as j:
                for i in range(DEEP):
                    step(Chunk(j, i))
            for i in range(DEEP):
                step(Chunk(0, TOTAL + i))

        block = ctx.enter_context(nc.Block())

        @block.sync
        def _(sp):
            for dst, src in loads:
                sp.dma_start(dst[:], src).then_inc(w_loaded, DMA)

            def load_y(b, s, p, waits=True):
                if waits:
                    sp.wait_ge(yc_ready, b * CHUNKS + s - DEEP + 1)
                sp.dma_start(y[p][:], yv[b, :, :, bass.ds(s * NPX, NPX)]).then_inc(y_loaded[p], DMA)

            def load_zx(b, s, p):
                px = bass.ds(s * NPX, NPX)
                sp.dma_start(sz[p][:], zv[b, :, :, px]).then_inc(zx_loaded[p], DMA)
                sp.dma_start(x4[p][:], x4v[b, :, :, px]).then_inc(zx_loaded[p], DMA)

            def store(b, s, p):
                sp.wait_ge(out_ready, b * CHUNKS + s + 1)
                sp.dma_start(ov[b, :, :, bass.ds(s * NPX, NPX)], out[p][:]).then_inc(stored[p], DMA)

            def turn(b, j, i, more):
                store(b, j * DEEP + i, i)
                for load, ahead in ((load_zx, DEEP), (load_y, 2 * DEEP - 1)):
                    s, p = j * DEEP + i + ahead, (i + ahead) % DEEP
                    if not isinstance(j, int) or s < CHUNKS:
                        load(b, s, p)
                    elif more:
                        load(b + 1, s - CHUNKS, p)

            def image(b, more):
                with sp.Fori(0, CHUNKS // DEEP - 2) as j:
                    for i in range(DEEP):
                        turn(b, j, i, more)
                for j in (CHUNKS // DEEP - 2, CHUNKS // DEEP - 1):
                    for i in range(DEEP):
                        turn(b, j, i, more)

            for s in range(DEEP):
                load_y(0, s, s, waits=False)
                load_zx(0, s, s)
            for s in range(DEEP, 2 * DEEP - 1):
                load_y(0, s, s - DEEP)
            with sp.Fori(0, B - 1) as b:
                image(b, True)
            image(B - 1, False)
            for p in range(DEEP):
                sp.wait_ge(stored[p], TOTAL // DEEP * DMA)

        @block.gpsimd
        def _(pool):
            nc.gpsimd.memset(mean_w[:], 1.0 / C)
            nc.gpsimd.memset(consts[:, 0:1], LN_EPS)
            nc.gpsimd.memset(consts[:, 1:2], 0.0).then_inc(w_ready, 1)

            def sum_y(k):
                pool.wait_ge(y_loaded[k.p], (k.turn + 1) * DMA)
                pool.wait_ge(mu_ready, k.q)
                nc.gpsimd.tensor_tensor(y_sum[:], y[k.p][:, 0], y[k.p][:, 1], ALU.add).then_inc(y_summed, 1)

            def sum_squares(k):
                pool.wait_ge(sq_ready, k.q + 1)
                pool.wait_ge(var_ready, k.q)
                nc.gpsimd.tensor_tensor(sq_sum[:], sq[:, 0], sq[:, 1], ALU.add).then_inc(sq_summed, 1)

            def step(k):
                if k.is_real:
                    sum_y(k)
                if k.back(1).is_real:
                    sum_squares(k.back(1))

            chunk_loop(pool, step)

        @block.vector
        def _(dve):
            dve.wait_ge(w_loaded, DMA * len(loads))

            def center(k):
                dve.wait_ge(mu_ready, k.q + 1)
                if not (isinstance(k.j, int) and k.q < DEEP):
                    dve.wait_ge(yz_ready, k.q - DEEP + 1)
                mu = stat_ps[0][:].unsqueeze(1).broadcast_to([P, 2, NPX])
                nc.vector.tensor_tensor(yn[k.p][:], y[k.p][:], mu, ALU.subtract).then_inc(yc_ready, 1)

            def scale(k):
                dve.wait_ge(r_ready, k.q + 1)
                dve.wait_ge(yc_ready, k.q + 1)
                for h in range(2):
                    last = nc.vector.scalar_tensor_tensor(yn[k.p][:, h], yn[k.p][:, h], ln_gb[:, h, 0:1],
                                                          rstd[:, 1, :], ALU.mult, ALU.mult)
                last.then_inc(yr_done, 1)

            def add_x4(k):
                dve.wait_ge(o_ready, k.q + 1)
                dve.wait_ge(zx_loaded[k.p], (k.turn + 1) * 2 * DMA)
                dve.wait_ge(stored[k.p], k.turn * DMA)
                nc.vector.tensor_tensor(out[k.p][:], x4[k.p][:], o_ps[k.i % 2][:], ALU.add).then_inc(out_ready, 1)

            def times_z(k):
                dve.wait_ge(yr_done, k.q + 1)
                dve.wait_ge(zx_loaded[k.p], (k.turn + 1) * 2 * DMA)
                if not (isinstance(k.j, int) and k.q < DEEP):
                    dve.wait_ge(o_ready, k.q - DEEP + 2)
                for h in range(2):
                    last = nc.vector.scalar_tensor_tensor(yz[k.p][:, h], yn[k.p][:, h], ln_gb[:, h, 1:2],
                                                          sz[k.p][:, h], ALU.add, ALU.mult)
                last.then_inc(yz_ready, 1)

            def step(k):
                if k.back(1).is_real:
                    center(k.back(1))
                if k.back(2).is_real:
                    scale(k.back(2))
                if k.back(4).is_real:
                    add_x4(k.back(4))
                if k.back(2).is_real:
                    times_z(k.back(2))

            chunk_loop(dve, step)

        @block.scalar
        def _(act):
            act.wait_ge(w_ready, 1)
            nc.scalar.preload_act_table_set("natural_log_exp_and_others")

            def deviation(k):
                act.wait_ge(var_ready, k.q + 1)
                act.wait_ge(yr_done, k.q)
                nc.scalar.activation(rstd[:, 0], stat_ps[1][:], ACT.Ln, bias=consts[:, 0:1]).then_inc(ln_done, 1)
                act.wait_ge(ln_done, k.q + 1)
                nc.scalar.activation(rstd[:, 1], rstd[:, 0], ACT.Exp, scale=-0.5, bias=consts[:, 1:2]).then_inc(r_ready, 1)

            def square(k):
                act.wait_ge(yc_ready, k.q + 1)
                act.wait_ge(sq_summed, k.q)
                nc.scalar.activation(sq[:], yn[k.p][:], ACT.Square).then_inc(sq_ready, 1)

            def step(k):
                if k.back(2).is_real:
                    deviation(k.back(2))
                if k.back(1).is_real:
                    square(k.back(1))

            chunk_loop(act, step)

        @block.tensor
        def _(pe):
            pe.wait_ge(w_ready, 1)
            pe.wait_ge(w_loaded, DMA * len(loads))

            def project(k, o):
                if o == 0:
                    pe.wait_ge(yz_ready, k.q + 1)
                    if not k.is_first:
                        pe.wait_ge(out_ready, k.q - 1)
                for h in range(2):
                    last = nc.tensor.matmul(o_ps[k.i % 2][:, o], w_out[:, h, P * o:P * o + P], yz[k.p][:, h],
                                            start=(h == 0), stop=(h == 1))
                if o == 1:
                    last.then_inc(o_ready, 1)

            def mean(k):
                pe.wait_ge(y_summed, k.q + 1)
                pe.wait_ge(yc_ready, k.q)
                nc.tensor.matmul(stat_ps[0][:], mean_w[:], y_sum[:], start=True, stop=True).then_inc(mu_ready, 1)

            def variance(k):
                pe.wait_ge(sq_summed, k.q + 1)
                pe.wait_ge(r_ready, k.q)
                nc.tensor.matmul(stat_ps[1][:], mean_w[:], sq_sum[:], start=True, stop=True).then_inc(var_ready, 1)

            def step(k):
                if k.back(3).is_real:
                    project(k.back(3), 0)
                if k.is_real:
                    mean(k)
                if k.back(3).is_real:
                    project(k.back(3), 1)
                if k.back(1).is_real:
                    variance(k.back(1))

            chunk_loop(pe, step)


def layout(inputs):
    a = {k: np.asarray(v) for k, v in inputs.items()}
    C, P = 192, 96
    def halves(m):
        return np.ascontiguousarray(m.reshape(2, P, *m.shape[1:]).swapaxes(0, 1))
    out = {}
    out["x"] = a["x"].reshape(4, C, -1)
    out["ident"] = np.eye(128, dtype=np.float32)
    out["ln1_gb"] = halves(np.stack([a["L0_conv_g1"], a["L0_conv_b1"]], -1))
    out["wqkv"] = halves(a["L0_conv_w_qkv"].reshape(576, C).T)
    out["wdw"] = np.ascontiguousarray(a["L0_conv_w_dw"].reshape(6, P, 9).swapaxes(0, 1))
    out["wproj"] = halves(a["L0_conv_w_proj"].reshape(C, C).T)
    out["temp"] = np.ascontiguousarray(np.repeat(a["L0_conv_temp"].reshape(2, 3), 32, 1).T)
    wh = a["L0_conv_w_head"].transpose(1, 3, 2, 0)
    wh = np.repeat(np.repeat(wh, 32, 0), 32, 3)
    out["head_w"] = halves(wh.reshape(C, 9, C))
    c = np.arange(C) % 32
    out["head_mask"] = halves(np.stack([(c[:, None] - c[None, :] + 1 == dy) for dy in range(3)], 1).astype(np.float32))
    out["ln2_gb"] = halves(np.stack([a["L0_conv_g2"], a["L0_conv_b2"]], -1))
    out["w1"] = halves(a["L0_conv_w_fc1"].T)
    out["b1"] = np.ascontiguousarray(a["L0_conv_b_fc1"].reshape(3, 128).T)
    out["w2"] = np.ascontiguousarray(a["L0_conv_w_fc2"].T.reshape(3, 128, C).swapaxes(0, 1))
    out["b2"] = np.ascontiguousarray(a["L0_conv_b_fc2"].reshape(2, P).T)
    out["wsa"] = halves(a["L0_conv_w_sa"].reshape(C, 9))
    out["ln3_gb"] = halves(np.stack([a["L1_conv_ln_w"], a["L1_conv_ln_b"]], -1))
    out["w_in"] = halves(a["L1_conv_in_proj_w"].T)
    out["cw"] = np.ascontiguousarray(a["L1_conv_conv_w"].reshape(2, P, 9).swapaxes(0, 1))
    out["cb"] = np.ascontiguousarray(a["L1_conv_conv_b"].reshape(2, P).T)
    out["b_sa"] = np.repeat(a["L0_conv_b_sa"].reshape(1, 1), P, 0)
    xp = a["L1_conv_x_proj_w"]
    xp = np.concatenate([xp[:, :12].reshape(48, C), xp[:, 12:].reshape(32, C)], 0)
    out["w_x"] = halves(xp.T)
    row = np.arange(384).reshape(3, 128)
    img, ch = row // C, row % C
    w_dt = a["L1_conv_dt_proj_w"][:, ch, :]
    two = np.zeros((3, 2, 12, 4, 128), np.float32)
    for t in range(3):
        for i in range(2):
            two[t, i][:, :, img[t] == i] = w_dt[:, t][:, img[t] == i].transpose(2, 0, 1)
    out["w_dt"] = two.reshape(3, 24, 4, 128)
    out["dt_bias"] = np.ascontiguousarray(a["L1_conv_dt_proj_b"][:, ch].transpose(1, 2, 0))
    out["a_log"] = np.ascontiguousarray(a["L1_conv_A_log"][:, ch].transpose(1, 2, 0, 3).reshape(3, 128, 16))
    out["skip"] = np.ascontiguousarray(a["L1_conv_Ds"][:, ch].transpose(1, 2, 0))
    sel = np.zeros((3, 3, 2, 8, 8, 128), np.float32)
    for t in range(3):
        for i in range(2):
            for r in range(8):
                sel[t, :, i, r, r, img[t] == i] = 1
    out["sel"] = sel.reshape(3, 48, 8, 128)
    out["ln4_gb"] = halves(np.stack([a["L1_conv_out_norm_w"], a["L1_conv_out_norm_b"]], -1))
    out["w_out"] = halves(a["L1_conv_out_proj_w"].T)
    return out


def build(nc, arrays):
    d = {}
    for name, array in arrays.items():
        d[name] = nc.dram_tensor("in_" + name, array.shape, mybir.dt.from_np(array.dtype), kind="ExternalInput").ap()
    image = [B, C, L]
    for name, shape, dt in (("x1", image, FP32), ("v", image, FP32), ("mt", [B, P, 2, C], FP32), ("x2", image, FP32),
                            ("y", image, FP32), ("planes", [B, 9 * PLANE + 3], FP32), ("x4", image, FP32),
                            ("sz", image, FP32), ("u", image, FP32), ("dts", [DIRS, B, RANK, L], FP32),
                            ("bc", [DIRS, B, 2 * STATES, L], FP32),
                            ("bcs", [DIRS, PAIRS, 6 * 2 * STATES, L], BF16), ("ys", image, FP32)):
        d[name] = nc.dram_tensor(name, shape, dt, kind="Internal").ap()
    d["out"] = nc.dram_tensor("out", image, FP32, kind="ExternalOutput").ap()
    attention_statistics(nc, d)
    attention_and_mlp(nc, d)
    gate_and_scan_inputs(nc, d)
    split_and_turn(nc, d)
    selective_scans(nc, d)
    output_projection(nc, d)


def kernel(**inputs):
    import concourse.bacc as bacc
    from concourse.bass_utils import run_bass_kernel_spmd

    arrays = layout(inputs)
    nc = bacc.Bacc("TRN2", target_bir_lowering=False, num_devices=1)
    build(nc, arrays)
    r = run_bass_kernel_spmd(nc, [{"in_" + k: v for k, v in arrays.items()}], core_ids=[0])
    return r.results[0]["out"].reshape(B, C, HH, WW)
```

```python
import concourse.bass as bass
from concourse import mybir
from contextlib import ExitStack
import numpy as np

FP32 = mybir.dt.float32
BF16 = mybir.dt.bfloat16
ALU = mybir.AluOpType
ACT = mybir.ActivationFunctionType
AXX = mybir.AxisListType.X

B, C, HH, WW = 4, 192, 128, 128
L = HH * WW
P = 96
ROWS = 4
NPX = ROWS * WW
CHUNKS = HH // ROWS
HEADS, HD = 6, 32
HID = 384
TAPS = [(dy, dx) for dy in range(3) for dx in range(3)]
PLANE = (HH + 2) * (WW + 2)
LN_EPS = 1e-5
DMA = 16


class Chunk:

    def __init__(self, b, j, i):
        self.b, self.j, self.i, self.p = b, j, i, i % 2
        self.s = 2 * j + i
        self.half = j + i // 2
        self.q = b * CHUNKS + self.s
        self.pairs = b * (CHUNKS // 2) + self.half
        self.c = b * (CHUNKS + 1) + self.s
        self.c_pairs = b * (CHUNKS // 2 + 1 - self.p) + self.half
        known = isinstance(j, int)
        self.is_first = known and self.s == 0
        self.is_real = not known or 0 <= self.s < CHUNKS
        self.is_last = known and self.s == CHUNKS
        self.is_convolved = self.is_real or self.is_last

    def back(self, k):
        return Chunk(self.b, self.j, self.i - k)


def image_loop(eng, step, more=0, start=None, end=None, out=0):
    with eng.Fori(0, B) as b:
        if start:
            start(b)
        for i in range(4):
            step(Chunk(b, 0, i))
        with eng.Fori(2, (CHUNKS - out) // 2) as j:
            step(Chunk(b, j, 0))
            step(Chunk(b, j, 1))
        for i in range(CHUNKS - out, CHUNKS + more):
            step(Chunk(b, 0, i))
        if end:
            end(b)


def attention_statistics(nc, d):
    with ExitStack() as ctx:
        def sb(name, shape, dt=FP32):
            return ctx.enter_context(nc.sbuf_tensor("a_" + name, shape, dt))

        def ps(name, shape):
            return ctx.enter_context(nc.psum_tensor("a_" + name, shape, FP32))

        sems = []
        ctx.callback(nc.all_engine_barrier)
        ctx.callback(nc.clear_and_free_semaphores, sems)

        def sem(name):
            sems.append(nc.alloc_semaphore("a_" + name))
            return sems[-1]

        PRODS = 6
        mean_w = sb("mean_w", [P, P])
        ones = sb("ones", [P, P])
        ident = sb("ident", [P, P])
        ln_gb = sb("ln_gb", [P, 2, 2])
        wqkv = sb("wqkv", [P, 2, 3 * C])
        wdw = sb("wdw", [P, 6, 9])
        qdiag = sb("qdiag", [P, 9, P])
        wproj = sb("wproj", [P, 2, C])
        temp = sb("temp", [P, 2])
        head_w = sb("head_w", [P, 2, 9, C])
        head_mask = sb("head_mask", [P, 2, 3, C])
        head_conv = sb("head_conv", [P, 2, 3, C])
        consts = sb("consts", [P, 2])
        x_sum = sb("x_sum", [P, NPX])
        sq_sum = sb("sq_sum", [P, NPX])
        x_in = [sb(f"x_in{p}", [P, 2, NPX]) for p in range(2)]
        xc = [sb(f"xc{p}", [P, 2, NPX]) for p in range(2)]
        sq = sb("sq", [P, 2, NPX])
        rstd = sb("rstd", [P, 2, NPX])
        x1 = [sb(f"x1{p}", [P, 2, NPX]) for p in range(2)]
        raw = [sb(f"raw{p}", [P, 6, ROWS + 2, WW + 2]) for p in range(2)]
        zeros = sb("zeros", [P, WW])
        prod = [sb(f"prod{i}", [P, ROWS, WW]) for i in range(PRODS)]
        qc = sb("qc", [P, ROWS, WW])
        kc = sb("kc", [P, 2, ROWS, WW])
        vc = [sb(f"vc{p}", [P, 2, ROWS, WW]) for p in range(2)]
        qkt = sb("qkt", [128, ROWS, 2, 2, P])
        gs = sb("gs", [P, 2, HD])
        dq = sb("dq", [P, 2, P])
        dk = sb("dk", [P, 2, P])
        nq = sb("nq", [P, 2])
        nk = sb("nk", [P, 2, HD])
        nqs = sb("nqs", [P, 2])
        nks = sb("nks", [P, 2, HD])
        s_pad = sb("s_pad", [P, 2, HD + 2])
        mx = sb("mx", [P, 2])
        ex = sb("ex", [P, 2, HD])
        sm = sb("sm", [P, 2])
        attn_bd = sb("attn_bd", [P, 2, P])
        mt = sb("mt", [P, 2, C])

        stat_ps = ps("stat_ps", [P, NPX])
        kt_ps = ps("kt_ps", [128, 2, 2, P])
        qkv_ps = [ps(f"qkv_ps{p}", [P, NPX]) for p in range(2)]
        qt_ps = [ps(f"qt_ps{p}", [128, 2, 2, P]) for p in range(2)]
        gram_ps = ps("gram_ps", [P, 2, 512])
        nk_ps = stat_ps[:, 0:2 * P].rearrange("p (h d) -> p h d", h=2)
        conv_ps = kt_ps[0:P, 0, 0, 0:2 * HD].rearrange("p (h d) -> p h d", h=2)
        mt_ps = qkv_ps[0][:, 0:2 * C].rearrange("p (h d) -> p h d", h=2)

        w_loaded = sem("w_loaded")
        w_ready = sem("w_ready")
        v_prep = sem("v_prep")
        x_loaded = [sem(f"x_loaded{p}") for p in range(2)]
        x1_stored = [sem(f"x1_stored{p}") for p in range(2)]
        v_stored = [sem(f"v_stored{p}") for p in range(2)]
        mt_stored = sem("mt_stored")
        img_done = sem("img_done")
        x_summed = sem("x_summed")
        sq_summed = sem("sq_summed")
        mu_ready = sem("mu_ready")
        xc_ready = sem("xc_ready")
        sq_ready = sem("sq_ready")
        var_ready = sem("var_ready")
        ln_done = sem("ln_done")
        r_ready = sem("r_ready")
        xr_done = sem("xr_done")
        x1_ready = sem("x1_ready")
        qkv_ready = sem("qkv_ready")
        qkv_evac = sem("qkv_evac")
        zero_row_ready = sem("zero_row_ready")
        zeros_ready = sem("zeros_ready")
        carried = sem("carried")
        raw_ready = sem("raw_ready")
        conv_seq = sem("conv_seq")
        prod_ready = sem("prod_ready")
        add_seq = sem("add_seq")
        qt_ready = sem("qt_ready")
        qt_evac = sem("qt_evac")
        kt_ready = sem("kt_ready")
        kt_evac = sem("kt_evac")
        gram_done = sem("gram_done")
        fin_v = sem("fin_v")
        fin_s = sem("fin_s")
        fin_t = sem("fin_t")
        FIN_V, FIN_S, FIN_T = 15, 2, 3
        VTAPS, PTAPS, PSUMS = 27, 18, 16

        loads = [(ident, d["ident"][0:P, 0:P]), (ln_gb, d["ln1_gb"]), (wqkv, d["wqkv"]), (wdw, d["wdw"]),
                 (wproj, d["wproj"]), (temp, d["temp"]), (head_w, d["head_w"]), (head_mask, d["head_mask"])]
        xv = d["x"].rearrange("b (h p) n -> b p h n", h=2)
        x1v = d["x1"].rearrange("b (h p) n -> b p h n", h=2)
        vv = d["v"].rearrange("b (h p) n -> b p h n", h=2)

        LATE = 4

        block = ctx.enter_context(nc.Block())

        @block.sync
        def _(sp):
            for dst, src in loads:
                sp.dma_start(dst[:], src).then_inc(w_loaded, DMA)

            def load(k, waits=True):
                if waits:
                    sp.wait_ge(xc_ready, k.q - 1)
                sp.dma_start(x_in[k.p][:], xv[k.b, :, :, bass.ds(k.s * NPX, NPX)]).then_inc(x_loaded[k.p], DMA)

            def store_x1(k):
                sp.wait_ge(x1_ready, k.q + 1)
                sp.dma_start(x1v[k.b, :, :, bass.ds(k.s * NPX, NPX)], x1[k.p][:]).then_inc(x1_stored[k.p], DMA)

            def store_v(k):
                lo, hi = 1 if k.is_first else 0, 1 if k.is_last else ROWS
                px = bass.ds(k.s * NPX + (lo - 1) * WW, (hi - lo) * WW)
                for h in range(2):
                    if h == 0:
                        sp.wait_ge(conv_seq, k.c * VTAPS + VTAPS)
                    else:
                        sp.wait_ge(add_seq, k.c * PSUMS + PSUMS)
                    sp.dma_start(vv[k.b, :, h, px],
                                 vc[k.p][:, h, lo:hi, :].rearrange("p r w -> p (r w)")).then_inc(v_stored[k.p], DMA)

            def step(k, following):
                if k.back(1).is_first:
                    store_x1(k.back(1))
                if following:
                    load(following)
                if k.back(4).is_convolved:
                    store_v(k.back(4))
                if k.back(1).is_real and not k.back(1).is_first:
                    store_x1(k.back(1))

            def image(b, more):
                for i in range(6):
                    step(Chunk(b, 0, i), Chunk(b, 0, i + 1) if i else None)
                with sp.Fori(3, CHUNKS // 2 - 1) as j:
                    step(Chunk(b, j, 0), Chunk(b, j, 1))
                    step(Chunk(b, j, 1), Chunk(b, j, 2))
                step(Chunk(b, 0, CHUNKS - 2), Chunk(b, 0, CHUNKS - 1))
                for i in range(2):
                    step(Chunk(b, 0, CHUNKS - 1 + i), Chunk(b + 1, 0, i) if more else None)
                for i in range(1, LATE + 1):
                    step(Chunk(b, 0, CHUNKS + i), None)
                sp.wait_ge(img_done, b + 1)
                sp.dma_start(d["mt"][b], mt[:]).then_inc(mt_stored, DMA)

            for i in range(2):
                load(Chunk(0, 0, i), waits=False)
            with sp.Fori(0, B - 1) as b:
                image(b, True)
            image(B - 1, False)
            for p in range(2):
                sp.wait_ge(x1_stored[p], DMA * B * CHUNKS // 2)
            sp.wait_ge(v_stored[0], 2 * DMA * B * (CHUNKS // 2 + 1))
            sp.wait_ge(v_stored[1], 2 * DMA * B * (CHUNKS // 2))
            sp.wait_ge(mt_stored, DMA * B)

        @block.gpsimd
        def _(pool):
            nc.gpsimd.memset(mean_w[:], 1.0 / C)
            nc.gpsimd.memset(ones[:], 1.0)
            nc.gpsimd.memset(consts[:, 0:1], LN_EPS)
            nc.gpsimd.memset(consts[:, 1:2], 0.0)
            nc.gpsimd.memset(s_pad[:], 0.0)
            nc.gpsimd.memset(attn_bd[:], 0.0)
            nc.gpsimd.memset(zeros[:], 0.0).then_inc(zero_row_ready, 1)
            for p in range(2):
                nc.gpsimd.memset(raw[p][:, :, :, 0:1], 0.0)
                last = nc.gpsimd.memset(raw[p][:, :, :, WW + 1:WW + 2], 0.0)
            last.then_inc(w_ready, 1)

            def clear(rows):
                z = zeros[:, None, None, :].to_broadcast(rows.shape)
                nc.gpsimd.tensor_tensor(rows, z, z, ALU.add).then_inc(zeros_ready, 1)

            def sum_x(k):
                pool.wait_ge(x_loaded[k.p], (k.pairs + 1) * DMA)
                pool.wait_ge(mu_ready, k.q)
                nc.gpsimd.tensor_tensor(x_sum[:], x_in[k.p][:, 0], x_in[k.p][:, 1], ALU.add).then_inc(x_summed, 1)

            def sum_squares(k):
                pool.wait_ge(sq_ready, k.q + 1)
                pool.wait_ge(var_ready, k.q)
                nc.gpsimd.tensor_tensor(sq_sum[:], sq[:, 0], sq[:, 1], ALU.add).then_inc(sq_summed, 1)

            def start(b):
                pool.wait_ge(zero_row_ready, 1)
                pool.wait_ge(img_done, b)
                clear(raw[0][:, :, 0:2, 1:WW + 1])

            def add(k, half, t):
                out = vc[k.p][:, 1] if half else qc[:]
                n = half * 9 + t
                if t == 1:
                    pool.wait_ge(prod_ready, k.c * PTAPS + n + 1)
                    if half:
                        pool.wait_ge(v_stored[k.p], k.c_pairs * 2 * DMA)
                    else:
                        pool.wait_ge(qt_ready, k.c * 2)
                    first = prod[(n - 1) % PRODS][:]
                else:
                    pool.wait_ge(prod_ready, k.c * PTAPS + n + 1)
                    pool.wait_ge(add_seq, k.c * PSUMS + half * 8 + t - 1)
                    first = out
                nc.gpsimd.tensor_tensor(out, first, prod[n % PRODS][:], ALU.add).then_inc(add_seq, 1)

            def step(k):
                if isinstance(k.j, int) and k.s == CHUNKS + 2:
                    pool.wait_ge(conv_seq, k.back(3).c * VTAPS)
                    pool.wait_ge(prod_ready, k.back(3).c * PTAPS)
                    pool.wait_ge(qt_ready, k.back(3).c * 2)
                    clear(raw[0][:, :, 2:3, 1:WW + 1])
                if k.is_real:
                    sum_x(k)
                if k.back(3).is_convolved:
                    add(k.back(3), 0, 1)
                if k.back(1).is_real:
                    sum_squares(k.back(1))
                if k.back(3).is_convolved:
                    for t in range(2, 9):
                        add(k.back(3), 0, t)
                    for t in range(1, 9):
                        add(k.back(3), 1, t)

            image_loop(pool, step, LATE, start)

        @block.vector
        def _(dve):
            dve.wait_ge(w_loaded, DMA * len(loads))
            for t in range(9):
                nc.vector.tensor_scalar(qdiag[:, t, :], ident[:], wdw[:, 0, t:t + 1], None, ALU.mult)
            for dx in range(3):
                nc.vector.tensor_tensor(head_w[:, :, 3 * dx:3 * dx + 3, :], head_w[:, :, 3 * dx:3 * dx + 3, :],
                                        head_mask[:], ALU.mult).then_inc(v_prep, 1)
            dve.wait_ge(v_prep, 3)
            hw = head_w[:].rearrange("p h (x y) c -> p h x y c", x=3)
            for h in range(2):
                nc.vector.tensor_tensor(head_conv[:, h], hw[:, h, :, 0, :], hw[:, h, :, 1, :], ALU.add).then_inc(v_prep, 1)
            dve.wait_ge(v_prep, 5)
            for h in range(2):
                last = nc.vector.tensor_tensor(head_conv[:, h], head_conv[:, h], hw[:, h, :, 2, :], ALU.add)
            last.then_inc(w_ready, 1)
            dve.wait_ge(w_ready, 2)

            def conv(k, tiles, op0):
                done = k.c * VTAPS + op0
                for t, (dy, dx) in enumerate(TAPS):
                    for h, (src, out) in enumerate(tiles):
                        window = raw[k.p][:, src, dy:dy + ROWS, dx:dx + WW]
                        w = wdw[:, src, t:t + 1]
                        if t == 0:
                            ins = nc.vector.tensor_scalar(out, window, w, None, ALU.mult)
                        else:
                            dve.wait_ge(conv_seq, done + len(tiles) * (t - 1) + h + 1)
                            ins = nc.vector.scalar_tensor_tensor(out, window, w, out, ALU.mult, ALU.add)
                        ins.then_inc(conv_seq, 1)

            def conv_k(k):
                dve.wait_ge(raw_ready, k.c + 1)
                dve.wait_ge(kt_ready, k.c * 2)
                conv(k, [(2, kc[:, 0]), (3, kc[:, 1])], 0)

            def conv_v(k):
                dve.wait_ge(v_stored[k.p], k.c_pairs * 2 * DMA)
                conv(k, [(4, vc[k.p][:, 0])], 18)

            def center(k):
                dve.wait_ge(mu_ready, k.q + 1)
                dve.wait_ge(x1_ready, k.q)
                mu = stat_ps[:].unsqueeze(1).broadcast_to([P, 2, NPX])
                nc.vector.tensor_tensor(xc[k.p][:], x_in[k.p][:], mu, ALU.subtract).then_inc(xc_ready, 1)

            def normalize(k):
                dve.wait_ge(r_ready, k.q + 1)
                dve.wait_ge(xc_ready, k.q + 1)
                r = rstd[:, 1:2, :].broadcast_to([P, 2, NPX])
                nc.vector.tensor_tensor(xc[k.p][:], xc[k.p][:], r, ALU.mult).then_inc(xr_done, 1)
                dve.wait_ge(xr_done, k.q + 1)
                dve.wait_ge(x1_stored[k.p], k.pairs * DMA)
                if not k.is_first:
                    dve.wait_ge(qkv_ready, k.q * 6 - 6)
                for h in range(2):
                    last = nc.vector.tensor_scalar(x1[k.p][:, h], xc[k.p][:, h], ln_gb[:, h, 0:1], ln_gb[:, h, 1:2],
                                                   ALU.mult, ALU.add)
                last.then_inc(x1_ready, 1)

            def step(k):
                now, older = k.back(1), k.back(3)
                if now.is_real:
                    center(now)
                if older.is_convolved:
                    conv_k(older)
                if now.is_real:
                    normalize(now)
                if older.is_convolved:
                    conv_v(older)

            def end(b):
                n = [0]

                def link(ins):
                    n[0] += 1
                    ins.then_inc(fin_v, 1)
                    return n[0]

                def after(k):
                    dve.wait_ge(fin_v, b * FIN_V + k)

                dve.wait_ge(gram_done, (b + 1) * (CHUNKS + 1))
                eye = ident[:].unsqueeze(1).broadcast_to([P, 2, P])
                nc.vector.tensor_tensor(dk[:], gram_ps[:, :, 2 * P:3 * P], eye, ALU.mult).then_inc(fin_v, 1)
                n[0] = 1
                dq_done = link(nc.vector.tensor_tensor(dq[:], gram_ps[:, :, 0:P], eye, ALU.mult))
                for j in range(3):
                    r = slice(32 * j, 32 * j + 32)
                    last = nc.vector.tensor_copy(gs[r], gram_ps[r, :, P + 32 * j:P + 32 * j + 32])
                gs_done = link(last)
                after(dq_done)
                link(nc.vector.reduce_sum(nq[:], dq[:], axis=AXX))
                dve.wait_ge(fin_t, b * FIN_T + 1)
                for j in range(3):
                    r = slice(32 * j, 32 * j + 32)
                    last = nc.vector.tensor_copy(nk[r], nk_ps[r, :, 32 * j:32 * j + 32])
                link(last)
                dve.wait_ge(fin_s, b * FIN_S + 1)
                k = link(nc.vector.tensor_scalar(nqs[:], nqs[:], 1e-12, None, ALU.max))
                link(nc.vector.tensor_scalar(nks[:], nks[:], 1e-12, None, ALU.max))
                after(k + 1)
                link(nc.vector.reciprocal(nqs[:], nqs[:]))
                k = link(nc.vector.reciprocal(nks[:], nks[:]))
                after(k)
                for h in range(2):
                    last = nc.vector.tensor_scalar(gs[:, h], gs[:, h], nqs[:, h:h + 1], temp[:, h:h + 1],
                                                   ALU.mult, ALU.mult)
                k = link(last)
                after(k)
                k = link(nc.vector.tensor_tensor(s_pad[:, :, 1:HD + 1], gs[:], nks[:], ALU.mult))
                dve.wait_ge(fin_t, b * FIN_T + 2)
                k = link(nc.vector.reduce_max(mx[:], conv_ps, axis=AXX))
                after(k)
                link(nc.vector.tensor_scalar(mx[:], mx[:], -1.0, None, ALU.mult))
                dve.wait_ge(fin_s, b * FIN_S + 2)
                k = link(nc.vector.reciprocal(sm[:], sm[:]))
                after(k)
                for h in range(2):
                    for j in range(3):
                        r = slice(32 * j, 32 * j + 32)
                        last = nc.vector.tensor_scalar(attn_bd[r, h, r], ex[r, h], sm[r, h:h + 1], None, ALU.mult)
                link(last)
                assert n[0] == FIN_V
                dve.wait_ge(fin_t, b * FIN_T + 3)
                dve.wait_ge(mt_stored, b * DMA)
                nc.vector.tensor_copy(mt[:], mt_ps).then_inc(img_done, 1)

            image_loop(dve, step, LATE, end=end)

        @block.scalar
        def _(act):
            act.wait_ge(w_ready, 2)

            def square(k):
                act.wait_ge(xc_ready, k.q + 1)
                act.wait_ge(sq_summed, k.q)
                nc.scalar.activation(sq[:], xc[k.p][:], ACT.Square).then_inc(sq_ready, 1)

            def deviation(k):
                act.wait_ge(var_ready, k.q + 1)
                act.wait_ge(xr_done, k.q)
                nc.scalar.activation(rstd[:, 0], stat_ps[:], ACT.Ln, bias=consts[:, 0:1]).then_inc(ln_done, 1)
                act.wait_ge(ln_done, k.q + 1)
                nc.scalar.activation(rstd[:, 1], rstd[:, 0], ACT.Exp, scale=-0.5, bias=consts[:, 1:2]).then_inc(r_ready, 1)

            def rows_above(k):
                if k.is_first:
                    act.wait_ge(zeros_ready, k.b * 2 + 1)
                    return
                act.wait_ge(conv_seq, k.back(1).c * VTAPS)
                act.wait_ge(qt_ready, k.back(1).c * 2)
                act.wait_ge(prod_ready, k.back(1).c * PTAPS)
                act.wait_ge(raw_ready, k.c)
                nc.scalar.copy(raw[k.p][:, :, 0:2, 1:WW + 1],
                               raw[1 - k.p][:, :, ROWS:ROWS + 2, 1:WW + 1]).then_inc(carried, 1)
                if k.is_last:
                    act.wait_ge(zeros_ready, k.b * 2 + 2)
                    act.wait_ge(carried, (k.b + 1) * CHUNKS)
                    act.sem_inc(raw_ready, 1)

            def take_qkv(k, tiles):
                for t in tiles:
                    act.wait_ge(qkv_ready, k.q * 6 + t + 1)
                    nc.scalar.copy(raw[k.p][:, t, 2:ROWS + 2, 1:WW + 1],
                                   qkv_ps[t % 2][:].rearrange("p (r w) -> p r w", w=WW)).then_inc(qkv_evac, 1)
                    if t == 5:
                        act.wait_ge(qkv_evac, k.q * 6 + 6)
                        act.sem_inc(raw_ready, 1)

            def take_q(k, i):
                act.wait_ge(gram_done, k.c)
                act.wait_ge(qt_ready, k.c * 2 + i + 1)
                nc.scalar.copy(qkt[:, 2 * i:2 * i + 2, :, 0, :], qt_ps[i][:]).then_inc(qt_evac, 1)

            def take_k(k, i):
                act.wait_ge(kt_ready, k.c * 2 + i + 1)
                nc.scalar.copy(qkt[:, 2 * i:2 * i + 2, :, 1, :], kt_ps[:]).then_inc(kt_evac, 1)

            def product(k, n):
                src, t = 1 if n < 9 else 5, n % 9
                if n == 0:
                    act.wait_ge(raw_ready, k.c + 1)
                added = lambda m: m // 9 * 8 + max(m % 9, 1)
                if n >= PRODS:
                    act.wait_ge(add_seq, k.c * PSUMS + added(n - PRODS))
                elif k.is_first:
                    act.wait_ge(add_seq, k.c * PSUMS)
                else:
                    act.wait_ge(add_seq, k.c * PSUMS - PSUMS + added(n + 18 - PRODS))
                dy, dx = TAPS[t]
                nc.scalar.activation(prod[n % PRODS][:], raw[k.p][:, src, dy:dy + ROWS, dx:dx + WW], ACT.Identity,
                                     scale=wdw[:, src, t:t + 1], bias=consts[:, 1:2]).then_inc(prod_ready, 1)

            def step(k):
                older = k.back(3)

                def products(lo, hi):
                    for n in range(lo, hi):
                        if older.is_convolved:
                            product(older, n)

                def take(tiles):
                    if k.back(2).is_real:
                        take_qkv(k.back(2), tiles)

                products(0, 1)
                if k.back(1).is_real:
                    square(k.back(1))
                products(1, 2)
                if k.back(2).is_convolved:
                    rows_above(k.back(2))
                take([0])
                products(2, 4)
                take([1])
                products(4, 5)
                take([2])
                products(5, 6)
                if k.back(1).is_real:
                    deviation(k.back(1))
                take([3])
                products(6, 8)
                take([4])
                products(8, 9)
                take([5])
                products(9, 12)
                if older.is_convolved:
                    take_q(older, 0)
                    take_k(older, 0)
                products(12, 15)
                if older.is_convolved:
                    take_q(older, 1)
                    take_k(older, 1)
                products(15, 18)

            def end(b):
                nc.scalar.preload_act_table_set("sqrt_and_others")
                act.wait_ge(fin_v, b * FIN_V + 5)
                nc.scalar.activation(nqs[:], nq[:], ACT.Sqrt, bias=consts[:, 1:2])
                nc.scalar.activation(nks[:], nk[:], ACT.Sqrt, bias=consts[:, 1:2]).then_inc(fin_s, 1)
                nc.scalar.preload_act_table_set("natural_log_exp_and_others")
                act.wait_ge(fin_v, b * FIN_V + 13)
                for h in range(2):
                    last = nc.scalar.activation(ex[:, h], conv_ps[:, h], ACT.Exp, bias=mx[:, h:h + 1],
                                                accum_out=sm[:, h:h + 1])
                last.then_inc(fin_s, 1)

            nc.scalar.preload_act_table_set("natural_log_exp_and_others")
            image_loop(act, step, LATE, end=end)

        @block.tensor
        def _(pe):
            pe.wait_ge(w_ready, 2)
            pe.wait_ge(w_loaded, DMA * len(loads))

            def q_conv(k, i):
                pe.wait_ge(raw_ready, k.c + 1)
                pe.wait_ge(qt_evac, k.c * 2)
                for r in range(2):
                    for t, (dy, dx) in enumerate(TAPS):
                        nc.tensor.matmul(qt_ps[i][:, r, 0], raw[k.p][:, 0, 2 * i + r + dy, dx:dx + WW],
                                         qdiag[:, t], start=(t == 0), stop=(t == 8))
                pe.wait_ge(add_seq, k.c * PSUMS + 8)
                for r in range(2):
                    last = nc.tensor.transpose(qt_ps[i][:, r, 1], qc[:, 2 * i + r], ident[:])
                last.then_inc(qt_ready, 1)

            def k_transpose(k, i):
                pe.wait_ge(conv_seq, k.c * VTAPS + 18)
                pe.wait_ge(kt_evac, k.c * 2 + i)
                for r in range(2):
                    for h in range(2):
                        last = nc.tensor.transpose(kt_ps[:, r, h], kc[:, h, 2 * i + r], ident[:])
                last.then_inc(kt_ready, 1)

            def gram(k):
                pe.wait_ge(qt_evac, k.c * 2 + 2)
                pe.wait_ge(kt_evac, k.c * 2 + 2)
                rows = range(1 if k.is_first else 0, 1 if k.is_last else ROWS)
                for n, r in enumerate(rows):
                    for h in range(2):
                        nc.tensor.matmul(gram_ps[:, h, 0:2 * P], qkt[:, r, h, 0], qkt[:, r, h],
                                         start=k.is_first and n == 0, stop=True, skip_group_check=True)
                        last = nc.tensor.matmul(gram_ps[:, h, 2 * P:3 * P], qkt[:, r, h, 1], qkt[:, r, h, 1],
                                                start=False, stop=True, skip_group_check=True)
                last.then_inc(gram_done, 1)

            def qkv(k, tiles):
                pe.wait_ge(x1_ready, k.q + 1)
                for t in tiles:
                    pe.wait_ge(qkv_evac, k.q * 6 + t - 1 if t >= 2 else k.q * 6)
                    for h in range(2):
                        last = nc.tensor.matmul(qkv_ps[t % 2][:], wqkv[:, h, t * P:(t + 1) * P], x1[k.p][:, h],
                                                start=(h == 0), stop=(h == 1))
                    last.then_inc(qkv_ready, 1)

            def mean(k):
                pe.wait_ge(x_summed, k.q + 1)
                pe.wait_ge(r_ready, k.q)
                nc.tensor.matmul(stat_ps[:], mean_w[:], x_sum[:], start=True, stop=True).then_inc(mu_ready, 1)

            def variance(k):
                pe.wait_ge(sq_summed, k.q + 1)
                nc.tensor.matmul(stat_ps[:], mean_w[:], sq_sum[:], start=True, stop=True).then_inc(var_ready, 1)

            def start(b):
                pe.wait_ge(img_done, b)

            def step(k):
                if k.back(2).is_real:
                    qkv(k.back(2), range(0, 3))
                if k.back(1).is_real:
                    variance(k.back(1))
                if k.back(2).is_real:
                    qkv(k.back(2), range(3, 6))
                if k.back(3).is_convolved:
                    for i in range(2):
                        q_conv(k.back(3), i)
                        k_transpose(k.back(3), i)
                if k.is_real:
                    mean(k)
                if k.back(3).is_convolved:
                    gram(k.back(3))

            def end(b):
                pe.wait_ge(fin_v, b * FIN_V + 1)
                for h in range(2):
                    last = nc.tensor.matmul(nk_ps[:, h], ones[:], dk[:, h], start=True, stop=True)
                last.then_inc(fin_t, 1)
                pe.wait_ge(fin_v, b * FIN_V + 11)
                for o in range(2):
                    for n, (h, dx) in enumerate((h, dx) for h in range(2) for dx in range(3)):
                        last = nc.tensor.matmul(conv_ps[:, o], head_conv[:, h, dx, o * P:(o + 1) * P],
                                                s_pad[:, h, dx:dx + HD], start=(n == 0), stop=(n == 5))
                last.then_inc(fin_t, 1)
                pe.wait_ge(fin_v, b * FIN_V + 15)
                for h in range(2):
                    last = nc.tensor.matmul(mt_ps[:, h], attn_bd[:, h], wproj[:, h], start=True, stop=True)
                last.then_inc(fin_t, 1)

            image_loop(pe, step, LATE, start, end)


def attention_and_mlp(nc, d):
    with ExitStack() as ctx:
        def sb(name, shape, dt=FP32):
            return ctx.enter_context(nc.sbuf_tensor("b_" + name, shape, dt))

        def ps(name, shape):
            return ctx.enter_context(nc.psum_tensor("b_" + name, shape, FP32))

        sems = []
        ctx.callback(nc.all_engine_barrier)
        ctx.callback(nc.clear_and_free_semaphores, sems)

        def sem(name):
            sems.append(nc.alloc_semaphore("b_" + name))
            return sems[-1]

        mean_w = sb("mean_w", [P, P])
        ln_gb = sb("ln_gb", [P, 2, 2])
        w1 = sb("w1", [P, 2, HID])
        b1 = sb("b1", [128, 3])
        w2 = sb("w2", [128, 3, C])
        b2 = sb("b2", [P, 2])
        wsa = sb("wsa", [P, 2, 9])
        consts = sb("consts", [P, 2])
        zeros = sb("zeros", [9 * PLANE // 1300, 1300])
        mt = sb("mt", [P, 2, C])
        x1 = [sb(f"x1{p}", [P, 2, NPX]) for p in range(2)]
        v = [sb(f"v{p}", [P, 2, NPX]) for p in range(2)]
        x2 = [sb(f"x2{p}", [P, 2, NPX]) for p in range(2)]
        xn = [sb(f"xn{p}", [P, 2, NPX]) for p in range(2)]
        xg = [sb(f"xg{p}", [P, 2, NPX]) for p in range(2)]
        x2_sum = sb("x2_sum", [P, NPX])
        sq = sb("sq", [P, 2, NPX])
        sq_sum = sb("sq_sum", [P, NPX])
        rstd = sb("rstd", [P, 2, NPX])
        hid = sb("hid", [128, 3, NPX])
        y = [sb(f"y{p}", [P, 2, NPX]) for p in range(2)]
        taps = [sb(f"taps{p}", [9, NPX]) for p in range(2)]

        o_ps = ps("o_ps", [P, 2, NPX])
        stat_ps = ps("stat_ps", [P, NPX])
        h_ps = [ps(f"h_ps{p}", [128, NPX]) for p in range(2)]
        y_ps = [ps(f"y_ps{p}", [P, NPX]) for p in range(2)]
        taps_ps = ps("taps_ps", [9, NPX])

        w_loaded = sem("w_loaded")
        w_ready = sem("w_ready")
        border_zero = sem("border_zero")
        mt_loaded = sem("mt_loaded")
        xv_loaded = [sem(f"xv_loaded{p}") for p in range(2)]
        x2_stored = [sem(f"x2_stored{p}") for p in range(2)]
        y_stored = [sem(f"y_stored{p}") for p in range(2)]
        taps_stored = [sem(f"taps_stored{p}") for p in range(2)]
        x2_summed = sem("x2_summed")
        sq_summed = sem("sq_summed")
        o_ready = sem("o_ready")
        x2_ready = sem("x2_ready")
        mu_ready = sem("mu_ready")
        xc_ready = sem("xc_ready")
        sq_ready = sem("sq_ready")
        var_ready = sem("var_ready")
        ln_done = sem("ln_done")
        r_ready = sem("r_ready")
        xr_done = sem("xr_done")
        xg_ready = sem("xg_ready")
        h_ready = sem("h_ready")
        h_gelu = sem("h_gelu")
        y_ready = sem("y_ready")
        y_gelu = sem("y_gelu")
        taps_ready = sem("taps_ready")
        taps_copied = sem("taps_copied")

        loads = [(ln_gb, d["ln2_gb"]), (w1, d["w1"]), (b1, d["b1"]), (w2, d["w2"]), (b2, d["b2"]), (wsa, d["wsa"])]
        x1v, vv, x2v, yv = (d[k].rearrange("b (h p) n -> b p h n", h=2) for k in ("x1", "v", "x2", "y"))
        planes = d["planes"][:, 0:9 * PLANE].rearrange("b (t r c) -> b t r c", t=9, c=WW + 2)

        TOTAL = B * CHUNKS

        class Turn:

            def __init__(self, j, i, b=0):
                self.j, self.i, self.p, self.b = j, i, i % 2, b
                self.q = 2 * j + i
                self.pairs = j + i // 2
                known = isinstance(j, int)
                self.is_first = known and self.q == 0
                self.is_real = not known or 0 <= self.q < TOTAL

            def back(self, k):
                return Turn(self.j, self.i - k, self.b)

        LATE = 3

        def turns(eng, step):
            for i in range(4):
                step(Turn(0, i))
            with eng.Fori(2, CHUNKS // 2) as j:
                step(Turn(j, 0))
                step(Turn(j, 1))
            with eng.Fori(1, B) as b:
                with eng.Fori(0, CHUNKS // 2) as j:
                    for i in range(2):
                        step(Turn(b * (CHUNKS // 2) + j, i, b))
            for i in range(LATE):
                step(Turn(0, TOTAL + i))

        block = ctx.enter_context(nc.Block())

        @block.sync
        def _(sp):
            for dst, src in loads:
                sp.dma_start(dst[:], src).then_inc(w_loaded, DMA)
            sp.wait_ge(w_ready, 1)
            for b in range(B):
                sp.dma_start(d["planes"][b, 0:9 * PLANE].rearrange("(p n) -> p n", n=1300), zeros[:]).then_inc(border_zero, DMA)
            sp.wait_ge(border_zero, DMA * B)

            def load(b, s, p, waits=True):
                if waits:
                    sp.wait_ge(x2_ready, b * CHUNKS + s - 1)
                px = bass.ds(s * NPX, NPX)
                sp.dma_start(x1[p][:], x1v[b, :, :, px]).then_inc(xv_loaded[p], DMA)
                sp.dma_start(v[p][:], vv[b, :, :, px]).then_inc(xv_loaded[p], DMA)

            def store_x2(b, s, p):
                sp.wait_ge(x2_ready, b * CHUNKS + s + 1)
                sp.dma_start(x2v[b, :, :, bass.ds(s * NPX, NPX)], x2[p][:]).then_inc(x2_stored[p], DMA)

            def store_y(b, s, p):
                sp.wait_ge(y_gelu, (b * CHUNKS + s + 1) * 2)
                sp.dma_start(yv[b, :, :, bass.ds(s * NPX, NPX)], y[p][:]).then_inc(y_stored[p], DMA)

            def store_taps(b, s, p):
                sp.wait_ge(taps_copied, b * CHUNKS + s + 1)
                sp.dma_start(planes[b, :, bass.ds(s * ROWS + 1, ROWS), 1:WW + 1],
                             taps[p][:].rearrange("t (r w) -> t r w", w=WW)).then_inc(taps_stored[p], DMA)

            def place(b, s, first):
                if isinstance(s, int) and s < 0:
                    return None if first else (b - 1, s + CHUNKS)
                if isinstance(s, int) and s >= CHUNKS:
                    return b + 1, s - CHUNKS
                return b, s

            def step(b, s, p, first, last):
                store_x2(b, s, p)
                if not (last and isinstance(s, int) and s + 2 >= CHUNKS):
                    load(*place(b, s + 2, first), p)
                at = place(b, s - 3, first)
                if at:
                    store_taps(*at, 1 - p)
                at = place(b, s - 2, first)
                if at:
                    store_y(*at, p)

            def image(b, first=False, last=False):
                sp.wait_ge(o_ready, b * CHUNKS)
                sp.dma_start(mt[:], d["mt"][b]).then_inc(mt_loaded, DMA)
                for s in range(4):
                    step(b, s, s % 2, first, last)
                with sp.Fori(2, CHUNKS // 2 - 1) as j:
                    for p in range(2):
                        step(b, j * 2 + p, p, first, last)
                for s in (CHUNKS - 2, CHUNKS - 1):
                    step(b, s, s % 2, first, last)

            for p in range(2):
                load(0, p, p, waits=False)
            image(0, first=True)
            with sp.Fori(1, B - 1) as b:
                image(b)
            image(B - 1, last=True)
            store_taps(B - 1, CHUNKS - 3, 1)
            store_y(B - 1, CHUNKS - 2, 0)
            store_taps(B - 1, CHUNKS - 2, 0)
            store_y(B - 1, CHUNKS - 1, 1)
            store_taps(B - 1, CHUNKS - 1, 1)
            for p in range(2):
                sp.wait_ge(x2_stored[p], DMA * B * CHUNKS // 2)
                sp.wait_ge(y_stored[p], DMA * B * CHUNKS // 2)
                sp.wait_ge(taps_stored[p], DMA * B * CHUNKS // 2)

        @block.gpsimd
        def _(pool):
            nc.gpsimd.memset(zeros[:], 0.0)
            nc.gpsimd.memset(mean_w[:], 1.0 / C)
            nc.gpsimd.memset(consts[:, 0:1], LN_EPS)
            nc.gpsimd.memset(consts[:, 1:2], 0.0).then_inc(w_ready, 1)

            def sum_squares(k):
                pool.wait_ge(sq_ready, k.q + 1)
                pool.wait_ge(var_ready, k.q)
                nc.gpsimd.tensor_tensor(sq_sum[:], sq[:, 0], sq[:, 1], ALU.add).then_inc(sq_summed, 1)

            def sum_x2(k):
                pool.wait_ge(x2_ready, k.q + 1)
                pool.wait_ge(mu_ready, k.q)
                nc.gpsimd.tensor_tensor(x2_sum[:], x2[k.p][:, 0], x2[k.p][:, 1], ALU.add).then_inc(x2_summed, 1)

            def step(k):
                if k.back(1).is_real:
                    sum_squares(k.back(1))
                if k.is_real:
                    sum_x2(k)

            turns(pool, step)

        @block.vector
        def _(dve):
            dve.wait_ge(w_loaded, DMA * len(loads))

            def center(k):
                dve.wait_ge(mu_ready, k.q + 1)
                dve.wait_ge(x2_ready, k.q + 1)
                dve.wait_ge(xg_ready, k.q)
                mu = stat_ps[:].unsqueeze(1).broadcast_to([P, 2, NPX])
                nc.vector.tensor_tensor(xn[k.p][:], x2[k.p][:], mu, ALU.subtract).then_inc(xc_ready, 1)

            def add_x1(k):
                dve.wait_ge(o_ready, k.q + 1)
                dve.wait_ge(x2_stored[k.p], k.pairs * DMA)
                if not k.is_first:
                    dve.wait_ge(x2_summed, k.q - 1)
                nc.vector.tensor_tensor(x2[k.p][:], x1[k.p][:], o_ps[:], ALU.add).then_inc(x2_ready, 1)

            def normalize(k):
                dve.wait_ge(r_ready, k.q + 1)
                dve.wait_ge(xc_ready, k.q + 1)
                r = rstd[:, 1:2, :].broadcast_to([P, 2, NPX])
                nc.vector.tensor_tensor(xn[k.p][:], xn[k.p][:], r, ALU.mult).then_inc(xr_done, 1)
                dve.wait_ge(xr_done, k.q + 1)
                if not k.is_first:
                    dve.wait_ge(h_ready, k.q * 3 - 3)
                for h in range(2):
                    last = nc.vector.tensor_scalar(xg[k.p][:, h], xn[k.p][:, h], ln_gb[:, h, 0:1], ln_gb[:, h, 1:2],
                                                   ALU.mult, ALU.add)
                last.then_inc(xg_ready, 1)

            def copy_taps(k):
                dve.wait_ge(taps_ready, k.q + 1)
                dve.wait_ge(taps_stored[k.p], k.pairs * DMA)
                nc.vector.tensor_copy(taps[k.p][:], taps_ps[:]).then_inc(taps_copied, 1)

            def step(k):
                if k.back(1).is_real:
                    center(k.back(1))
                if k.is_real:
                    add_x1(k)
                if k.back(1).is_real:
                    normalize(k.back(1))
                if k.back(3).is_real:
                    copy_taps(k.back(3))

            turns(dve, step)

        @block.scalar
        def _(act):
            act.wait_ge(w_ready, 1)
            act.wait_ge(w_loaded, DMA * len(loads))

            def gelu_h(k, t):
                act.wait_ge(y_ready, k.q * 2)
                act.wait_ge(h_ready, k.q * 3 + t + 1)
                nc.scalar.activation(hid[:, t], h_ps[t % 2][:], ACT.Gelu, bias=b1[:, t:t + 1]).then_inc(h_gelu, 1)

            def square(k):
                act.wait_ge(xc_ready, k.q + 1)
                act.wait_ge(sq_summed, k.q)
                nc.scalar.activation(sq[:], xn[k.p][:], ACT.Square).then_inc(sq_ready, 1)

            def deviation(k):
                nc.scalar.preload_act_table_set("natural_log_exp_and_others")
                act.wait_ge(var_ready, k.q + 1)
                act.wait_ge(xr_done, k.q)
                nc.scalar.activation(rstd[:, 0], stat_ps[:], ACT.Ln, bias=consts[:, 0:1]).then_inc(ln_done, 1)
                act.wait_ge(ln_done, k.q + 1)
                nc.scalar.activation(rstd[:, 1], rstd[:, 0], ACT.Exp, scale=-0.5, bias=consts[:, 1:2]).then_inc(r_ready, 1)

            def gelu_y(k):
                act.wait_ge(y_stored[k.p], k.pairs * DMA)
                if not k.is_first:
                    act.wait_ge(taps_ready, k.q - 1)
                for h in range(2):
                    act.wait_ge(y_ready, k.q * 2 + h + 1)
                    nc.scalar.activation(y[k.p][:, h], y_ps[h][:], ACT.Gelu, bias=b2[:, h:h + 1]).then_inc(y_gelu, 1)

            def step(k):
                old = k.back(2)
                if old.is_real:
                    for t in range(3):
                        gelu_h(old, t)
                if k.back(1).is_real:
                    square(k.back(1))
                    deviation(k.back(1))
                if k.back(1).is_real or old.is_real:
                    nc.scalar.preload_act_table_set("gelu_and_others")
                if old.is_real:
                    gelu_y(old)

            turns(act, step)

        @block.tensor
        def _(pe):
            pe.wait_ge(w_ready, 1)
            pe.wait_ge(w_loaded, DMA * len(loads))

            def fc1(k, tiles):
                pe.wait_ge(xg_ready, k.q + 1)
                for t in tiles:
                    pe.wait_ge(h_gelu, k.q * 3 + t - 1 if t >= 2 else k.q * 3)
                    for h in range(2):
                        last = nc.tensor.matmul(h_ps[t % 2][:], w1[:, h, 128 * t:128 * t + 128], xg[k.p][:, h],
                                                start=(h == 0), stop=(h == 1))
                    last.then_inc(h_ready, 1)

            def mean(k):
                pe.wait_ge(x2_summed, k.q + 1)
                pe.wait_ge(r_ready, k.q)
                nc.tensor.matmul(stat_ps[:], mean_w[:], x2_sum[:], start=True, stop=True).then_inc(mu_ready, 1)

            def variance(k):
                pe.wait_ge(sq_summed, k.q + 1)
                nc.tensor.matmul(stat_ps[:], mean_w[:], sq_sum[:], start=True, stop=True).then_inc(var_ready, 1)

            def attend(k):
                pe.wait_ge(mt_loaded, (k.b + 1) * DMA)
                pe.wait_ge(xv_loaded[k.p], (k.pairs + 1) * 2 * DMA)
                pe.wait_ge(x2_ready, k.q)
                for o in range(2):
                    for h in range(2):
                        last = nc.tensor.matmul(o_ps[:, o], mt[:, h, P * o:P * o + P], v[k.p][:, h],
                                                start=(h == 0), stop=(h == 1))
                last.then_inc(o_ready, 1)

            def fc2(k, h):
                pe.wait_ge(h_gelu, k.q * 3 + 3)
                pe.wait_ge(y_gelu, k.q * 2)
                for t in range(3):
                    last = nc.tensor.matmul(y_ps[h][:], w2[:, t, P * h:P * h + P], hid[:, t], start=(t == 0), stop=(t == 2))
                last.then_inc(y_ready, 1)

            def gate_taps(k):
                pe.wait_ge(taps_copied, k.q)
                for h in range(2):
                    pe.wait_ge(y_gelu, k.q * 2 + h + 1)
                    last = nc.tensor.matmul(taps_ps[:], wsa[:, h], y[k.p][:, h], start=(h == 0), stop=(h == 1))
                last.then_inc(taps_ready, 1)

            def step(k):
                old = k.back(2)
                if old.is_real:
                    fc1(old, range(0, 2))
                if k.back(1).is_real:
                    mean(k.back(1))
                if old.is_real:
                    fc1(old, range(2, 3))
                if k.is_real:
                    attend(k)
                if k.back(1).is_real:
                    variance(k.back(1))
                if k.back(3).is_real:
                    gate_taps(k.back(3))
                if old.is_real:
                    fc2(old, 0)
                    fc2(old, 1)

            turns(pe, step)


DIRS, RANK, STATES = 4, 12, 4
NDT, NBC = DIRS * RANK, DIRS * 2 * STATES


def gate_and_scan_inputs(nc, d):
    with ExitStack() as ctx:
        def sb(name, shape, dt=FP32):
            return ctx.enter_context(nc.sbuf_tensor("c_" + name, shape, dt))

        def ps(name, shape):
            return ctx.enter_context(nc.psum_tensor("c_" + name, shape, FP32))

        sems = []
        ctx.callback(nc.all_engine_barrier)
        ctx.callback(nc.clear_and_free_semaphores, sems)

        def sem(name):
            sems.append(nc.alloc_semaphore("c_" + name))
            return sems[-1]

        mean_w = sb("mean_w", [P, P])
        ones = sb("ones", [9, P])
        ln_gb = sb("ln_gb", [P, 2, 2])
        w_in = sb("w_in", [P, 2, 2 * C])
        cw = sb("cw", [P, 2, 9])
        cb = sb("cb", [P, 2])
        w_x = sb("w_x", [P, 2, NDT + NBC])
        b_sa = sb("b_sa", [P, 1])
        consts = sb("consts", [P, 2])
        bias_in = sb("bias_in", [P, 4])
        x2 = [sb(f"x2{p}", [P, 2, NPX]) for p in range(2)]
        y = [sb(f"y{p}", [P, 2, NPX]) for p in range(2)]
        taps = [sb(f"taps{p}", [9, NPX]) for p in range(2)]
        gate = sb("gate", [P, NPX])
        x4 = [sb(f"x4{p}", [P, 2, NPX]) for p in range(2)]
        xn = [sb(f"xn{p}", [P, 2, NPX]) for p in range(2)]
        xg = [sb(f"xg{p}", [P, 2, NPX]) for p in range(2)]
        x4_sum = sb("x4_sum", [P, NPX])
        sq = sb("sq", [P, 2, NPX])
        sq_sum = sb("sq_sum", [P, NPX])
        prod = [sb(f"prod{p}", [P, 2, ROWS, WW]) for p in range(2)]
        rstd = sb("rstd", [P, 2, NPX])
        raw = [sb(f"raw{p}", [P, 2, ROWS + 2, WW + 2]) for p in range(2)]
        zeros = sb("zeros", [P, WW])
        acc = [sb(f"acc{p}", [P, 2, ROWS, WW]) for p in range(2)]
        sz = [sb(f"sz{p}", [P, 2, NPX]) for p in range(2)]
        u = [sb(f"u{p}", [P, 2, ROWS, WW]) for p in range(2)]
        xd = [sb(f"xd{p}", [NDT + NBC, NPX]) for p in range(2)]

        gate_ps = ps("gate_ps", [P, NPX])
        mean_ps = ps("mean_ps", [P, NPX])
        var_ps = ps("var_ps", [P, NPX])
        xz_ps = [ps(f"xz_ps{t}", [P, NPX]) for t in range(4)]
        xd_ps = ps("xd_ps", [P, NPX])

        w_loaded = sem("w_loaded")
        w_ready = sem("w_ready")
        in_loaded = [sem(f"in_loaded{p}") for p in range(2)]
        x4_stored = [sem(f"x4_stored{p}") for p in range(2)]
        z_stored = [sem(f"z_stored{p}") for p in range(2)]
        u_stored = [sem(f"u_stored{p}") for p in range(2)]
        bias_ready = sem("bias_ready")
        w_folded = sem("w_folded")
        x4_summed = sem("x4_summed")
        sq_summed = sem("sq_summed")
        prod_ready = sem("prod_ready")
        tail_added = sem("tail_added")
        gate_sum = sem("gate_sum")
        gate_ready = sem("gate_ready")
        gated = sem("gated")
        x4_ready = sem("x4_ready")
        mu_ready = sem("mu_ready")
        xc_ready = sem("xc_ready")
        sq_ready = sem("sq_ready")
        var_ready = sem("var_ready")
        ln_done = sem("ln_done")
        r_ready = sem("r_ready")
        xg_ready = sem("xg_ready")
        xz_ready = sem("xz_ready")
        x_evac = sem("x_evac")
        z_ready = sem("z_ready")
        zero_row_ready = sem("zero_row_ready")
        zeros_ready = sem("zeros_ready")
        carried = sem("carried")
        raw_ready = sem("raw_ready")
        conv_seq = sem("conv_seq")
        u_ready = sem("u_ready")
        xd_ready = sem("xd_ready")
        xd_evac = sem("xd_evac")

        IN_DMAS, U_DMAS = 5, 3
        VTAPS = 16
        loads = [(ln_gb, d["ln3_gb"]), (w_in, d["w_in"]), (cw, d["cw"]), (cb, d["cb"]), (w_x, d["w_x"]), (b_sa, d["b_sa"])]
        x2v, yv, x4v, zv, uv = (d[k].rearrange("b (h p) n -> b p h n", h=2) for k in ("x2", "y", "x4", "sz", "u"))

        LATE = 5

        block = ctx.enter_context(nc.Block())

        @block.sync
        def _(sp):
            for dst, src in loads:
                sp.dma_start(dst[:], src).then_inc(w_loaded, DMA)

            def load(k, waits=True):
                b, s, p = k.b, k.s, k.p
                if waits:
                    sp.wait_ge(x4_ready, k.q - 1)
                px = bass.ds(s * NPX, NPX)
                for dy in range(3):
                    view = d["planes"][b, 3 * dy * PLANE:3 * dy * PLANE + 3 * (PLANE + 1)].rearrange("(t n) -> t n", t=3)
                    rows = view[:, bass.ds((s * ROWS + dy) * (WW + 2), ROWS * (WW + 2))]
                    rows = rows.rearrange("t (r c) -> t r c", c=WW + 2)[:, :, 0:WW]
                    sp.dma_start(taps[p][3 * dy:3 * dy + 3, :].rearrange("t (r w) -> t r w", w=WW),
                                 rows).then_inc(in_loaded[p], DMA)
                sp.dma_start(y[p][:], yv[b, :, :, px]).then_inc(in_loaded[p], DMA)
                sp.dma_start(x2[p][:], x2v[b, :, :, px]).then_inc(in_loaded[p], DMA)

            def store_x4(k):
                sp.wait_ge(x4_ready, k.q + 1)
                sp.dma_start(x4v[k.b, :, :, bass.ds(k.s * NPX, NPX)], x4[k.p][:]).then_inc(x4_stored[k.p], DMA)

            def store_z(k):
                sp.wait_ge(z_ready, k.q + 1)
                sp.dma_start(zv[k.b, :, :, bass.ds(k.s * NPX, NPX)], sz[k.p][:]).then_inc(z_stored[k.p], DMA)

            def store_u(k):
                lo, hi = 1 if k.is_first else 0, 1 if k.is_last else ROWS
                b, p = k.b, k.p
                sp.wait_ge(u_ready, k.c + 1)
                px = bass.ds(k.s * NPX + (lo - 1) * WW, (hi - lo) * WW)
                own = slice(lo * WW, hi * WW)
                sp.dma_start(uv[b, :, :, px], u[p][:, :, lo:hi, :].rearrange("p h r w -> p h (r w)")).then_inc(u_stored[p], DMA)
                sp.wait_ge(xd_evac, k.c + 1)
                sp.dma_start(d["dts"][:, b, :, px], xd[p][0:NDT, own]).then_inc(u_stored[p], DMA)
                sp.dma_start(d["bc"][:, b, :, px], xd[p][NDT:NDT + NBC, own]).then_inc(u_stored[p], DMA)

            def step(k, following=None):
                if k.is_real:
                    store_x4(k)
                    if following:
                        load(following)
                if k.back(2).is_real:
                    store_z(k.back(2))
                if k.back(4).is_convolved:
                    store_u(k.back(4))

            def image(b, more):
                for i in range(6):
                    step(Chunk(b, 0, i), Chunk(b, 0, i + 2))
                with sp.Fori(3, CHUNKS // 2 - 1) as j:
                    step(Chunk(b, j, 0), Chunk(b, j, 2))
                    step(Chunk(b, j, 1), Chunk(b, j, 3))
                for i in range(2):
                    step(Chunk(b, 0, CHUNKS - 2 + i), Chunk(b + 1, 0, i) if more else None)
                for i in range(LATE):
                    step(Chunk(b, 0, CHUNKS + i))

            for i in range(2):
                load(Chunk(0, 0, i), waits=False)
            with sp.Fori(0, B - 1) as b:
                image(b, True)
            image(B - 1, False)
            for p in range(2):
                sp.wait_ge(x4_stored[p], DMA * B * CHUNKS // 2)
                sp.wait_ge(z_stored[p], DMA * B * CHUNKS // 2)
                sp.wait_ge(u_stored[p], DMA * U_DMAS * B * (CHUNKS // 2 + 1 - p))

        @block.gpsimd
        def _(pool):
            nc.gpsimd.memset(mean_w[:], 1.0 / C)
            nc.gpsimd.memset(ones[:], 1.0)
            nc.gpsimd.memset(consts[:, 0:1], LN_EPS)
            nc.gpsimd.memset(consts[:, 1:2], 0.0)
            nc.gpsimd.memset(zeros[:], 0.0).then_inc(zero_row_ready, 1)
            for p in range(2):
                nc.gpsimd.memset(raw[p][:, :, :, 0:1], 0.0)
                last = nc.gpsimd.memset(raw[p][:, :, :, WW + 1:WW + 2], 0.0)
            last.then_inc(w_ready, 1)

            def clear(rows):
                z = zeros[:, None, None, :].to_broadcast(rows.shape)
                nc.gpsimd.tensor_tensor(rows, z, z, ALU.add).then_inc(zeros_ready, 1)

            def add_last_tap(k):
                pool.wait_ge(prod_ready, k.c + 1)
                pool.wait_ge(conv_seq, k.c * VTAPS + VTAPS)
                nc.gpsimd.tensor_tensor(acc[k.p][:], acc[k.p][:], prod[k.p][:], ALU.add).then_inc(tail_added, 1)

            def sum_squares(k):
                pool.wait_ge(sq_ready, k.q + 1)
                pool.wait_ge(var_ready, k.q)
                nc.gpsimd.tensor_tensor(sq_sum[:], sq[:, 0], sq[:, 1], ALU.add).then_inc(sq_summed, 1)

            def times_gate(k):
                pool.wait_ge(gate_ready, k.q + 1)
                pool.wait_ge(in_loaded[k.p], (k.pairs + 1) * IN_DMAS * DMA)
                g = gate[:].unsqueeze(1).broadcast_to([P, 2, NPX])
                nc.gpsimd.tensor_tensor(y[k.p][:], y[k.p][:], g, ALU.mult).then_inc(gated, 1)

            def add_gated(k):
                pool.wait_ge(x4_stored[k.p], k.pairs * DMA)
                pool.wait_ge(gated, k.q + 1)
                nc.gpsimd.tensor_tensor(x4[k.p][:], x2[k.p][:], y[k.p][:], ALU.add).then_inc(x4_ready, 1)
                pool.wait_ge(x4_ready, k.q + 1)
                pool.wait_ge(mu_ready, k.q)
                nc.gpsimd.tensor_tensor(x4_sum[:], x4[k.p][:, 0], x4[k.p][:, 1], ALU.add).then_inc(x4_summed, 1)

            def step(k):
                if k.is_first:
                    pool.wait_ge(zero_row_ready, 1)
                    pool.wait_ge(conv_seq, k.c * VTAPS)
                    pool.wait_ge(prod_ready, k.c)
                    clear(raw[0][:, :, 0:2, 1:WW + 1])
                if isinstance(k.j, int) and k.s == CHUNKS + 2:
                    pool.wait_ge(conv_seq, k.back(3).c * VTAPS)
                    pool.wait_ge(prod_ready, k.back(3).c)
                    clear(raw[0][:, :, 2:3, 1:WW + 1])
                if k.is_real:
                    times_gate(k)
                if k.back(4).is_convolved:
                    add_last_tap(k.back(4))
                if k.back(1).is_real:
                    sum_squares(k.back(1))
                if k.is_real:
                    add_gated(k)

            image_loop(pool, step, LATE)

        @block.vector
        def _(dve):
            dve.wait_ge(w_loaded, DMA * len(loads))
            dve.wait_ge(w_ready, 1)
            dve.wait_ge(bias_ready, 1)
            nc.vector.tensor_copy(bias_in[:], xd_ps[0:P, 0:4])
            for h in range(2):
                last = nc.vector.tensor_scalar(w_in[:, h], w_in[:, h], ln_gb[:, h, 0:1], None, ALU.mult)
            last.then_inc(w_folded, 1)

            def conv(k, lo, hi):
                if lo == 0:
                    dve.wait_ge(raw_ready, k.c + 1)
                    dve.wait_ge(u_ready, k.c - 1) if not k.is_first else dve.wait_ge(u_ready, k.c)
                for i in range(lo, hi):
                    (dy, dx), h, t = TAPS[i // 2], i % 2, i // 2
                    window = raw[k.p][:, h, dy:dy + ROWS, dx:dx + WW]
                    w = cw[:, h, t:t + 1]
                    if t == 0:
                        ins = nc.vector.tensor_scalar(acc[k.p][:, h], window, w, None, ALU.mult)
                    else:
                        dve.wait_ge(conv_seq, k.c * VTAPS + i - 1)
                        ins = nc.vector.scalar_tensor_tensor(acc[k.p][:, h], window, w, acc[k.p][:, h], ALU.mult, ALU.add)
                    ins.then_inc(conv_seq, 1)

            def center(k):
                dve.wait_ge(mu_ready, k.q + 1)
                dve.wait_ge(x4_ready, k.q + 1)
                dve.wait_ge(xg_ready, k.q)
                mu = mean_ps[:].unsqueeze(1).broadcast_to([P, 2, NPX])
                nc.vector.tensor_tensor(xn[k.p][:], x4[k.p][:], mu, ALU.subtract).then_inc(xc_ready, 1)

            def normalize(k):
                dve.wait_ge(r_ready, k.q + 1)
                dve.wait_ge(xc_ready, k.q + 1)
                if k.is_first:
                    dve.wait_ge(xz_ready, k.q * 4)
                else:
                    dve.wait_ge(xz_ready, k.q * 4 - 4)
                r = rstd[:, 1:2, :].broadcast_to([P, 2, NPX])
                nc.vector.tensor_tensor(xg[k.p][:], xn[k.p][:], r, ALU.mult).then_inc(xg_ready, 1)

            def step(k):
                now, older = k.back(1), k.back(3)
                if now.is_real:
                    center(now)
                if older.is_convolved:
                    conv(older, 0, 14)
                if now.is_real:
                    normalize(now)
                if older.is_convolved:
                    conv(older, 14, 16)

            image_loop(dve, step, LATE - 1)

        @block.scalar
        def _(act):
            act.wait_ge(w_ready, 1)
            act.wait_ge(w_loaded, DMA * len(loads))
            act.wait_ge(w_folded, 1)

            def square(k):
                act.wait_ge(xc_ready, k.q + 1)
                act.wait_ge(sq_summed, k.q)
                nc.scalar.activation(sq[:], xn[k.p][:], ACT.Square).then_inc(sq_ready, 1)

            def gate_of(k):
                nc.scalar.preload_act_table_set("sigmoid_and_others")
                act.wait_ge(gate_sum, k.q + 1)
                act.wait_ge(gated, k.q)
                nc.scalar.activation(gate[:], gate_ps[:], ACT.Sigmoid, bias=b_sa[:]).then_inc(gate_ready, 1)

            def deviation(k):
                nc.scalar.preload_act_table_set("natural_log_exp_and_others")
                act.wait_ge(var_ready, k.q + 1)
                act.wait_ge(xg_ready, k.q)
                nc.scalar.activation(rstd[:, 0], var_ps[:], ACT.Ln, bias=consts[:, 0:1]).then_inc(ln_done, 1)
                act.wait_ge(ln_done, k.q + 1)
                nc.scalar.activation(rstd[:, 1], rstd[:, 0], ACT.Exp, scale=-0.5, bias=consts[:, 1:2]).then_inc(r_ready, 1)

            def rows_above(k):
                if k.is_first:
                    act.wait_ge(zeros_ready, k.b * 2 + 1)
                    return
                act.wait_ge(conv_seq, k.back(1).c * VTAPS)
                act.wait_ge(prod_ready, k.back(1).c)
                act.wait_ge(raw_ready, k.c)
                nc.scalar.copy(raw[k.p][:, :, 0:2, 1:WW + 1],
                               raw[1 - k.p][:, :, ROWS:ROWS + 2, 1:WW + 1]).then_inc(carried, 1)
                if k.is_last:
                    act.wait_ge(zeros_ready, k.b * 2 + 2)
                    act.wait_ge(carried, (k.b + 1) * CHUNKS)
                    act.sem_inc(raw_ready, 1)

            def take_x(k):
                for t in range(2):
                    act.wait_ge(xz_ready, k.q * 4 + t + 1)
                    nc.scalar.activation(raw[k.p][:, t, 2:ROWS + 2, 1:WW + 1],
                                         xz_ps[t][:].rearrange("p (r w) -> p r w", w=WW), ACT.Identity,
                                         bias=bias_in[:, t:t + 1]).then_inc(x_evac, 1)
                act.wait_ge(x_evac, k.q * 2 + 2)
                act.sem_inc(raw_ready, 1)

            def last_tap(k):
                act.wait_ge(raw_ready, k.c + 1)
                act.wait_ge(tail_added, k.c if k.is_first else k.c - 1)
                dy, dx = TAPS[8]
                for h in range(2):
                    last = nc.scalar.activation(prod[k.p][:, h], raw[k.p][:, h, dy:dy + ROWS, dx:dx + WW], ACT.Identity,
                                                scale=cw[:, h, 8:9], bias=consts[:, 1:2])
                last.then_inc(prod_ready, 1)

            def silu_u(k):
                act.wait_ge(tail_added, k.c + 1)
                act.wait_ge(u_stored[k.p], k.c_pairs * U_DMAS * DMA)
                for h in range(2):
                    last = nc.scalar.activation(u[k.p][:, h], acc[k.p][:, h], ACT.Silu, bias=cb[:, h:h + 1])
                last.then_inc(u_ready, 1)

            def silu_z(k):
                act.wait_ge(z_stored[k.p], k.pairs * DMA)
                for t in range(2):
                    act.wait_ge(xz_ready, k.q * 4 + t + 3)
                    last = nc.scalar.activation(sz[k.p][:, t], xz_ps[2 + t][:], ACT.Silu, bias=bias_in[:, 2 + t:3 + t])
                last.then_inc(z_ready, 1)

            def take_xd(k):
                act.wait_ge(xd_ready, k.c + 1)
                act.wait_ge(u_stored[k.p], k.c_pairs * U_DMAS * DMA)
                nc.scalar.copy(xd[k.p][:], xd_ps[0:NDT + NBC, :]).then_inc(xd_evac, 1)

            def step(k):
                if k.is_first:
                    gate_of(k)
                if k.back(1).is_real:
                    square(k.back(1))
                if k.back(2).is_convolved:
                    rows_above(k.back(2))
                if k.back(3).is_convolved:
                    last_tap(k.back(3))
                if k.back(2).is_real:
                    take_x(k.back(2))
                if k.back(1).is_real:
                    deviation(k.back(1))
                if k.back(-1).is_real:
                    gate_of(k.back(-1))
                if k.back(4).is_convolved or k.back(2).is_real:
                    nc.scalar.preload_act_table_set("silu_and_others")
                if k.back(4).is_convolved:
                    silu_u(k.back(4))
                if k.back(2).is_real:
                    silu_z(k.back(2))
                if k.back(4).is_convolved:
                    take_xd(k.back(4))

            image_loop(act, step, LATE, out=2)

        @block.tensor
        def _(pe):
            pe.wait_ge(w_ready, 1)
            pe.wait_ge(w_loaded, DMA * len(loads))
            for t in range(4):
                for h in range(2):
                    last = nc.tensor.matmul(xd_ps[0:P, t:t + 1], w_in[:, h, P * t:P * t + P], ln_gb[:, h, 1:2],
                                            start=(h == 0), stop=(h == 1))
            last.then_inc(bias_ready, 1)
            pe.wait_ge(w_folded, 1)

            def project(k, outs):
                pe.wait_ge(xg_ready, k.q + 1)
                for t in outs:
                    if t == 0:
                        pe.wait_ge(x_evac, k.q * 2)
                    if t == 2:
                        pe.wait_ge(z_ready, k.q)
                    for h in range(2):
                        last = nc.tensor.matmul(xz_ps[t][:], w_in[:, h, P * t:P * t + P], xg[k.p][:, h],
                                                start=(h == 0), stop=(h == 1))
                    last.then_inc(xz_ready, 1)

            def sum_taps(k):
                pe.wait_ge(in_loaded[k.p], (k.pairs + 1) * IN_DMAS * DMA)
                pe.wait_ge(gate_ready, k.q)
                nc.tensor.matmul(gate_ps[:], ones[:], taps[k.p][:], start=True, stop=True).then_inc(gate_sum, 1)

            def mean(k):
                pe.wait_ge(x4_summed, k.q + 1)
                pe.wait_ge(xc_ready, k.q)
                nc.tensor.matmul(mean_ps[:], mean_w[:], x4_sum[:], start=True, stop=True).then_inc(mu_ready, 1)

            def variance(k):
                pe.wait_ge(sq_summed, k.q + 1)
                pe.wait_ge(r_ready, k.q)
                nc.tensor.matmul(var_ps[:], mean_w[:], sq_sum[:], start=True, stop=True).then_inc(var_ready, 1)

            def x_proj(k):
                pe.wait_ge(u_ready, k.c + 1)
                pe.wait_ge(xd_evac, k.c)
                for h in range(2):
                    last = nc.tensor.matmul(xd_ps[0:NDT + NBC, :], w_x[:, h], u[k.p][:, h].rearrange("p r w -> p (r w)"),
                                            start=(h == 0), stop=(h == 1))
                last.then_inc(xd_ready, 1)

            def step(k):
                if k.is_first:
                    sum_taps(k)
                if k.back(2).is_real:
                    project(k.back(2), (0, 1))
                if k.back(1).is_real:
                    variance(k.back(1))
                if k.back(-1).is_real:
                    sum_taps(k.back(-1))
                if k.back(2).is_real:
                    project(k.back(2), (2, 3))
                if k.is_real:
                    mean(k)
                if k.back(4).is_convolved:
                    x_proj(k.back(4))

            image_loop(pe, step, LATE, out=2)


SPLIT = 1024
PAIRS = B // 2


def split_and_turn(nc, d):
    with ExitStack() as ctx:
        def sb(name, shape, dt=FP32):
            return ctx.enter_context(nc.sbuf_tensor("t_" + name, shape, dt))

        sems = []
        ctx.callback(nc.all_engine_barrier)
        ctx.callback(nc.clear_and_free_semaphores, sems)

        def sem(name):
            sems.append(nc.alloc_semaphore("t_" + name))
            return sems[-1]

        rows = sb("rows", [128, L])
        dts = sb("dts", [2 * B * RANK, L])
        flat = [sb(f"flat{p}", [128, SPLIT]) for p in range(2)]
        rest = [sb(f"rest{p}", [128, SPLIT]) for p in range(2)]
        parts = [sb(f"parts{p}", [128, 3, SPLIT], BF16) for p in range(2)]
        dtt = [sb(f"dtt{p}", [2 * B * RANK, SPLIT]) for p in range(2)]

        loaded = sem("loaded")
        dt_loaded = sem("dt_loaded")
        by_row = [sem(f"by_row{p}") for p in range(2)]
        by_col = [sem(f"by_col{p}") for p in range(2)]
        high = [sem(f"high{p}") for p in range(2)]
        rested = [sem(f"rested{p}") for p in range(2)]
        middle = [sem(f"middle{p}") for p in range(2)]
        low = [sem(f"low{p}") for p in range(2)]
        turned = [sem(f"turned{p}") for p in range(2)]
        stored = [sem(f"stored{p}") for p in range(2)]
        dt_stored = [sem(f"dt_stored{p}") for p in range(2)]
        STORES = 12
        COLS = SPLIT // HH
        by_order = d["bc"].rearrange("(e g) b r n -> g e (b r) n", g=2)
        dt_order = d["dts"].rearrange("(e g) b r n -> g e (b r) n", g=2)[1]
        turn = lambda x: x.rearrange("p (h w) -> p w h", w=WW)

        block = ctx.enter_context(nc.Block())

        def steps(eng, step):
            with eng.Fori(0, L // SPLIT // 2) as j:
                step(2 * j, 0, j)
                step(2 * j + 1, 1, j)

        @block.sync
        def _(sp):
            for g in range(2):
                for e in range(2):
                    at = 64 * g + 32 * e
                    sp.dma_start(rows[at:at + 32, :], by_order[g, e]).then_inc(loaded, DMA)
            for e in range(2):
                at = B * RANK * e
                sp.dma_start(dts[at:at + B * RANK, :], dt_order[e]).then_inc(dt_loaded, DMA)

            def step(n, p, j):
                px = bass.ds(n * SPLIT, SPLIT)
                sp.wait_ge(low[p], j + 1)
                sp.wait_ge(middle[p], j + 1)
                sp.wait_ge(high[p], j + 1)
                for g in range(2):
                    for e in range(2):
                        at = 64 * g + 32 * e
                        for k in range(3):
                            dst = d["bcs"][2 * e + g].rearrange("q (k r) n -> k q r n", k=3)[k]
                            sp.dma_start(dst[:, :, px], parts[p][at:at + 32, k, :]).then_inc(stored[p], DMA)
                sp.wait_ge(turned[p], j + 1)
                for e in range(2):
                    at = B * RANK * e
                    sp.dma_start(dt_order[e][:, px], dtt[p][at:at + B * RANK, :]).then_inc(dt_stored[p], DMA)

            steps(sp, step)
            for p in range(2):
                sp.wait_ge(stored[p], L // SPLIT // 2 * STORES * DMA)
                sp.wait_ge(dt_stored[p], L // SPLIT // 2 * 2 * DMA)

        @block.gpsimd
        def _(pool):
            pool.wait_ge(dt_loaded, 2 * DMA)

            def step(n, p, j):
                pool.wait_ge(dt_stored[p], j * 2 * DMA)
                out = dtt[p][:].rearrange("p (w h) -> p w h", h=HH)
                nc.gpsimd.tensor_copy(out, turn(dts[:])[:, bass.ds(n * COLS, COLS), :]).then_inc(turned[p], 1)

            steps(pool, step)

        @block.scalar
        def _(act):
            act.wait_ge(loaded, 4 * DMA)

            def step(n, p, j):
                act.wait_ge(rested[p], j)
                nc.scalar.copy(flat[p][0:64, :], rows[0:64, bass.ds(n * SPLIT, SPLIT)]).then_inc(by_row[p], 1)
                act.wait_ge(rested[p], j + 1)
                act.wait_ge(stored[p], j * STORES * DMA)
                nc.scalar.copy(parts[p][:, 1, :], rest[p][:]).then_inc(middle[p], 1)

            steps(act, step)

        @block.vector
        def _(dve):
            dve.wait_ge(loaded, 4 * DMA)

            def step(n, p, j):
                dve.wait_ge(rested[p], j)
                nc.vector.tensor_copy(flat[p][64:128, :].rearrange("p (w h) -> p w h", h=HH),
                                      turn(rows[64:128, :])[:, bass.ds(n * COLS, COLS), :]).then_inc(by_col[p], 1)
                dve.wait_ge(by_row[p], j + 1)
                dve.wait_ge(by_col[p], j + 1)
                dve.wait_ge(stored[p], j * STORES * DMA)
                nc.vector.tensor_copy(parts[p][:, 0, :], flat[p][:]).then_inc(high[p], 1)
                dve.wait_ge(high[p], j + 1)
                dve.wait_ge(low[p], j)
                dve.wait_ge(middle[p], j)
                nc.vector.tensor_tensor(rest[p][:], flat[p][:], parts[p][:, 0, :], ALU.subtract).then_inc(rested[p], 1)
                dve.wait_ge(middle[p], j + 1)
                dve.wait_ge(rested[p], j + 1)
                nc.vector.tensor_tensor(parts[p][:, 2, :], rest[p][:], parts[p][:, 1, :], ALU.subtract).then_inc(low[p], 1)

            steps(dve, step)


UNIT = 512
UNITS = L // UNIT
GROUPS = UNITS // 4
TILES = B * C // 128
ORDER = [(0, False, False), (1, True, False), (3, True, True), (2, False, True)]
EXP_CAP = 2.0 ** 63
LOG_MAX = 88.72283
TINY = 2.0 ** -22
RATE_MAX = 2.0 ** 120
DT_MIN = 2.0 ** -113


def selective_scans(nc, d):
    with ExitStack() as ctx:
        def sb(name, shape, dt=FP32):
            return ctx.enter_context(nc.sbuf_tensor("d_" + name, shape, dt))

        def ps(name, shape):
            return ctx.enter_context(nc.psum_tensor("d_" + name, shape, FP32))

        sems = []
        ctx.callback(nc.all_engine_barrier)
        ctx.callback(nc.clear_and_free_semaphores, sems)

        def sem(name):
            sems.append(nc.alloc_semaphore("d_" + name))
            return sems[-1]

        def two(name):
            return [sem(f"{name}{p}") for p in range(2)]

        u = sb("u", [128, L])
        y = sb("y", [128, L])
        ident = sb("ident", [128, 128])
        sel = sb("sel", [6 * 2 * STATES, 2 * STATES, 128], BF16)
        w_dt = sb("w_dt", [2 * RANK, DIRS, 128])
        dt_bias = sb("dt_bias", [128, DIRS])
        a_log = sb("a_log", [128, DIRS * STATES])
        a = sb("a", [128, DIRS * STATES])
        skip = sb("skip", [128, DIRS])
        skip_sum = sb("skip_sum", [128, 1])
        zero = sb("zero", [128, 2])
        dts = [sb(f"dts{h}", [2 * RANK, 2 * UNIT]) for h in range(2)]
        bcs = [sb(f"bcs{h}", [6 * 2 * STATES, 2 * UNIT], BF16) for h in range(2)]
        ex = [sb(f"ex{p}", [128, UNIT]) for p in range(2)]
        dt = [sb(f"dt{p}", [128, UNIT]) for p in range(2)]
        du = [sb(f"du{p}", [128, UNIT]) for p in range(2)]
        da = [sb(f"da{p}", [128, STATES, UNIT]) for p in range(2)]
        h = [sb(f"h{p}", [128, STATES, UNIT]) for p in range(2)]
        hc = [sb(f"hc{p}", [128, STATES, UNIT]) for p in range(2)]
        sel32 = hc[0][0:6 * 2 * STATES, 0:2].rearrange("p a (b c) -> p (a b) c", c=128)

        raw_ps = ps("raw_ps", [128, UNIT])
        b_ps = [ps(f"b_ps{n}", [128, UNIT]) for n in range(STATES)]
        c_ps = [ps(f"c_ps{p}", [128, UNIT]) for p in range(2)]
        y_ps = ps("y_ps", [128, UNIT])

        const_ready = sem("const_ready")
        ident_loaded = sem("ident_loaded")
        w_loaded = sem("w_loaded")
        u_begun = sem("u_begun")
        u_loaded = sem("u_loaded")
        a_capped = sem("a_capped")
        sel_ready = sem("sel_ready")
        a_exp = sem("a_exp")
        a_ready = sem("a_ready")
        y_stored = sem("y_stored")
        xd_loaded = two("xd_loaded")
        raw_ready = two("raw_ready")
        e_ready = two("e_ready")
        clipped = two("clipped")
        ln_ready = two("ln_ready")
        dt_max = two("dt_max")
        dt_ready = two("dt_ready")
        du_ready = two("du_ready")
        da_ready = two("da_ready")
        b_ready = two("b_ready")
        dbu_ready = two("dbu_ready")
        scanned = two("scanned")
        c_ready = two("c_ready")
        cs_ready = two("cs_ready")
        hc_ready = two("hc_ready")
        y_summed = two("y_summed")
        y_begun = two("y_begun")
        y_added = two("y_added")

        W_DMAS, HALF, U_CUT = 5, UNITS // 2, L // 4
        uv = d["u"].rearrange("b c n -> (b c) n")
        yv = d["ys"].rearrange("b c n -> (b c) n")

        class Unit:

            def __init__(self, t, o, j, i):
                self.t, self.o, self.j, self.i, self.p = t, o, j, i, i % 2
                self.first = isinstance(j, int) and j == 0 and i == 0
                self.direction, self.columns, self.reverse = ORDER[o]
                self.n = (t * len(ORDER) + o) * HALF + j * 2 + i // 2
                self.k = j * -4 + (UNITS - 1 - i) if self.reverse else j * 4 + i
                self.groups = (t * len(ORDER) + o) * GROUPS + j
                self.very_first = self.first and o == 0

            def following(self):
                if self.i < 3:
                    return Unit(self.t, self.o, self.j, self.i + 1)
                if isinstance(self.j, int) and self.j == GROUPS - 1:
                    return Unit(self.t, self.o + 1, 0, 0) if self.o + 1 < len(ORDER) else None
                return Unit(self.t, self.o, self.j + 1, 0)

            def loaded(self, x):
                at = (1 - self.p if self.reverse else self.p) * UNIT
                return x[self.i // 2][:, at:at + UNIT]

            def states(self, k):
                return self.n * STATES + k

            def before(self, k):
                if self.very_first:
                    return self.n * STATES
                return self.n * STATES + (k if self.p else k - STATES)

            def where(self, x):
                if self.columns:
                    return x[:].rearrange("p (h w) -> p w h", w=WW)[:, bass.ds(self.k * (UNIT // HH), UNIT // HH), :]
                return x[:, bass.ds(self.k * UNIT, UNIT)]

            def begun(self, k=0):
                return (self.t + self.o) * HALF + (self.j * 2 + self.i // 2 + k)

            def added(self, k=0):
                return (self.t * 3 + (self.o - 1)) * HALF + (self.j * 2 + self.i // 2 + k)

            def shaped(self, x):
                return x.rearrange("p (w h) -> p w h", h=HH) if self.columns else x

            def run(self, x):
                return x[:, ::-1] if self.reverse else x

        def units(eng, body, start, end):
            with eng.Fori(0, PAIRS) as pair:
                with eng.Fori(0, TILES // PAIRS) as third:
                    t = pair * (TILES // PAIRS) + third
                    start(t, pair, third)
                    last = None
                    for o in range(len(ORDER)):
                        def group(j, before, after):
                            own = [before, *(Unit(t, o, j, i) for i in range(4)), after]
                            for i in range(4):
                                body(*own[i:i + 3])
                            return own[4]

                        group(0, last, Unit(t, o, 1, 0))
                        with eng.Fori(1, GROUPS - 1) as j:
                            group(j, Unit(t, o, j - 1, 3), Unit(t, o, j + 1, 0))
                        last = group(GROUPS - 1, Unit(t, o, GROUPS - 2, 3),
                                     Unit(t, o + 1, 0, 0) if o + 1 < len(ORDER) else None)
                    end(t, last)

        block = ctx.enter_context(nc.Block())

        @block.sync
        def _(sp):
            sp.dma_start(ident[:], d["ident"]).then_inc(ident_loaded, DMA)

            with sp.Fori(0, PAIRS) as pair:
                with sp.Fori(0, TILES // PAIRS) as third:
                    t = pair * (TILES // PAIRS) + third
                    sp.wait_ge(y_added[1], t * 3 * HALF)
                    sp.wait_ge(y_added[0], t * 3 * HALF)
                    sp.dma_start(w_dt[:], d["w_dt"][third]).then_inc(w_loaded, DMA)
                    sp.dma_start(dt_bias[:], d["dt_bias"][third]).then_inc(w_loaded, DMA)
                    sp.dma_start(a_log[:], d["a_log"][third]).then_inc(w_loaded, DMA)
                    sp.dma_start(skip[:], d["skip"][third]).then_inc(w_loaded, DMA)
                    sp.dma_start(sel32, d["sel"][third]).then_inc(w_loaded, DMA)
                    sp.dma_start(u[:, 0:U_CUT], uv[bass.ds(t * 128, 128), 0:U_CUT]).then_inc(u_begun, DMA)

                    def store(x):
                        px = bass.ds(x.k * UNIT, UNIT)
                        sp.wait_ge(y_added[x.p], x.added(1))
                        sp.dma_start(yv[bass.ds(t * 128, 128), px], y[:, px]).then_inc(y_stored, DMA)

                    def load(o, j, half):
                        x = Unit(t, o, j, 2 * half + 1)
                        k = x.k if x.reverse else j * 4 + 2 * half
                        px = bass.ds(k * UNIT, 2 * UNIT)
                        if not (o == 0 and isinstance(j, int) and j == 0):
                            sp.wait_ge(c_ready[1], x.states(0) - STATES)
                        src = d["dts"][x.direction, bass.ds(pair * 2, 2), :, px]
                        sp.dma_start(dts[half][:], src.rearrange("i r n -> (i r) n")).then_inc(xd_loaded[half], DMA)
                        sp.dma_start(bcs[half][:], d["bcs"][x.direction, pair, :, px]).then_inc(xd_loaded[half], DMA)

                    for o in range(len(ORDER)):
                        stores = o == len(ORDER) - 1
                        for half in range(2):
                            load(o, 0, half)
                        if o == 0:
                            for at in range(U_CUT, L, U_CUT):
                                sp.dma_start(u[:, at:at + U_CUT],
                                             uv[bass.ds(t * 128, 128), at:at + U_CUT]).then_inc(u_loaded, DMA)
                        with sp.Fori(1, GROUPS) as j:
                            for half in range(2):
                                load(o, j, half)
                                if stores:
                                    store(Unit(t, o, j - 1, 2 * half))
                                    store(Unit(t, o, j - 1, 2 * half + 1))
                        if stores:
                            for i in range(4):
                                store(Unit(t, o, GROUPS - 1, i))
            sp.wait_ge(y_stored, TILES * UNITS * DMA)

        @block.gpsimd
        def _(pool):
            nc.gpsimd.memset(zero[:, 0:1], 0.0)
            nc.gpsimd.memset(zero[:, 1:2], 1.0).then_inc(const_ready, 1)

            def start(t, pair, third):
                pool.wait_ge(u_begun, (t + 1) * DMA)
                times_u(Unit(t, 0, 0, 0))

            def times_u(x):
                pool.wait_ge(dt_ready[x.p], x.n + 1)
                pool.wait_ge(dbu_ready[x.p], x.states(0))
                nc.gpsimd.tensor_tensor(x.shaped(du[x.p][:]), x.shaped(dt[x.p][:]), x.where(u),
                                        ALU.mult).then_inc(du_ready[x.p], 1)

            def times_c(x, n):
                pool.wait_ge(scanned[x.p], x.states(n + 1))
                pool.wait_ge(cs_ready[x.p], x.states(n + 1))
                nc.gpsimd.tensor_tensor(hc[x.p][:, n], h[x.p][:, n], hc[x.p][:, n], ALU.mult).then_inc(hc_ready[x.p], 1)

            def body(before, x, after):
                times_c(x, 0)
                times_c(x, 1)
                if x.o == 0 and x.i == 3 and isinstance(x.j, int) and x.j == 0:
                    pool.wait_ge(u_loaded, (x.t + 1) * 3 * DMA)
                if after:
                    times_u(after)
                times_c(x, 2)
                times_c(x, 3)

            units(pool, body, start, lambda t, last: None)

        @block.vector
        def _(dve):
            dve.wait_ge(const_ready, 1)

            def clip(x):
                dve.wait_ge(e_ready[x.p], x.n + 1)
                nc.vector.tensor_scalar(ex[x.p][:], ex[x.p][:], EXP_CAP, DT_MIN, ALU.min, ALU.max).then_inc(clipped[x.p], 1)

            def softplus(x):
                dve.wait_ge(ln_ready[x.p], x.n + 1)
                o = x.direction
                nc.vector.scalar_tensor_tensor(dt[x.p][:], raw_ps[:], dt_bias[:, o:o + 1], dt[x.p][:],
                                               ALU.add, ALU.max).then_inc(dt_max[x.p], 1)

            def softplus_tiny(x):
                dve.wait_ge(dt_max[x.p], x.n + 1)
                nc.vector.scalar_tensor_tensor(dt[x.p][:], dt[x.p][:], TINY, ex[x.p][:],
                                               ALU.max, ALU.min).then_inc(dt_ready[x.p], 1)

            def times_b(x, n):
                dve.wait_ge(b_ready[x.p], x.states(n + 1))
                dve.wait_ge(du_ready[x.p], x.n + 1)
                nc.vector.tensor_tensor(b_ps[n][:], b_ps[n][:], du[x.p][:], ALU.mult).then_inc(dbu_ready[x.p], 1)

            def scan(x, n):
                dve.wait_ge(dbu_ready[x.p], x.states(n + 1))
                dve.wait_ge(da_ready[x.p], x.states(n + 1))
                dve.wait_ge(hc_ready[x.p], x.states(0))
                initial = 0.0
                if not x.first:
                    dve.wait_ge(scanned[1 - x.p], x.before(n + 1))
                    end = 0 if x.reverse else UNIT - 1
                    initial = h[1 - x.p][:, n, end:end + 1]
                nc.vector.tensor_tensor_scan(x.run(h[x.p][:, n]), x.run(da[x.p][:, n]), x.run(b_ps[n][:]), initial,
                                             ALU.mult, ALU.add).then_inc(scanned[x.p], 1)

            def begin_y(x):
                if not x.o:
                    dve.wait_ge(y_summed[x.p], x.states(STATES))
                    nc.vector.scalar_tensor_tensor(x.where(y), x.where(u), skip_sum[:], y_ps[:], ALU.mult,
                                                   ALU.add).then_inc(y_begun[x.p], 1)

            def start(t, pair, third):
                dve.wait_ge(w_loaded, (t + 1) * W_DMAS * DMA)
                dve.wait_ge(u_begun, (t + 1) * DMA)
                dve.wait_ge(y_stored, t * UNITS * DMA)
                nc.vector.tensor_scalar(a_log[:], a_log[:], LOG_MAX, None, ALU.min).then_inc(a_capped, 1)
                nc.vector.tensor_copy(sel[:], sel32).then_inc(sel_ready, 1)
                nc.vector.reduce_sum(skip_sum[:], skip[:], axis=AXX)
                dve.wait_ge(a_exp, t + 1)
                nc.vector.tensor_scalar(a[:], a[:], RATE_MAX, -1.0, ALU.min, ALU.mult).then_inc(a_ready, 1)
                dve.wait_ge(a_ready, t + 1)
                x = Unit(t, 0, 0, 0)
                clip(x)
                softplus(x)
                softplus_tiny(x)

            def body(before, x, after):
                if x.o == 0 and x.i == 3 and isinstance(x.j, int) and x.j == 0:
                    dve.wait_ge(u_loaded, (x.t + 1) * 3 * DMA)
                times_b(x, 0)
                times_b(x, 1)
                scan(x, 0)
                if after:
                    clip(after)
                scan(x, 1)
                times_b(x, 2)
                times_b(x, 3)
                if after:
                    softplus(after)
                    softplus_tiny(after)
                scan(x, 2)
                if before:
                    begin_y(before)
                scan(x, 3)

            units(dve, body, start, lambda t, last: None)

        @block.scalar
        def _(act):
            act.wait_ge(const_ready, 1)
            nc.scalar.preload_act_table_set("natural_log_exp_and_others")

            def e_of(x):
                act.wait_ge(raw_ready[x.p], x.n + 1)
                act.wait_ge(dt_ready[x.p], x.n)
                o = x.direction
                nc.scalar.activation(ex[x.p][:], raw_ps[:], ACT.Exp, bias=dt_bias[:, o:o + 1]).then_inc(e_ready[x.p], 1)

            def ln_of(x):
                act.wait_ge(clipped[x.p], x.n + 1)
                act.wait_ge(du_ready[x.p], x.n)
                act.wait_ge(da_ready[x.p], x.states(0))
                nc.scalar.activation(dt[x.p][:], ex[x.p][:], ACT.Ln, bias=zero[:, 1:2]).then_inc(ln_ready[x.p], 1)

            def decay(x, n):
                act.wait_ge(dt_ready[x.p], x.n + 1)
                act.wait_ge(scanned[x.p], x.states(0))
                o = x.direction * STATES + n
                nc.scalar.activation(da[x.p][:, n], dt[x.p][:], ACT.Exp, scale=a[:, o:o + 1],
                                     bias=zero[:, 0:1]).then_inc(da_ready[x.p], 1)

            def copy_c(x, n):
                act.wait_ge(c_ready[x.p], x.states(n + 1))
                act.wait_ge(y_summed[x.p], x.states(0))
                nc.scalar.copy(hc[x.p][:, n], c_ps[n % 2][:]).then_inc(cs_ready[x.p], 1)

            def take_y(x):
                if x.o:
                    act.wait_ge(y_summed[x.p], x.states(STATES))
                    nc.scalar.copy(x.where(y), x.shaped(y_ps[:])).then_inc(y_added[x.p], 1)

            def start(t, pair, third):
                act.wait_ge(w_loaded, (t + 1) * W_DMAS * DMA)
                act.wait_ge(a_capped, t + 1)
                nc.scalar.activation(a[:], a_log[:], ACT.Exp, bias=zero[:, 0:1]).then_inc(a_exp, 1)
                act.wait_ge(a_ready, t + 1)
                x = Unit(t, 0, 0, 0)
                e_of(x)
                ln_of(x)

            def body(before, x, after):
                if after:
                    e_of(after)
                decay(x, 0)
                decay(x, 1)
                copy_c(x, 0)
                if after:
                    ln_of(after)
                copy_c(x, 1)
                decay(x, 2)
                if before:
                    take_y(before)
                decay(x, 3)
                copy_c(x, 2)
                copy_c(x, 3)

            units(act, body, start, lambda t, last: take_y(last))

        @block.tensor
        def _(pe):
            pe.wait_ge(ident_loaded, DMA)

            def raw_dt(x):
                pe.wait_ge(xd_loaded[x.i // 2], (x.groups + 1) * 2 * DMA)
                pe.wait_ge(dt_max[1 - x.p], x.n if x.p == 0 else x.n + 1)
                nc.tensor.matmul(raw_ps[:], w_dt[:, x.direction], x.loaded(dts), start=True,
                                 stop=True).then_inc(raw_ready[x.p], 1)

            def spread_b(x, n):
                pe.wait_ge(scanned[1 - x.p], x.before(n + 1))
                nc.tensor.matmul(b_ps[n][:], sel[:, n], x.loaded(bcs), start=True, stop=True).then_inc(b_ready[x.p], 1)

            def spread_c(x, n):
                if n < 2:
                    pe.wait_ge(cs_ready[1 - x.p], x.before(n + 3))
                else:
                    pe.wait_ge(cs_ready[x.p], x.states(n - 1))
                nc.tensor.matmul(c_ps[n % 2][:], sel[:, STATES + n], x.loaded(bcs), start=True,
                                 stop=True).then_inc(c_ready[x.p], 1)

            def sum_y(x, n):
                if n == 0:
                    if x.o == 0 or x.o == 1 and x.first:
                        pe.wait_ge(y_begun[1 - x.p], x.begun(x.p))
                    else:
                        pe.wait_ge(y_added[1 - x.p], x.added(x.p))
                    if x.o:
                        if x.first and x.o == 1:
                            pe.wait_ge(y_begun[0], x.begun())
                        elif x.first:
                            pe.wait_ge(y_added[0], x.added())
                        nc.tensor.matmul(y_ps[:], ident[:], x.where(y), start=True, stop=False)
                pe.wait_ge(hc_ready[x.p], x.states(n + 1))
                nc.tensor.matmul(y_ps[:], ident[:], hc[x.p][:, n], start=(n == 0 and not x.o),
                                 stop=(n == STATES - 1)).then_inc(y_summed[x.p], 1)

            def start(t, pair, third):
                pe.wait_ge(w_loaded, (t + 1) * W_DMAS * DMA)
                pe.wait_ge(sel_ready, t + 1)
                x = Unit(t, 0, 0, 0)
                raw_dt(x)
                spread_b(x, 0)
                spread_b(x, 1)
                raw_dt(x.following())

            def body(before, x, after):
                spread_b(x, 2)
                spread_b(x, 3)
                spread_c(x, 0)
                spread_c(x, 1)
                if before:
                    sum_y(before, 2)
                    sum_y(before, 3)
                spread_c(x, 2)
                spread_c(x, 3)
                if after:
                    spread_b(after, 0)
                    spread_b(after, 1)
                    if after.following():
                        raw_dt(after.following())
                sum_y(x, 0)
                sum_y(x, 1)

            def end(t, last):
                sum_y(last, 2)
                sum_y(last, 3)

            units(pe, body, start, end)


def output_projection(nc, d):
    with ExitStack() as ctx:
        def sb(name, shape, dt=FP32):
            return ctx.enter_context(nc.sbuf_tensor("e_" + name, shape, dt))

        def ps(name, shape):
            return ctx.enter_context(nc.psum_tensor("e_" + name, shape, FP32))

        sems = []
        ctx.callback(nc.all_engine_barrier)
        ctx.callback(nc.clear_and_free_semaphores, sems)

        def sem(name):
            sems.append(nc.alloc_semaphore("e_" + name))
            return sems[-1]

        mean_w = sb("mean_w", [P, P])
        ln_gb = sb("ln_gb", [P, 2, 2])
        w_out = sb("w_out", [P, 2, C])
        consts = sb("consts", [P, 2])
        DEEP = 4
        y = [sb(f"y{p}", [P, 2, NPX]) for p in range(DEEP)]
        sz = [sb(f"sz{p}", [P, 2, NPX]) for p in range(DEEP)]
        x4 = [sb(f"x4{p}", [P, 2, NPX]) for p in range(DEEP)]
        yn = [sb(f"yn{p}", [P, 2, NPX]) for p in range(DEEP)]
        yz = [sb(f"yz{p}", [P, 2, NPX]) for p in range(DEEP)]
        out = [sb(f"out{p}", [P, 2, NPX]) for p in range(DEEP)]
        y_sum = sb("y_sum", [P, NPX])
        sq = sb("sq", [P, 2, NPX])
        sq_sum = sb("sq_sum", [P, NPX])
        rstd = sb("rstd", [P, 2, NPX])
        stat_ps = [ps(f"stat_ps{i}", [P, NPX]) for i in range(2)]
        o_ps = [ps(f"o_ps{p}", [P, 2, NPX]) for p in range(2)]

        w_loaded = sem("w_loaded")
        w_ready = sem("w_ready")
        y_loaded = [sem(f"y_loaded{p}") for p in range(DEEP)]
        zx_loaded = [sem(f"zx_loaded{p}") for p in range(DEEP)]
        stored = [sem(f"stored{p}") for p in range(DEEP)]
        y_summed = sem("y_summed")
        sq_summed = sem("sq_summed")
        mu_ready = sem("mu_ready")
        yc_ready = sem("yc_ready")
        sq_ready = sem("sq_ready")
        var_ready = sem("var_ready")
        ln_done = sem("ln_done")
        r_ready = sem("r_ready")
        yr_done = sem("yr_done")
        yz_ready = sem("yz_ready")
        o_ready = sem("o_ready")
        out_ready = sem("out_ready")

        TOTAL = B * CHUNKS
        loads = [(ln_gb, d["ln4_gb"]), (w_out, d["w_out"])]
        yv, zv, x4v, ov = (d[k].rearrange("b (h p) n -> b p h n", h=2) for k in ("ys", "sz", "x4", "out"))

        class Chunk:

            def __init__(self, j, i):
                self.j, self.i, self.p = j, i, i % DEEP
                self.q = DEEP * j + i
                self.turn = j + i // DEEP
                self.is_real = not isinstance(j, int) or 0 <= self.q < TOTAL
                self.is_first = isinstance(j, int) and self.q == 0

            def back(self, k):
                return Chunk(self.j, self.i - k)

        def chunk_loop(eng, step):
            for i in range(DEEP):
                step(Chunk(0, i))
            with eng.Fori(1, TOTAL // DEEP) as j:
                for i in range(DEEP):
                    step(Chunk(j, i))
            for i in range(DEEP):
                step(Chunk(0, TOTAL + i))

        block = ctx.enter_context(nc.Block())

        @block.sync
        def _(sp):
            for dst, src in loads:
                sp.dma_start(dst[:], src).then_inc(w_loaded, DMA)

            def load_y(b, s, p, waits=True):
                if waits:
                    sp.wait_ge(yc_ready, b * CHUNKS + s - DEEP + 1)
                sp.dma_start(y[p][:], yv[b, :, :, bass.ds(s * NPX, NPX)]).then_inc(y_loaded[p], DMA)

            def load_zx(b, s, p):
                px = bass.ds(s * NPX, NPX)
                sp.dma_start(sz[p][:], zv[b, :, :, px]).then_inc(zx_loaded[p], DMA)
                sp.dma_start(x4[p][:], x4v[b, :, :, px]).then_inc(zx_loaded[p], DMA)

            def store(b, s, p):
                sp.wait_ge(out_ready, b * CHUNKS + s + 1)
                sp.dma_start(ov[b, :, :, bass.ds(s * NPX, NPX)], out[p][:]).then_inc(stored[p], DMA)

            def turn(b, j, i, more):
                store(b, j * DEEP + i, i)
                for load, ahead in ((load_zx, DEEP), (load_y, 2 * DEEP - 1)):
                    s, p = j * DEEP + i + ahead, (i + ahead) % DEEP
                    if not isinstance(j, int) or s < CHUNKS:
                        load(b, s, p)
                    elif more:
                        load(b + 1, s - CHUNKS, p)

            def image(b, more):
                with sp.Fori(0, CHUNKS // DEEP - 2) as j:
                    for i in range(DEEP):
                        turn(b, j, i, more)
                for j in (CHUNKS // DEEP - 2, CHUNKS // DEEP - 1):
                    for i in range(DEEP):
                        turn(b, j, i, more)

            for s in range(DEEP):
                load_y(0, s, s, waits=False)
                load_zx(0, s, s)
            for s in range(DEEP, 2 * DEEP - 1):
                load_y(0, s, s - DEEP)
            with sp.Fori(0, B - 1) as b:
                image(b, True)
            image(B - 1, False)
            for p in range(DEEP):
                sp.wait_ge(stored[p], TOTAL // DEEP * DMA)

        @block.gpsimd
        def _(pool):
            nc.gpsimd.memset(mean_w[:], 1.0 / C)
            nc.gpsimd.memset(consts[:, 0:1], LN_EPS)
            nc.gpsimd.memset(consts[:, 1:2], 0.0).then_inc(w_ready, 1)

            def sum_y(k):
                pool.wait_ge(y_loaded[k.p], (k.turn + 1) * DMA)
                pool.wait_ge(mu_ready, k.q)
                nc.gpsimd.tensor_tensor(y_sum[:], y[k.p][:, 0], y[k.p][:, 1], ALU.add).then_inc(y_summed, 1)

            def sum_squares(k):
                pool.wait_ge(sq_ready, k.q + 1)
                pool.wait_ge(var_ready, k.q)
                nc.gpsimd.tensor_tensor(sq_sum[:], sq[:, 0], sq[:, 1], ALU.add).then_inc(sq_summed, 1)

            def step(k):
                if k.is_real:
                    sum_y(k)
                if k.back(1).is_real:
                    sum_squares(k.back(1))

            chunk_loop(pool, step)

        @block.vector
        def _(dve):
            dve.wait_ge(w_loaded, DMA * len(loads))

            def center(k):
                dve.wait_ge(mu_ready, k.q + 1)
                if not (isinstance(k.j, int) and k.q < DEEP):
                    dve.wait_ge(yz_ready, k.q - DEEP + 1)
                mu = stat_ps[0][:].unsqueeze(1).broadcast_to([P, 2, NPX])
                nc.vector.tensor_tensor(yn[k.p][:], y[k.p][:], mu, ALU.subtract).then_inc(yc_ready, 1)

            def scale(k):
                dve.wait_ge(r_ready, k.q + 1)
                dve.wait_ge(yc_ready, k.q + 1)
                for h in range(2):
                    last = nc.vector.scalar_tensor_tensor(yn[k.p][:, h], yn[k.p][:, h], ln_gb[:, h, 0:1],
                                                          rstd[:, 1, :], ALU.mult, ALU.mult)
                last.then_inc(yr_done, 1)

            def add_x4(k):
                dve.wait_ge(o_ready, k.q + 1)
                dve.wait_ge(zx_loaded[k.p], (k.turn + 1) * 2 * DMA)
                dve.wait_ge(stored[k.p], k.turn * DMA)
                nc.vector.tensor_tensor(out[k.p][:], x4[k.p][:], o_ps[k.i % 2][:], ALU.add).then_inc(out_ready, 1)

            def times_z(k):
                dve.wait_ge(yr_done, k.q + 1)
                dve.wait_ge(zx_loaded[k.p], (k.turn + 1) * 2 * DMA)
                if not (isinstance(k.j, int) and k.q < DEEP):
                    dve.wait_ge(o_ready, k.q - DEEP + 2)
                for h in range(2):
                    last = nc.vector.scalar_tensor_tensor(yz[k.p][:, h], yn[k.p][:, h], ln_gb[:, h, 1:2],
                                                          sz[k.p][:, h], ALU.add, ALU.mult)
                last.then_inc(yz_ready, 1)

            def step(k):
                if k.back(1).is_real:
                    center(k.back(1))
                if k.back(2).is_real:
                    scale(k.back(2))
                if k.back(4).is_real:
                    add_x4(k.back(4))
                if k.back(2).is_real:
                    times_z(k.back(2))

            chunk_loop(dve, step)

        @block.scalar
        def _(act):
            act.wait_ge(w_ready, 1)
            nc.scalar.preload_act_table_set("natural_log_exp_and_others")

            def deviation(k):
                act.wait_ge(var_ready, k.q + 1)
                act.wait_ge(yr_done, k.q)
                nc.scalar.activation(rstd[:, 0], stat_ps[1][:], ACT.Ln, bias=consts[:, 0:1]).then_inc(ln_done, 1)
                act.wait_ge(ln_done, k.q + 1)
                nc.scalar.activation(rstd[:, 1], rstd[:, 0], ACT.Exp, scale=-0.5, bias=consts[:, 1:2]).then_inc(r_ready, 1)

            def square(k):
                act.wait_ge(yc_ready, k.q + 1)
                act.wait_ge(sq_summed, k.q)
                nc.scalar.activation(sq[:], yn[k.p][:], ACT.Square).then_inc(sq_ready, 1)

            def step(k):
                if k.back(2).is_real:
                    deviation(k.back(2))
                if k.back(1).is_real:
                    square(k.back(1))

            chunk_loop(act, step)

        @block.tensor
        def _(pe):
            pe.wait_ge(w_ready, 1)
            pe.wait_ge(w_loaded, DMA * len(loads))

            def project(k, o):
                if o == 0:
                    pe.wait_ge(yz_ready, k.q + 1)
                    if not k.is_first:
                        pe.wait_ge(out_ready, k.q - 1)
                for h in range(2):
                    last = nc.tensor.matmul(o_ps[k.i % 2][:, o], w_out[:, h, P * o:P * o + P], yz[k.p][:, h],
                                            start=(h == 0), stop=(h == 1))
                if o == 1:
                    last.then_inc(o_ready, 1)

            def mean(k):
                pe.wait_ge(y_summed, k.q + 1)
                pe.wait_ge(yc_ready, k.q)
                nc.tensor.matmul(stat_ps[0][:], mean_w[:], y_sum[:], start=True, stop=True).then_inc(mu_ready, 1)

            def variance(k):
                pe.wait_ge(sq_summed, k.q + 1)
                pe.wait_ge(r_ready, k.q)
                nc.tensor.matmul(stat_ps[1][:], mean_w[:], sq_sum[:], start=True, stop=True).then_inc(var_ready, 1)

            def step(k):
                if k.back(3).is_real:
                    project(k.back(3), 0)
                if k.is_real:
                    mean(k)
                if k.back(3).is_real:
                    project(k.back(3), 1)
                if k.back(1).is_real:
                    variance(k.back(1))

            chunk_loop(pe, step)


def layout(inputs):
    a = {k: np.asarray(v) for k, v in inputs.items()}
    C, P = 192, 96
    def halves(m):
        return np.ascontiguousarray(m.reshape(2, P, *m.shape[1:]).swapaxes(0, 1))
    out = {}
    out["x"] = a["x"].reshape(4, C, -1)
    out["ident"] = np.eye(128, dtype=np.float32)
    out["ln1_gb"] = halves(np.stack([a["L0_conv_g1"], a["L0_conv_b1"]], -1))
    out["wqkv"] = halves(a["L0_conv_w_qkv"].reshape(576, C).T)
    out["wdw"] = np.ascontiguousarray(a["L0_conv_w_dw"].reshape(6, P, 9).swapaxes(0, 1))
    out["wproj"] = halves(a["L0_conv_w_proj"].reshape(C, C).T)
    out["temp"] = np.ascontiguousarray(np.repeat(a["L0_conv_temp"].reshape(2, 3), 32, 1).T)
    wh = a["L0_conv_w_head"].transpose(1, 3, 2, 0)
    wh = np.repeat(np.repeat(wh, 32, 0), 32, 3)
    out["head_w"] = halves(wh.reshape(C, 9, C))
    c = np.arange(C) % 32
    out["head_mask"] = halves(np.stack([(c[:, None] - c[None, :] + 1 == dy) for dy in range(3)], 1).astype(np.float32))
    out["ln2_gb"] = halves(np.stack([a["L0_conv_g2"], a["L0_conv_b2"]], -1))
    out["w1"] = halves(a["L0_conv_w_fc1"].T)
    out["b1"] = np.ascontiguousarray(a["L0_conv_b_fc1"].reshape(3, 128).T)
    out["w2"] = np.ascontiguousarray(a["L0_conv_w_fc2"].T.reshape(3, 128, C).swapaxes(0, 1))
    out["b2"] = np.ascontiguousarray(a["L0_conv_b_fc2"].reshape(2, P).T)
    out["wsa"] = halves(a["L0_conv_w_sa"].reshape(C, 9))
    out["ln3_gb"] = halves(np.stack([a["L1_conv_ln_w"], a["L1_conv_ln_b"]], -1))
    out["w_in"] = halves(a["L1_conv_in_proj_w"].T)
    out["cw"] = np.ascontiguousarray(a["L1_conv_conv_w"].reshape(2, P, 9).swapaxes(0, 1))
    out["cb"] = np.ascontiguousarray(a["L1_conv_conv_b"].reshape(2, P).T)
    out["b_sa"] = np.repeat(a["L0_conv_b_sa"].reshape(1, 1), P, 0)
    xp = a["L1_conv_x_proj_w"]
    xp = np.concatenate([xp[:, :12].reshape(48, C), xp[:, 12:].reshape(32, C)], 0)
    out["w_x"] = halves(xp.T)
    row = np.arange(384).reshape(3, 128)
    img, ch = row // C, row % C
    w_dt = a["L1_conv_dt_proj_w"][:, ch, :]
    two = np.zeros((3, 2, 12, 4, 128), np.float32)
    for t in range(3):
        for i in range(2):
            two[t, i][:, :, img[t] == i] = w_dt[:, t][:, img[t] == i].transpose(2, 0, 1)
    out["w_dt"] = two.reshape(3, 24, 4, 128)
    out["dt_bias"] = np.ascontiguousarray(a["L1_conv_dt_proj_b"][:, ch].transpose(1, 2, 0))
    out["a_log"] = np.ascontiguousarray(a["L1_conv_A_log"][:, ch].transpose(1, 2, 0, 3).reshape(3, 128, 16))
    out["skip"] = np.ascontiguousarray(a["L1_conv_Ds"][:, ch].transpose(1, 2, 0))
    sel = np.zeros((3, 3, 2, 8, 8, 128), np.float32)
    for t in range(3):
        for i in range(2):
            for r in range(8):
                sel[t, :, i, r, r, img[t] == i] = 1
    out["sel"] = sel.reshape(3, 48, 8, 128)
    out["ln4_gb"] = halves(np.stack([a["L1_conv_out_norm_w"], a["L1_conv_out_norm_b"]], -1))
    out["w_out"] = halves(a["L1_conv_out_proj_w"].T)
    return out


def build(nc, arrays):
    d = {}
    for name, array in arrays.items():
        d[name] = nc.dram_tensor("in_" + name, array.shape, mybir.dt.from_np(array.dtype), kind="ExternalInput").ap()
    image = [B, C, L]
    for name, shape, dt in (("x1", image, FP32), ("v", image, FP32), ("mt", [B, P, 2, C], FP32), ("x2", image, FP32),
                            ("y", image, FP32), ("planes", [B, 9 * PLANE + 3], FP32), ("x4", image, FP32),
                            ("sz", image, FP32), ("u", image, FP32), ("dts", [DIRS, B, RANK, L], FP32),
                            ("bc", [DIRS, B, 2 * STATES, L], FP32),
                            ("bcs", [DIRS, PAIRS, 6 * 2 * STATES, L], BF16), ("ys", image, FP32)):
        d[name] = nc.dram_tensor(name, shape, dt, kind="Internal").ap()
    d["out"] = nc.dram_tensor("out", image, FP32, kind="ExternalOutput").ap()
    attention_statistics(nc, d)
    attention_and_mlp(nc, d)
    gate_and_scan_inputs(nc, d)
    split_and_turn(nc, d)
    selective_scans(nc, d)
    output_projection(nc, d)


def kernel(**inputs):
    import concourse.bacc as bacc
    from concourse.bass_utils import run_bass_kernel_spmd

    arrays = layout(inputs)
    nc = bacc.Bacc("TRN2", target_bir_lowering=False, num_devices=1)
    build(nc, arrays)
    r = run_bass_kernel_spmd(nc, [{"in_" + k: v for k, v in arrays.items()}], core_ids=[0])
    return r.results[0]["out"].reshape(B, C, HH, WW)
```
